# Optimizing a Trainium2 kernel written in Bass

```python
import numpy as np
import jax
import jax.numpy as jnp

def _softmax(x, axis=-1):
    return jax.nn.softmax(x, axis=axis)

def _gelu(x):
    return jax.nn.gelu(x, approximate=True)

def _silu(x):
    return jax.nn.silu(x)

def _sigmoid(x):
    return jax.nn.sigmoid(x)

def _layernorm(x, axis=-1, eps=1e-05):
    m = jnp.mean(x, axis=axis, keepdims=True)
    v = jnp.var(x, axis=axis, keepdims=True)
    return (x - m) / jnp.sqrt(v + eps)

def _scatter_add(tgt, idx, src, axis=0):
    return tgt.at[idx].add(src)

def _segment_sum(src, seg, n):
    return jax.ops.segment_sum(src, seg, n)
kernel_name = 'mk_xattn_ffn_d2_seqx_r4_08d087'

def setup_inputs(seed: int=0):
    np.random.seed(seed)
    _w = jnp.asarray

    def _rec_inputs():
        import jax
        import jax.numpy as jnp
        _rk = jax.random.key(seed)
        x = -0.0003929 + 0.9999 * jax.random.normal(jax.random.fold_in(_rk, 1), (8, 112, 256), jnp.float32)
        _lenS = 112 - jax.random.randint(jax.random.fold_in(_rk, 7), (8,), 0, max(1, 112 // 4) + 1, jnp.int32)
        _lenS2 = 375 - jax.random.randint(jax.random.fold_in(_rk, 8), (8,), 0, max(1, 375 // 4) + 1, jnp.int32)
        _ctx_512P = jax.random.normal(jax.random.fold_in(_rk, 11), (8, 16, 128), jnp.float32)
        _ctx_512c = jax.random.dirichlet(jax.random.fold_in(_rk, 511), 0.3 * jnp.ones((16,), jnp.float32), (8, 375))
        _ctx_512t = jnp.einsum('bsk,bkd->bsd', _ctx_512c, _ctx_512P)
        _ctx_512t = _ctx_512t * jax.lax.rsqrt(jnp.mean(jnp.square(_ctx_512t)) + 1e-12) * 0.953939
        ctx_512 = 4.13588e-05 + 0.999923 * (_ctx_512t + 0.3 * jax.random.normal(jax.random.fold_in(_rk, 611), (8, 375, 128), jnp.float32))
        return (x, ctx_512)
    x, ctx_512 = _rec_inputs()

    def _L0_xattn_setup():
        import jax, jax.numpy as jnp
        import numpy as np
        B, LQ, LK = (8, 512, 512)
        QD, KD, VD = (256, 128, 128)
        key = jax.random.key(seed)
        ks = jax.random.split(key, 9)
        s = 0.02
        return {'query': jax.random.normal(ks[0], (B, LQ, QD), jnp.float32), 'key': jax.random.normal(ks[1], (B, LK, KD), jnp.float32), 'value': jax.random.normal(ks[2], (B, LK, VD), jnp.float32), 'Wq': jax.random.normal(ks[3], (QD, QD), jnp.float32) * s, 'bq': jnp.zeros((QD,), jnp.float32), 'Wk': jax.random.normal(ks[4], (KD, QD), jnp.float32) * s, 'bk': jnp.zeros((QD,), jnp.float32), 'Wv': jax.random.normal(ks[5], (VD, QD), jnp.float32) * s, 'bv': jnp.zeros((QD,), jnp.float32)}
    _L0_xattn_all = _L0_xattn_setup()
    _L0_xattn_in = {k: v for k, v in _L0_xattn_all.items() if k in ('Wq', 'bq', 'Wk', 'bk', 'Wv', 'bv')}
    del _L0_xattn_all

    def _L0_ffn_setup():
        import jax, jax.numpy as jnp
        import numpy as np
        EPS = 0.05
        N_ITERS = 20
        TOP_K = 2

        def _sinkhorn(cost, n_iters=N_ITERS, epsilon=EPS):
            la = cost / epsilon
            for _ in range(n_iters):
                la = la - jax.scipy.special.logsumexp(la, axis=-1, keepdims=True)
                la = la - jax.scipy.special.logsumexp(la, axis=-2, keepdims=True)
            return jnp.exp(la)
        key = jax.random.key(seed)
        k0, k1, k2, k3, k4 = jax.random.split(key, 5)
        B, T, D, F, E = (2, 512, 256, 1024, 8)
        x = jax.random.normal(k0, (B, T, D), dtype=jnp.float32)
        gate_W = jax.random.normal(k1, (E, D), dtype=jnp.float32) * 0.02
        W_gate = jax.random.normal(k2, (E, F, D), dtype=jnp.float32) * 0.02
        W_up = jax.random.normal(k3, (E, F, D), dtype=jnp.float32) * 0.02
        W_down = jax.random.normal(k4, (E, D, F), dtype=jnp.float32) * 0.02
        return {'x': x, 'gate_W': gate_W, 'W_gate': W_gate, 'W_up': W_up, 'W_down': W_down}
    _L0_ffn_all = _L0_ffn_setup()
    _L0_ffn_in = {k: v for k, v in _L0_ffn_all.items() if k in ('gate_W', 'W_gate', 'W_up', 'W_down')}
    del _L0_ffn_all

    def _L1_xattn_setup():
        import jax, jax.numpy as jnp
        import numpy as np
        HEADS = 16
        D_MODEL = 256
        IMG_MODEL = 128
        D_K = D_MODEL // HEADS
        key = jax.random.key(seed)
        ks = jax.random.split(key, 12)
        B, LQ, LKV = (8, 512, 256)
        s_dm = 1.0 / np.sqrt(D_MODEL)
        s_im = 1.0 / np.sqrt(IMG_MODEL)
        return {'q': jax.random.normal(ks[0], (B, LQ, D_MODEL), jnp.float32), 'k': jax.random.normal(ks[1], (B, LKV, IMG_MODEL), jnp.float32), 'v': jax.random.normal(ks[2], (B, LKV, IMG_MODEL), jnp.float32), 'Wq': jax.random.normal(ks[3], (D_MODEL, D_MODEL), jnp.float32) * s_dm, 'bq': jnp.zeros((D_MODEL,), jnp.float32), 'Wk': jax.random.normal(ks[4], (IMG_MODEL, D_MODEL), jnp.float32) * s_im, 'bk': jnp.zeros((D_MODEL,), jnp.float32), 'Wv': jax.random.normal(ks[5], (IMG_MODEL, D_MODEL), jnp.float32) * s_im, 'bv': jnp.zeros((D_MODEL,), jnp.float32), 'Wo': jax.random.normal(ks[6], (D_MODEL, D_MODEL), jnp.float32) * s_dm, 'bo': jnp.zeros((D_MODEL,), jnp.float32)}
    _L1_xattn_all = _L1_xattn_setup()
    _L1_xattn_in = {k: v for k, v in _L1_xattn_all.items() if k in ('Wq', 'bq', 'Wk', 'bk', 'Wv', 'bv', 'Wo', 'bo')}
    del _L1_xattn_all

    def _L1_ffn_setup():
        import jax, jax.numpy as jnp
        import numpy as np
        HIDDEN = 256
        INTER = 512
        NUM_EXPERTS = 8
        TOPK = 2
        STD = 0.02
        key = jax.random.key(seed)
        k1, k2, k3, k4 = jax.random.split(key, 4)
        return {'hidden_states': jax.random.normal(k1, (1, 512, HIDDEN), dtype=jnp.float32), 'w1': jax.random.normal(k2, (NUM_EXPERTS, 2 * INTER, HIDDEN), dtype=jnp.float32) * STD, 'w2': jax.random.normal(k3, (NUM_EXPERTS, HIDDEN, INTER), dtype=jnp.float32) * STD, 'router_w': jax.random.normal(k4, (NUM_EXPERTS, HIDDEN), dtype=jnp.float32) * STD}
    _L1_ffn_all = _L1_ffn_setup()
    _L1_ffn_in = {k: v for k, v in _L1_ffn_all.items() if k in ('w1', 'w2', 'router_w')}
    del _L1_ffn_all
    return {'x': x, 'ctx_512': ctx_512, 'L0_xattn_Wq': _L0_xattn_in['Wq'], 'L0_xattn_bq': _L0_xattn_in['bq'], 'L0_xattn_Wk': _L0_xattn_in['Wk'], 'L0_xattn_bk': _L0_xattn_in['bk'], 'L0_xattn_Wv': _L0_xattn_in['Wv'], 'L0_xattn_bv': _L0_xattn_in['bv'], 'L0_ffn_gate_W': _L0_ffn_in['gate_W'], 'L0_ffn_W_gate': _L0_ffn_in['W_gate'], 'L0_ffn_W_up': _L0_ffn_in['W_up'], 'L0_ffn_W_down': _L0_ffn_in['W_down'], 'L1_xattn_Wq': _L1_xattn_in['Wq'], 'L1_xattn_bq': _L1_xattn_in['bq'], 'L1_xattn_Wk': _L1_xattn_in['Wk'], 'L1_xattn_bk': _L1_xattn_in['bk'], 'L1_xattn_Wv': _L1_xattn_in['Wv'], 'L1_xattn_bv': _L1_xattn_in['bv'], 'L1_xattn_Wo': _L1_xattn_in['Wo'], 'L1_xattn_bo': _L1_xattn_in['bo'], 'L1_ffn_w1': _L1_ffn_in['w1'], 'L1_ffn_w2': _L1_ffn_in['w2'], 'L1_ffn_router_w': _L1_ffn_in['router_w']}

def reference(x, ctx_512, L0_xattn_Wq, L0_xattn_bq, L0_xattn_Wk, L0_xattn_bk, L0_xattn_Wv, L0_xattn_bv, L0_ffn_gate_W, L0_ffn_W_gate, L0_ffn_W_up, L0_ffn_W_down, L1_xattn_Wq, L1_xattn_bq, L1_xattn_Wk, L1_xattn_bk, L1_xattn_Wv, L1_xattn_bv, L1_xattn_Wo, L1_xattn_bo, L1_ffn_w1, L1_ffn_w2, L1_ffn_router_w):
    import jax
    import jax.numpy as jnp

    def _L0_xattn_ref(query, key, value, Wq, bq, Wk, bk, Wv, bv):
        import jax, jax.numpy as jnp
        import numpy as np
        B, LQ, LK = (8, 512, 512)
        QD, KD, VD = (256, 128, 128)
        q = jnp.einsum('bld,de->ble', query, Wq) + bq
        k = jnp.einsum('bld,de->ble', key, Wk) + bk
        v = jnp.einsum('bld,de->ble', value, Wv) + bv
        scores = jnp.einsum('bqe,bke->bqk', q, k)
        attn = jax.nn.softmax(scores, axis=-1)
        out = jnp.einsum('bqk,bke->bqe', attn, v)
        return out

    def _L0_ffn_ref(x, gate_W, W_gate, W_up, W_down):
        import jax, jax.numpy as jnp
        import numpy as np
        EPS = 0.05
        N_ITERS = 20
        TOP_K = 2

        def _sinkhorn(cost, n_iters=N_ITERS, epsilon=EPS):
            la = cost / epsilon
            for _ in range(n_iters):
                la = la - jax.scipy.special.logsumexp(la, axis=-1, keepdims=True)
                la = la - jax.scipy.special.logsumexp(la, axis=-2, keepdims=True)
            return jnp.exp(la)
        B, T, D = x.shape
        xf = x.reshape(B * T, D)
        logits = xf @ gate_W.T
        pi = _sinkhorn(-logits)
        _, top_idx = jax.lax.top_k(pi, TOP_K)
        g = jnp.einsum('nd,efd->enf', xf, W_gate)
        u = jnp.einsum('nd,efd->enf', xf, W_up)
        y = jnp.einsum('enf,edf->end', jax.nn.silu(g) * u, W_down)
        n_ar = jnp.arange(xf.shape[0])
        out = jnp.zeros_like(xf)
        for k in range(TOP_K):
            out = out + y[top_idx[:, k], n_ar] * pi[:, k:k + 1]
        return out.reshape(B, T, D)

    def _L1_xattn_ref(q, k, v, Wq, bq, Wk, bk, Wv, bv, Wo, bo):
        import jax, jax.numpy as jnp
        import numpy as np
        HEADS = 16
        D_MODEL = 256
        IMG_MODEL = 128
        D_K = D_MODEL // HEADS
        B, LQ, _ = q.shape
        LKV = k.shape[1]
        qh = (q @ Wq + bq).reshape(B, LQ, HEADS, D_K).transpose(0, 2, 1, 3)
        kh = (k @ Wk + bk).reshape(B, LKV, HEADS, D_K).transpose(0, 2, 1, 3)
        vh = (v @ Wv + bv).reshape(B, LKV, HEADS, D_K).transpose(0, 2, 1, 3)
        scale = 1.0 / np.sqrt(D_K)
        scores = jnp.einsum('bhqd,bhkd->bhqk', qh, kh) * scale
        attn = jax.nn.softmax(scores, axis=-1)
        out = jnp.einsum('bhqk,bhkd->bhqd', attn, vh)
        concat = out.transpose(0, 2, 1, 3).reshape(B, LQ, D_MODEL)
        return concat @ Wo + bo

    def _L1_ffn_ref(hidden_states, w1, w2, router_w):
        import jax, jax.numpy as jnp
        import numpy as np
        HIDDEN = 256
        INTER = 512
        NUM_EXPERTS = 8
        TOPK = 2
        STD = 0.02
        orig_shape = hidden_states.shape
        dtype = hidden_states.dtype
        x = hidden_states.reshape(-1, orig_shape[-1])
        E = w1.shape[0]
        gating = x @ router_w.T
        probs = jax.nn.softmax(gating.astype(jnp.float32), axis=-1)
        topk_w, sel = jax.lax.top_k(probs, TOPK)
        topk_w = topk_w.astype(dtype)
        combine = (jax.nn.one_hot(sel, E, dtype=dtype) * topk_w[..., None]).sum(axis=1)
        h = jnp.einsum('td,eid->tei', x, w1)
        gate = jax.nn.silu(h[..., :INTER])
        y = h[..., INTER:] * gate
        out = jnp.einsum('tei,ehi,te->th', y, w2, combine)
        return out.reshape(orig_shape)
    x = x + _L0_xattn_ref(_layernorm(x, axis=-1), ctx_512, ctx_512, L0_xattn_Wq, L0_xattn_bq, L0_xattn_Wk, L0_xattn_bk, L0_xattn_Wv, L0_xattn_bv)
    x = x + _L0_ffn_ref(_layernorm(x, axis=-1), L0_ffn_gate_W, L0_ffn_W_gate, L0_ffn_W_up, L0_ffn_W_down)
    x = x + _L1_xattn_ref(_layernorm(x, axis=-1), ctx_512, ctx_512, L1_xattn_Wq, L1_xattn_bq, L1_xattn_Wk, L1_xattn_bk, L1_xattn_Wv, L1_xattn_bv, L1_xattn_Wo, L1_xattn_bo)
    x = x + _L1_ffn_ref(_layernorm(x, axis=-1), L1_ffn_w1, L1_ffn_w2, L1_ffn_router_w)
    return x

_drawn_inputs = setup_inputs


def setup_inputs(seed=0):
    import zlib

    import numpy as np

    out = dict(_drawn_inputs(seed))
    spreads = {'L0_xattn_bq': (0.0, 0.385),
     'L0_xattn_bk': (0.0, 0.8),
     'L0_xattn_bv': (0.0, 0.1),
     'L1_xattn_bq': (0.0, 0.413),
     'L1_xattn_bk': (0.0, 0.8),
     'L1_xattn_bv': (0.0, 0.1),
     'L1_xattn_bo': (0.0, 0.1)}
    factors = {'L0_ffn_gate_W': 8.0,
     'L0_ffn_W_gate': 8.0,
     'L0_ffn_W_up': 8.0,
     'L0_ffn_W_down': 8.0,
     'L1_ffn_w1': 8.0,
     'L1_ffn_w2': 8.0,
     'L1_ffn_router_w': 8.0}
    for name, (base, spread) in spreads.items():
        noise = np.random.default_rng([zlib.crc32(name.encode()), seed]).standard_normal(out[name].shape)
        drawn = base * np.exp(spread * noise) if base else spread * noise
        out[name] = jnp.asarray(drawn.astype(out[name].dtype))
    for name, factor in factors.items():
        out[name] = (out[name] * factor).astype(out[name].dtype)
    return out
```

```python
from contextlib import ExitStack

import concourse.bass as bass
from concourse import mybir

ALU = mybir.AluOpType
ACT = mybir.ActivationFunctionType
F32 = mybir.dt.float32
F16 = mybir.dt.float16
I32 = mybir.dt.int32
U32 = mybir.dt.uint32
AX = mybir.AxisListType
ds = bass.ds

B, T, D = 8, 112, 256
KEYS, C = 375, 128
KC, NKC = 125, 3
KD = D // 128
E = 8
TOPK = 2
HEADS, DK = 16, 16
HP = 4
NTOK = B * T
SLOTS = 128
TILES = (NTOK * TOPK + E * (SLOTS - 1)) // SLOTS
CPE = NTOK // SLOTS
FC = 256
PHASES = (1024 // FC, 512 // FC)
EW = KD * 2 * FC + (FC // 128) * D
WSCALE = 256.0
EPS = 1e-5
SINK_ITERS, SINK_EPS = 20, 0.05


class Chain:

    def __init__(self, eng, sem):
        self.eng, self.sem, self.base, self.n = eng, sem, 0, 0

    def __call__(self, ins):
        self.n += 1
        ins.then_inc(self.sem, 1)
        self.eng.wait_ge(self.sem, self.base + self.n)

    def enter(self, i, per, start):
        self.base, self.n = start + i * per, 0

    def leave(self, per, trips, start):
        assert self.n == per, (self.n, per)
        self.base, self.n = start + trips * per, 0

    @property
    def now(self):
        return self.base + self.n


class Step:

    def __init__(self, i, k):
        self.i, self.k = i, k

    def __add__(self, n):
        return self.i * 4 + (self.k + n)

    @property
    def at(self):
        return self + 0


def build(nc, a):
    ctx = ExitStack()
    with ctx:
        def sb(name, shape, dt=F32):
            return ctx.enter_context(nc.sbuf_tensor(name, shape, dt))

        sems = {}

        def S(name):
            if name not in sems:
                sems[name] = ctx.enter_context(nc.semaphore(name))
            return sems[name]

        pb = [ctx.enter_context(nc.psum_tensor(f"bank{i}", [128, 512], F32)) for i in range(8)]
        pall = None

        xg_dram = nc.dram_tensor("expert_rows", [TILES * SLOTS, D], F32, kind="Internal").ap()
        ys_dram = nc.dram_tensor("expert_results", [TILES * SLOTS, D], F32, kind="Internal").ap()

        x = sb("x", [T, B, D])
        xn = sb("xn", [T, B, D])
        whi = sb("whi", [128, 2, E * EW], F16)
        wlo = sb("wlo", [128, 2, E * EW], F16)
        stage = sb("stage", [128, 2, EW])
        ident = sb("ident", [128, 128])
        ones = sb("ones", [128, 128])
        lower = sb("lower", [T, T])
        ctT = sb("ctT", [128, 2, KEYS])
        bq0 = sb("bq0", [128, KD])
        bk0 = sb("bk0", [128, KD])
        bv0 = sb("bv0", [T, D])
        fold = sb("fold", [128, 2 * C + 4])
        wq1 = sb("wq1", [128, KD, HP * 128])
        wk1 = sb("wk1", [C, HP * 128])
        wv1 = sb("wv1", [C, D])
        wo1 = sb("wo1", [128, KD, D])
        bq1 = sb("bq1", [128, HP])
        bk1 = sb("bk1", [128, HP])
        bv1 = sb("bv1", [T, D])
        bo1 = sb("bo1", [T, D])
        router = sb("router", [128, 2, KD, E])
        xnb = sb("xnb", [T, 2, D])
        stats = sb("stats", [T, 2, 6])
        mv = sb("mv", [T, 2, 2])
        vare = sb("vare", [T, 2, 1])
        rstd = sb("rstd", [T, 2, 1])
        carrier = sb("carrier", [T, 4, 1])
        mhalf = sb("mhalf", [T, 1])
        xnT = sb("xnT", [128, 2, KD, T])
        aT = sb("aT", [128, 2, T])
        qbk = sb("qbk", [T, 2, 1])
        mx0 = sb("mx0", [T, 2, 1])
        nb0 = sb("nb0", [T, 2, 1])
        rs0 = sb("rs0", [T, 2, 1])
        rc0 = sb("rc0", [T, 2, 1])
        upd = sb("upd", [T, 2, D])
        zT = sb("zT", [C, 2, T])
        la = sb("la", [T, B, E])
        pi = sb("pi", [T, B, E])
        tmp = sb("tmp", [T, B, E])
        msk = sb("msk", [T, B, E])
        m1h = sb("m1h", [T, B, E])
        m2h = sb("m2h", [T, B, E])
        slotv = sb("slotv", [T, B, E])
        rr = sb("rr", [T, B])
        rl = sb("rl", [T, B])
        cc = sb("cc", [T, E])
        cl = sb("cl", [T, E])
        cm = sb("cm", [E, 1])
        cdiag = sb("cdiag", [E, E])
        wtop = sb("wtop", [T, 2, TOPK, B])
        sf = sb("sf", [T, B])
        slot = sb("slot", [T, TOPK, B], U32)
        iota_e = sb("iota_e", [T, B, E])
        kgrid = sb("kgrid", [T, E, CPE])
        kcmp = sb("kcmp", [T, E, CPE])
        nt = sb("nt", [T, E])
        tri = sb("tri", [T, E, E])
        tcmp = sb("tcmp", [T, E, E])
        tb = sb("tb", [T, E])
        tend = sb("tend", [T, E])
        sgrid = sb("sgrid", [T, TILES, E])
        scmp = sb("scmp", [T, TILES, E])
        tef = sb("tef", [T, TILES])
        te = sb("te", [T, TILES], I32)
        sg = sb("sg", [128, 2, FC])
        hh = sb("hh", [128, 2, FC])
        hThi = sb("hThi", [128, 2, FC // 128, 128], F16)
        hTlo = sb("hTlo", [128, 2, FC // 128, 128], F16)

        REGION = 10752
        region = sb("region", [128, REGION])
        XT = TILES * KD * 128
        xThi = region[:, 0:XT // 2].bitcast(F16).rearrange("p (s k n) -> p s k n", k=KD, n=128)
        xTlo = region[:, XT // 2:XT].bitcast(F16).rearrange("p (s k n) -> p s k n", k=KD, n=128)
        yacc = region[:, XT:XT + TILES * D].rearrange("p (s d) -> p s d", d=D)
        xrow = sb("xrow", [128, 2, D])
        yg = region[0:T, 0:TOPK * B * D].rearrange("p (k b d) -> p k b d", k=TOPK, b=B)
        at = [0]

        def carve(p, *dims):
            n = 1
            for v in dims:
                n *= v
            v = region[0:p, at[0]:at[0] + n]
            at[0] += n
            assert at[0] <= REGION, at
            if len(dims) == 1:
                return v
            names = "abcd"[:len(dims)]
            return v.rearrange(f"p ({' '.join(names)}) -> p {' '.join(names)}",
                               **{k: d for k, d in zip(names[1:], dims[1:])})

        NP = 4
        probs = carve(T, NP, KEYS)
        probsT = carve(KC, 2, NKC, T)
        both = at[0]
        ctN = carve(KC, 2, NKC, C)
        wq0T = carve(128, KD, D)
        wk0T = carve(128, KD, C)
        wv0 = carve(C, D)
        at[0] = both
        kT = carve(128, HP, KEYS)
        qT = carve(128, HP, T)
        v1 = carve(KC, NKC, D)
        cat = carve(T, D)
        catT = carve(128, KD, T)
        mx1 = carve(T, 2, 2)
        nb1 = carve(T, HEADS)
        rs1 = carve(T, HEADS)
        rc1 = carve(T, HEADS)

        def bc(ap, shape):
            return ap.to_broadcast(shape) if hasattr(ap, "to_broadcast") else ap.broadcast(shape)

        block = ctx.enter_context(nc.Block())
        NPH = sum(PHASES)

        def w_src(c0):
            return a["wst"][:, c0]

        def rows_in(lay, s, par, eng, wait):
            if wait is not None:
                eng.wait_ge(S("xrow_used"), wait)
            eng.dma_start(xrow[:, par, :], xg_dram[ds(s * SLOTS, SLOTS), :]).then_inc(S(f"xrow_in{par}"), 16)

        def results(eng, lay):
            eng.wait_ge(S("y_acc"), TILES * sum(PHASES[:lay + 1]))
            eng.dma_start(ys_dram.rearrange("(s p) d -> p s d", p=SLOTS), yacc).then_inc(S("ys_out"), 16)

        @block.sync
        def _(sp):
            sp.dma_start(x[:], a["x"].rearrange("b t d -> t b d")).then_inc(S("x_in"), 16)
            for dst, src in ((wq0T, "wq0T"), (wk0T, "wk0T"), (wv0, "wv0"), (bq0, "bq0"), (bk0, "bk0"),
                             (bv0, "bv0"), (wq1, "wq1"), (wk1, "wk1"), (wv1, "wv1"), (wo1, "wo1"),
                             (bq1, "bq1"), (bk1, "bk1"), (bv1, "bv1"), (bo1, "bo1"), (router, "router")):
                sp.dma_start(dst[:], a[src]).then_inc(S("weights_in"), 16)

            def ctx_in(lay, i, u, wait):
                if wait is not None:
                    sp.wait_ge(S(("z_ps", "qkv_ps")[lay]), wait)
                sp.dma_start(ctT[:, u, :], a["ctxT"][:, ds(i * 2 + u, 1), :].rearrange("p o k -> p (o k)")
                             ).then_inc(S(f"ctx_in{u}"), 16)
                if lay == 0:
                    sp.dma_start(ctN[:, u, :, :], a["ctxN"][:, ds(i * 2 + u, 1), :, :].rearrange(
                        "p o j c -> p (o j) c")).then_inc(S(f"ctx_in{u}"), 16)

            def chunk_in(c, v, wait):
                if wait is not None:
                    sp.wait_ge(S("w_hi"), wait)
                    sp.wait_ge(S("w_lo"), wait)
                sp.dma_start(stage[:, v, :], a["wst"][:, ds(c, 1), :].rearrange("p o n -> p (o n)")
                             ).then_inc(S(f"w_in{v}"), 16)

            for u in range(2):
                ctx_in(0, 0, u, None)
            for v in range(2):
                chunk_in(v, v, None)
            with sp.Fori(1, 4) as i:
                for u in range(2):
                    ctx_in(0, i, u, i * 2 - 1 + u)
                for v in range(2):
                    chunk_in(i * 2 + v, v, i * 2 + v - 1)
            for u in range(2):
                sp.wait_ge(S("z_ps"), B)
                ctx_in(1, 0, u, None)
            with sp.Fori(E // 2, (PHASES[0] + 1) * E // 2) as i:
                for v in range(2):
                    chunk_in(i * 2 + v, v, i * 2 + v - 1)
            results(sp, 0)
            with sp.Fori(1, 4) as i:
                for u in range(2):
                    ctx_in(1, i, u, i * 2 - 1 + u)
            with sp.Fori((PHASES[0] + 1) * E // 2, NPH * E // 2) as i:
                for v in range(2):
                    chunk_in(i * 2 + v, v, i * 2 + v - 1)
            results(sp, 1)
            sp.wait_ge(S("x_done"), B)
            sp.dma_start(a["out"].rearrange("b t d -> t b d"), x[:]).then_inc(S("out_done"), 16)
            sp.wait_ge(S("out_done"), 16)

        @block.gpsimd
        def _(pool):
            g = Chain(pool, S("pool_step"))
            g(pool.memset(ident[:], 0.0))
            g(pool.affine_select(out=ident[:], in_=ident[:], compare_op=ALU.not_equal, fill=1.0, base=0,
                                 pattern=[[-1, 128]], channel_multiplier=1))
            pool.memset(xnb[:], 0.0).then_inc(S("xn_kept"), 1)
            pool.memset(mhalf[:], -0.5).then_inc(S("const"), 1)
            pool.memset(ones[:], 1.0).then_inc(S("const"), 1)
            g(pool.memset(lower[:], 1.0))
            pool.affine_select(out=lower[:], in_=lower[:], compare_op=ALU.is_gt, fill=0.0, base=0,
                               pattern=[[1, T]], channel_multiplier=-1).then_inc(S("const"), 1)
            pool.iota(iota_e[:], [[0, B], [1, E]], base=-E, channel_multiplier=0,
                      allow_small_or_imprecise_dtypes=True).then_inc(S("const"), 1)
            pool.iota(kgrid[:], [[0, E], [SLOTS, CPE]], base=0, channel_multiplier=0,
                      allow_small_or_imprecise_dtypes=True).then_inc(S("const"), 1)
            pool.iota(sgrid[:], [[1, TILES], [0, E]], base=0, channel_multiplier=0,
                      allow_small_or_imprecise_dtypes=True).then_inc(S("const"), 1)
            g(pool.memset(tri[:], 1.0))
            pool.affine_select(out=tri[:], in_=tri[:], compare_op=ALU.is_gt, fill=0.0, base=0,
                               pattern=[[1, E], [-1, E]], channel_multiplier=0).then_inc(S("const"), 1)
            zeros = whi[:, 1, 0:2 * TILES * D].bitcast(F32)
            g(pool.memset(zeros, 0.0))
            pool.dma_start(xg_dram.rearrange("(s p) d -> p s d", p=SLOTS),
                           zeros.rearrange("p (s d) -> p s d", d=D)).then_inc(S("zeroed"), 16)

            for lay in range(2):
                with pool.Fori(0, 4) as i:
                    for half in range(2):
                        for u in range(2):
                            n = i * 4 + half * 2 + u + 1 + lay * 2 * B
                            pool.wait_ge(S("var_ready"), n)
                            pool.tensor_tensor(rstd[:, u, :], vare[:, u, :], mhalf[:], ALU.pow
                                               ).then_inc(S("rstd_ready"), 1)
                pool.wait_ge(S("slots_ready"), lay + 1)
                pool.wait_ge(S("zeroed"), 16)
                pool.wait_ge(S("xn_kept"), B * (lay + 1) + 1)
                for k in range(TOPK):
                    for b in range(B):
                        pool.indirect_dma_start(
                            out=xg_dram, out_offset=bass.IndirectOffsetOnAxis(ap=slot[:, k, b:b + 1], axis=0),
                            in_=xn[:, b, :], in_offset=None).then_inc(S("scattered"), 16)
                pool.wait_ge(S("scattered"), 16 * TOPK * B * (lay + 1))
                for s in range(TILES):
                    g0 = lay * TILES + s
                    rows_in(lay, s, g0 % 2, pool, g0 - 1 if g0 >= 2 else None)
                pool.wait_ge(S("ys_out"), 16 * (lay + 1))
                for b in range(B):
                    for k in range(TOPK):
                        pool.indirect_dma_start(
                            out=yg[:, k, b, :], out_offset=None, in_=ys_dram,
                            in_offset=bass.IndirectOffsetOnAxis(ap=slot[:, k, b:b + 1], axis=0),
                        ).then_inc(S(f"gathered{b}"), 16)

        def pipeline(A, Bf, Cf, extra=None, eng=None):
            def step(s, par):
                A(s, par, None)
                Bf(Step(s.i, s.k - 1) if isinstance(s, Step) else s - 1, 1 - par)
                Cf(Step(s.i, s.k - 2) if isinstance(s, Step) else s - 2, par)

            A(0, 0, 0)
            A(1, 1, 1)
            Bf(0, 0)
            for s in (2, 3):
                step(s, s % 2)
            with eng.Fori(0, 4) as i:
                for q in range(4):
                    step(Step(i, 4 + q), q % 2)
                    if extra is not None and q % 2:
                        extra(i, q // 2)
            step(TILES - 1, 0)
            last = TILES - 1
            Bf(last, last % 2)
            Cf(last - 1, (last - 1) % 2)
            Cf(last, last % 2)

        @block.tensor
        def _(pe):
            pe.wait_ge(S("weights_in"), 16 * 15)
            pe.wait_ge(S("const"), 7)
            pe.wait_ge(S("pool_step"), 4)
            f = pb[7]
            for k in range(KD):
                for e in range(KD):
                    pe.matmul(f[:, k * C:(k + 1) * C], wq0T[:, e, k * 128:(k + 1) * 128], wk0T[:, e, :],
                              start=(e == 0), stop=(e == KD - 1))
            for e in range(KD):
                pe.matmul(f[:, 2 * C:2 * C + 1], wk0T[:, e, :], bq0[:, e:e + 1], start=(e == 0), stop=(e == 1))
            for k in range(KD):
                for e in range(KD):
                    pe.matmul(f[:, 2 * C + 1 + k:2 * C + 2 + k], wq0T[:, e, k * 128:(k + 1) * 128],
                              bk0[:, e:e + 1], start=(e == 0), stop=(e == 1))
            for e in range(KD):
                last = pe.matmul(f[:, 2 * C + 3:2 * C + 4], bq0[:, e:e + 1].to_broadcast([128, 128]),
                                 bk0[:, e:e + 1], start=(e == 0), stop=(e == 1))
            last.then_inc(S("fold_ps"), 1)
            pe.wait_ge(S("fold_sb"), 1)

            def turn(lay, i, half):
                for u in range(2):
                    n = i * 4 + half * 2 + u + 1 + lay * 2 * B
                    pe.wait_ge(S("ln_ready"), n)
                    for k in range(KD):
                        last = pe.transpose(pb[4 + u][:, k * T:(k + 1) * T], xnb[:, u, k * 128:(k + 1) * 128],
                                            ident[0:T, 0:T])
                    last.then_inc(S("xnT_ps"), 1)

            def route(lay, i):
                for u in range(2):
                    pe.wait_ge(S("xnT_sb"), i * 4 + 2 + u + 1 + lay * 2 * B)
                    for k in range(KD):
                        last = pe.matmul(pb[4 + u][0:T, 256:256 + E], xnT[:, u, k, :], router[:, lay, k, :],
                                         start=(k == 0), stop=(k == 1))
                    last.then_inc(S("logit_ps"), 1)

            with pe.Fori(0, 4) as i:
                turn(0, i, 0)
                for u in range(2):
                    n = i * 2 + u + 1
                    pe.wait_ge(S("xnT_sb"), i * 4 + u + 1)
                    for k in range(KD):
                        pe.matmul(pb[6 + u][:, 0:T], fold[:, k * C:(k + 1) * C], xnT[:, u, k, :],
                                  start=(k == 0), stop=(k == 1))
                    for k in range(KD):
                        last = pe.matmul(pb[2 + u][0:T, 400:401], xnT[:, u, k, :],
                                         fold[:, 2 * C + 1 + k:2 * C + 2 + k], start=(k == 0), stop=(k == 1))
                    last.then_inc(S("a_ps"), 1)
                for u in range(2):
                    n = i * 2 + u + 1
                    pe.wait_ge(S("a_sb"), n)
                    pe.wait_ge(S(f"ctx_in{u}"), i * 32 + 32)
                    pe.matmul(pb[u][0:T, 0:KEYS], aT[:, u, :], ctT[:, u, :], start=True, stop=True
                              ).then_inc(S("s_ps"), 1)
                for u in range(2):
                    n = i * 2 + u + 1
                    pe.wait_ge(S("p_ready"), n)
                    for j in range(NKC):
                        last = pe.transpose(pb[2 + u][0:KC, j * T:(j + 1) * T],
                                            probs[:, u, j * KC:(j + 1) * KC], ident[0:T, 0:T])
                    last.then_inc(S("pT_ps"), 1)
                for u in range(2):
                    n = i * 2 + u + 1
                    pe.wait_ge(S("pT_sb"), n)
                    for j in range(NKC):
                        last = pe.matmul(pb[6 + u][:, 128:128 + T], ctN[:, u, j, :], probsT[:, u, j, :],
                                         start=(j == 0), stop=(j == NKC - 1))
                    last.then_inc(S("z_ps"), 1)
                for u in range(2):
                    n = i * 2 + u + 1
                    pe.wait_ge(S("z_sb"), n)
                    pe.matmul(pb[u][0:T, 0:D], zT[:, u, :], wv0[:], start=True, stop=True
                              ).then_inc(S("o_ps"), 1)
                turn(0, i, 1)
                route(0, i)

            def routing(lay):
                if lay == 0:
                    pe.wait_ge(S("cmax_part"), 1)
                    pe.transpose(pb[0][0:E, 0:T], cc[:], ident[0:T, 0:T]).then_inc(S("cmaxT"), 1)
                    pe.wait_ge(S("cdiag_ready"), 1)
                    pe.matmul(pb[1][0:T, 0:E], ones[0:E, 0:T], cdiag[:], start=True, stop=True
                              ).then_inc(S("cmax_all"), 1)

                    def colsum(n):
                        pe.wait_ge(S("colpart"), n)
                        pe.matmul(pb[0][0:T, 0:E], ones[0:T, 0:T], cl[:], start=True, stop=True
                                  ).then_inc(S("colsum"), 1)

                    colsum(1)
                    with pe.Fori(0, SINK_ITERS - 1) as j:
                        colsum(j + 2)
                pe.wait_ge(S("mask_ready"), lay + 1)
                rank = pb[2][0:T, 0:B * E]
                pe.matmul(rank, lower[:], m1h[:].rearrange("p b e -> p (b e)"), start=True, stop=False)
                for b in range(B - 1):
                    later = B - 1 - b
                    pe.matmul(pb[2][0:T, (b + 1) * E:B * E].rearrange("p (b e) -> p b e", e=E), ones[0:T, 0:T],
                              msk[:, b:b + 1, :].to_broadcast([T, later, E]), start=False, stop=False)
                pe.matmul(rank, lower[:], m2h[:].rearrange("p b e -> p (b e)"), start=False, stop=True)
                for b in range(B):
                    last = pe.matmul(pb[3][0:T, 0:E], ones[0:T, 0:T], msk[:, b, :], start=(b == 0),
                                     stop=(b == B - 1))
                last.then_inc(S("rank_ps"), 1)

            def experts(lay):
                for s in range(TILES):
                    g0 = lay * TILES + s
                    pe.wait_ge(S(f"xrow_in{g0 % 2}"), 16 * (g0 // 2 + 1))
                    if s >= 2:
                        pe.wait_ge(S("xT_sb"), g0 - 1)
                    for k in range(KD):
                        last = pe.transpose(pb[6 + s % 2][:, k * 128:(k + 1) * 128],
                                            xrow[:, g0 % 2, k * 128:(k + 1) * 128], ident[:])
                    last.then_inc(S("xrow_used"), 1)
                pe.wait_ge(S("xT_sb"), TILES * (lay + 1))
                pe.wait_ge(S("te_ready"), lay + 1)
                reg = pe.alloc_register(f"expert_at{lay}")
                for p in range(PHASES[lay]):
                    ph = sum(PHASES[:lay]) + p
                    G = ph * TILES
                    w = ph % 2
                    pe.wait_ge(S("w_lo"), (ph + 1) * E)
                    pe.wait_ge(S("w_hi"), (ph + 1) * E)

                    def gate_up(s, par, first):
                        pe.reg_load(reg, te[0:1, ds(s + 0, 1)])
                        off = pe.snap(reg, min_val=0, max_val=(E - 1) * EW)
                        offs[par] = off
                        if first is None:
                            pe.wait_ge(S("h_ready"), s + (G - 1))
                        elif G:
                            pe.wait_ge(S("h_ready"), G)
                        n = 0
                        for k in range(KD):
                            for st, mvg in ((xThi, whi), (xThi, wlo), (xTlo, whi)):
                                last = pe.matmul(pb[par][:, :], st_at(st, s, k), mvg[:, w, ds(off + k * 2 * FC, 2 * FC)],
                                                 start=(n == 0), stop=(n == 3 * KD - 1))
                                n += 1
                        last.then_inc(S("gu_ps"), 1)

                    offs = {}

                    def st_at(st, s, k):
                        if isinstance(s, int):
                            return st[:, s, k, :]
                        return st[:, ds(s.at, 1), k, :].rearrange("p o n -> p (o n)")

                    def turn_h(s, par):
                        pe.wait_ge(S("h_ready"), s + (G + 1))
                        if G or not isinstance(s, int) or s >= 2:
                            pe.wait_ge(S("hT_lo"), s + (G - 1))
                        for k in range(FC // 128):
                            last = pe.transpose(pb[2 + par][:, k * 128:(k + 1) * 128],
                                                hh[:, par, k * 128:(k + 1) * 128], ident[:])
                        last.then_inc(S("hT_ps"), 1)

                    def down(s, par):
                        pe.reg_load(reg, te[0:1, ds(s + 0, 1)])
                        off = pe.snap(reg, min_val=0, max_val=(E - 1) * EW)
                        pe.wait_ge(S("hT_lo"), s + (G + 1))
                        if G or not isinstance(s, int) or s >= 2:
                            pe.wait_ge(S("y_acc"), s + (G - 1))
                        n = 0
                        for k in range(FC // 128):
                            for st, mvg in ((hThi, whi), (hThi, wlo), (hTlo, whi)):
                                last = pe.matmul(pb[4 + par][:, 0:D], st[:, par, k, :],
                                                 mvg[:, w, ds(off + KD * 2 * FC + k * D, D)],
                                                 start=(n == 0), stop=(n == 3 * (FC // 128) - 1))
                                n += 1
                        last.then_inc(S("y_ps"), 1)

                    pipeline(gate_up, turn_h, down, eng=pe)

            routing(0)
            experts(0)

            with pe.Fori(0, 4) as i:
                turn(1, i, 0)
                for u in range(2):
                    b = i * 2 + u
                    pe.wait_ge(S("xnT_sb"), i * 4 + 2 + 2 * B)
                    pe.wait_ge(S(f"ctx_in{u}"), i * 16 + 16 + 4 * 32)
                    if u == 1:
                        pe.wait_ge(S("cat_ready"), i * 2 + 1)
                    for m in range(HP):
                        for k in range(KD):
                            pe.matmul(pb[7][:, m * T:(m + 1) * T], wq1[:, k, m * 128:(m + 1) * 128],
                                      xnT[:, u, k, :], start=(k == 0), stop=(k == 1))
                    for j in range(NKC):
                        pe.matmul(pb[4 + j // 2][0:KC, (j % 2) * D:(j % 2) * D + D], ctT[:, u, j * KC:(j + 1) * KC],
                                  wv1[:], start=True, stop=True)
                    for m in range(HP):
                        last = pe.matmul(pb[m][:, 0:KEYS], wk1[:, m * 128:(m + 1) * 128], ctT[:, u, :],
                                         start=True, stop=True)
                    last.then_inc(S("qkv_ps"), 1)
                    pe.wait_ge(S("k_sb"), b + 1)
                    pe.wait_ge(S("qv_sb"), b + 1)

                    def scores(j):
                        if j >= 2:
                            pe.wait_ge(S("e_ready"), b * HEADS + 2 * (j - 1))
                        for t in range(2):
                            h = 2 * j + t
                            r = 32 * (h % HP)
                            last = pe.matmul(pb[2 * (j % 2) + t][0:T, 0:KEYS], qT[r:r + DK, h // HP, :],
                                             kT[r:r + DK, h // HP, :], start=True, stop=True)
                        last.then_inc(S("ss_ps"), 1)

                    def turn_p(h):
                        pe.wait_ge(S("e_ready"), b * HEADS + h + 1)
                        if h >= 2:
                            pe.wait_ge(S(f"eT_sb{h % 2}"), b * (HEADS // 2) + h // 2)
                        for j in range(NKC):
                            last = pe.transpose(pb[4 + h % 2][0:KC, j * T:(j + 1) * T],
                                                probs[:, h % 4, j * KC:(j + 1) * KC], ident[0:T, 0:T])
                        last.then_inc(S("eT_ps"), 1)

                    def values(h):
                        pe.wait_ge(S(f"eT_sb{h % 2}"), b * (HEADS // 2) + h // 2 + 1)
                        for j in range(NKC):
                            last = pe.matmul(pb[6][0:T, h * DK:(h + 1) * DK], probsT[:, h % 2, j, :],
                                             v1[:, j, h * DK:(h + 1) * DK], start=(j == 0), stop=(j == NKC - 1))
                        last.then_inc(S("av_ps"), 1)

                    scores(0)
                    for j in range(HEADS // 2):
                        if j + 1 < HEADS // 2:
                            scores(j + 1)
                        turn_p(2 * j)
                        if j:
                            values(2 * j - 1)
                        turn_p(2 * j + 1)
                        values(2 * j)
                    values(HEADS - 1)
                    pe.wait_ge(S("cat_ready"), b + 1)
                    for k in range(KD):
                        last = pe.transpose(pb[7][:, k * T:(k + 1) * T], cat[:, k * 128:(k + 1) * 128],
                                            ident[0:T, 0:T])
                    last.then_inc(S("catT_ps"), 1)
                    pe.wait_ge(S("catT_sb"), b + 1)
                    for k in range(KD):
                        last = pe.matmul(pb[7][0:T, 256:256 + D], catT[:, k, :], wo1[:, k, :],
                                         start=(k == 0), stop=(k == 1))
                    last.then_inc(S("wo_ps"), 1)
                    pe.wait_ge(S("wo_used"), b + 1)
                turn(1, i, 1)
                route(1, i)
            routing(1)
            experts(1)

        def odd_out(act, b, h):
            act.wait_ge(S("eT_ps"), b * HEADS + h + 1)
            if h >= 2:
                act.wait_ge(S("av_ps"), b * HEADS + h - 1)
            nc.scalar.copy(probsT[:, 1, :, :].rearrange("p j t -> p (j t)"), pb[5][0:KC, 0:NKC * T]
                           ).then_inc(S("eT_sb1"), 1)

        @block.scalar
        def _(act):
            def xnT_out(lay, i, half):
                for u in range(2):
                    n = i * 4 + half * 2 + u + 1 + lay * 2 * B
                    act.wait_ge(S("xnT_ps"), n)
                    nc.scalar.copy(xnT[:, u, :, :].rearrange("p k t -> p (k t)"), pb[4 + u][:, 0:KD * T]
                                   ).then_inc(S("xnT_sb"), 1)
                    if half:
                        nc.scalar.copy(xn[:, ds(i * 2 + u, 1), :].rearrange("p o d -> p (o d)"), xnb[:, u, :]
                                       ).then_inc(S("xn_kept"), 1)

            def w_hi(c, v, m):
                act.wait_ge(S(f"w_in{v}"), m * 16 + 16)
                nc.scalar.mul(whi[:, c[0], ds(c[1] * EW, EW)], stage[:, v, :], WSCALE).then_inc(S("w_hi"), 1)

            with act.Fori(0, 4) as i:
                xnT_out(0, i, 0)
                for u in range(2):
                    act.wait_ge(S("a_ps"), i * 2 + u + 1)
                    nc.scalar.activation(aT[:, u, :], pb[6 + u][:, 0:T], ACT.Identity,
                                         bias=fold[:, 2 * C:2 * C + 1]).then_inc(S("a_sb"), 1)
                w_hi((0, i * 2), 0, i)
                for u in range(2):
                    act.wait_ge(S("nb_ready"), i * 2 + u + 1)
                    nc.scalar.activation(probs[:, u, :], pb[u][0:T, 0:KEYS], ACT.Exp, bias=nb0[:, u, :],
                                         accum_out=rs0[:, u, :]).then_inc(S("p_ready"), 1)
                w_hi((0, i * 2 + 1), 1, i)
                for u in range(2):
                    act.wait_ge(S("z_ps"), i * 2 + u + 1)
                    nc.scalar.copy(zT[:, u, :], pb[6 + u][:, 128:128 + T]).then_inc(S("z_sb"), 1)
                xnT_out(0, i, 1)

            def routing(lay):
                lv = la[:].rearrange("p b e -> p (b e)")
                pv = pi[:].rearrange("p b e -> p (b e)")
                n = S("act_in")
                if lay == 1:
                    act.wait_ge(n, 5 + 2 * 3 + 1)
                    nc.scalar.activation(pv, lv, ACT.Exp).then_inc(S("act_out"), 1)
                    return
                act.wait_ge(n, 1)
                nc.scalar.activation(pv, lv, ACT.Exp).then_inc(S("act_out"), 1)
                act.wait_ge(n, 2)
                nc.scalar.activation(rl[:], rr[:], ACT.Ln).then_inc(S("act_out"), 1)
                act.wait_ge(n, 3)
                nc.scalar.activation(pv, lv, ACT.Exp).then_inc(S("act_out"), 1)
                act.wait_ge(n, 4)
                nc.scalar.activation(cc[:], pb[0][0:T, 0:E], ACT.Ln).then_inc(S("act_out"), 1)
                act.wait_ge(n, 5)
                nc.scalar.activation(pv, lv, ACT.Exp).then_inc(S("act_out"), 1)
                for seg in range(3):
                    act.wait_ge(n, 5 + 2 * seg + 1)
                    nc.scalar.activation(rl[:], rr[:], ACT.Ln).then_inc(S("act_out"), 1)
                    nc.scalar.activation(tmp[:, 0, :], cc[:], ACT.Ln).then_inc(S("act_out"), 1)
                    act.wait_ge(n, 5 + 2 * seg + 2)
                    nc.scalar.activation(pv, lv, ACT.Exp).then_inc(S("act_out"), 1)

            def experts(lay):
                for s in range(TILES):
                    g0 = lay * TILES + s
                    act.wait_ge(S("xrow_used"), g0 + 1)
                    nc.scalar.copy(xThi[:, s, :, :].rearrange("p k n -> p (k n)"), pb[6 + s % 2][:, 0:KD * 128]
                                   ).then_inc(S("xT_hi"), 1)
                for p in range(PHASES[lay]):
                    ph = sum(PHASES[:lay]) + p
                    G = ph * TILES

                    def silu(s, par, first):
                        act.wait_ge(S("gu_ps"), s + (G + 1))
                        if first is None:
                            act.wait_ge(S("h_ready"), s + (G - 1))
                        elif G:
                            act.wait_ge(S("h_ready"), G)
                        nc.scalar.activation(sg[:, par, :], pb[par][:, 0:FC], ACT.Silu, scale=1.0 / WSCALE
                                             ).then_inc(S("silu_ready"), 1)

                    def hT_high(s, par):
                        act.wait_ge(S("hT_ps"), s + (G + 1))
                        if G or not isinstance(s, int) or s >= 2:
                            act.wait_ge(S("y_ps"), s + (G - 1))
                        nc.scalar.copy(hThi[:, par, :, :].rearrange("p k n -> p (k n)"), pb[2 + par][:, 0:FC]
                                       ).then_inc(S("hT_hi"), 1)

                    def split(i, v):
                        w_hi(((ph + 1) % 2, i * 2 + v), v, i + (ph + 1) * (E // 2))

                    pipeline(silu, hT_high, lambda s, par: None, split if ph + 1 < NPH else None, act)

            routing(0)
            act.wait_ge(S("zeroed"), 16)
            experts(0)
            with act.Fori(0, 4) as i:
                xnT_out(1, i, 0)
                for u in range(2):
                    b = i * 2 + u
                    act.wait_ge(S("qkv_ps"), b + 1)
                    for m in range(HP):
                        last = nc.scalar.activation(kT[:, m, :], pb[m][:, 0:KEYS], ACT.Identity,
                                                    bias=bk1[:, m:m + 1])
                    last.then_inc(S("k_sb"), 1)
                    for j in range(HEADS // 2):
                        act.wait_ge(S("nb1_ready"), b * (HEADS // 2) + j + 1)
                        for t in range(2):
                            h = 2 * j + t
                            if h >= 4:
                                act.wait_ge(S("eT_ps"), b * HEADS + h - 3)
                            nc.scalar.activation(probs[:, h % 4, :], pb[2 * (j % 2) + t][0:T, 0:KEYS], ACT.Exp,
                                                 bias=nb1[:, h:h + 1], scale=DK ** -0.5,
                                                 accum_out=rs1[:, h:h + 1]).then_inc(S("e_ready"), 1)
                        if j:
                            odd_out(act, b, 2 * j - 1)
                    odd_out(act, b, HEADS - 1)
                    act.wait_ge(S("catT_ps"), b + 1)
                    nc.scalar.copy(catT[:].rearrange("p k t -> p (k t)"), pb[7][:, 0:KD * T]
                                   ).then_inc(S("catT_sb"), 1)
                xnT_out(1, i, 1)
            routing(1)
            experts(1)

        @block.vector
        def _(dve):
            ch = Chain(dve, S("dve_step"))
            dve.wait_ge(S("fold_ps"), 1)
            nc.vector.tensor_copy(fold[:], pb[7][:, 0:2 * C + 4]).then_inc(S("fold_sb"), 1)
            dve.wait_ge(S("fold_sb"), 1)
            dve.wait_ge(S("x_in"), 16)
            dve.wait_ge(S("weights_in"), 16 * 15)
            dve.wait_ge(S("const"), 7)
            dve.wait_ge(S("pool_step"), 5)

            def carry(u):
                nc.vector.memset(carrier[:, u, :], 0.0)

            def xb(i, u):
                return x[:, ds(i * 2 + u, 1), :].rearrange("p o d -> p (o d)")

            def norm(lay, i, half):
                for u in range(2):
                    n = i * 4 + half * 2 + u + 1 + lay * 2 * B
                    carry(2 * u)
                    ch(nc.vector.bn_stats(stats[:, u, :], xb(i, u)))
                    carry(2 * u + 1)
                    ch(nc.vector.bn_aggr(mv[:, u, :], stats[:, u, :]))
                    nc.vector.tensor_scalar(vare[:, u, :], mv[:, u, 1:2], EPS, None, ALU.add
                                            ).then_inc(S("var_ready"), 1)
                for u in range(2):
                    n = i * 4 + half * 2 + u + 1 + lay * 2 * B
                    dve.wait_ge(S("rstd_ready"), n)
                    if half == 0:
                        kept = i * 2 + lay * B + 1
                        dve.wait_ge(S("xn_kept"), kept)
                    nc.vector.tensor_scalar(xnb[:, u, :], xb(i, u), mv[:, u, 0:1], rstd[:, u, :],
                                            ALU.subtract, ALU.mult).then_inc(S("ln_ready"), 1)

            def logits(lay, i):
                for u in range(2):
                    dve.wait_ge(S("logit_ps"), i * 2 + u + 1 + lay * B)
                    nc.vector.tensor_scalar(la[:, ds(i * 2 + u, 1), :].rearrange("p o e -> p (o e)"),
                                            pb[4 + u][0:T, 256:256 + E], -1.0 / SINK_EPS if lay == 0 else 1.0,
                                            None, ALU.mult).then_inc(S("la_ready"), 1)

            def w_lo(c, v, m):
                w, e, n = c
                dve.wait_ge(S(f"w_in{v}"), m * 16 + 16)
                dve.wait_ge(S("w_hi"), n)
                nc.vector.scalar_tensor_tensor(wlo[:, w, ds(e * EW, EW)], stage[:, v, :], WSCALE,
                                               whi[:, w, ds(e * EW, EW)], ALU.mult, ALU.subtract
                                               ).then_inc(S("w_lo"), 1)

            per = 2 * (2 * 2) + 2 * 2 + 2 * 2
            start = ch.now
            with dve.Fori(0, 4) as i:
                ch.enter(i, per, start)
                norm(0, i, 0)
                for u in range(2):
                    n = i * 2 + u + 1
                    dve.wait_ge(S("a_ps"), n)
                    nc.vector.tensor_scalar(qbk[:, u, :], pb[2 + u][0:T, 400:401], fold[0:T, 2 * C + 3:2 * C + 4],
                                            None, ALU.add).then_inc(S("qbk_ready"), 1)
                for u in range(2):
                    n = i * 2 + u + 1
                    dve.wait_ge(S("s_ps"), n)
                    dve.wait_ge(S("qbk_ready"), n)
                    ch(nc.vector.tensor_reduce(mx0[:, u, :], pb[u][0:T, 0:KEYS], AX.X, ALU.max))
                    ch(nc.vector.tensor_tensor(mx0[:, u, :], mx0[:, u, :], qbk[:, u, :], ALU.add))
                    nc.vector.tensor_tensor(nb0[:, u, :], qbk[:, u, :], mx0[:, u, :], ALU.subtract
                                            ).then_inc(S("nb_ready"), 1)
                w_lo((0, i * 2, i * 2 + 1), 0, i)
                for u in range(2):
                    dve.wait_ge(S("pT_ps"), i * 2 + u + 1)
                    nc.vector.tensor_copy(probsT[:, u, :, :].rearrange("p j t -> p (j t)"),
                                          pb[2 + u][0:KC, 0:NKC * T]).then_inc(S("pT_sb"), 1)
                w_lo((0, i * 2 + 1, i * 2 + 2), 1, i)
                for u in range(2):
                    dve.wait_ge(S("p_ready"), i * 2 + u + 1)
                    ch(nc.vector.reciprocal(rc0[:, u, :], rs0[:, u, :]))
                    dve.wait_ge(S("o_ps"), i * 2 + u + 1)
                    ch(nc.vector.scalar_tensor_tensor(upd[:, u, :], pb[u][0:T, 0:D], rc0[:, u, :], bv0[:],
                                                      ALU.mult, ALU.add))
                    nc.vector.tensor_tensor(xb(i, u), xb(i, u), upd[:, u, :], ALU.add).then_inc(S("x_upd"), 1)
                dve.wait_ge(S("x_upd"), i * 2 + 2)
                norm(0, i, 1)
                logits(0, i)
            ch.leave(per, 4, start)
            dve.wait_ge(S("la_ready"), B)

            def v3(t):
                return t[:]

            def over_e(t):
                return t[:].unsqueeze(2).to_broadcast([T, B, E])

            def over_b(t):
                return t.unsqueeze(1).to_broadcast([T, B, E])

            def routing(lay):
                a_in, a_out = S("act_in"), S("act_out")
                if lay == 0:
                    ch(nc.vector.tensor_reduce(rr[:], la[:], AX.X, ALU.max))
                    nc.vector.tensor_tensor(la[:], la[:], over_e(rr), ALU.subtract).then_inc(a_in, 1)
                    dve.wait_ge(a_out, 1)
                    nc.vector.tensor_reduce(rr[:], pi[:], AX.X, ALU.add).then_inc(a_in, 1)
                    dve.wait_ge(a_out, 2)
                    ch(nc.vector.tensor_tensor(la[:], la[:], over_e(rl), ALU.subtract))
                    nc.vector.tensor_reduce(cc[:], la[:].rearrange("p b e -> p e b"), AX.X, ALU.max
                                            ).then_inc(S("cmax_part"), 1)
                    dve.wait_ge(S("cmaxT"), 1)
                    ch(nc.vector.tensor_reduce(cm[:], pb[0][0:E, 0:T], AX.X, ALU.max))
                    nc.vector.tensor_scalar(cdiag[:], ident[0:E, 0:E], cm[:], None, ALU.mult
                                            ).then_inc(S("cdiag_ready"), 1)
                    dve.wait_ge(S("cmax_all"), 1)
                    ch(nc.vector.tensor_copy(cl[:], pb[1][0:T, 0:E]))
                    nc.vector.tensor_tensor(la[:], la[:], over_b(cl[:]), ALU.subtract).then_inc(a_in, 1)
                    dve.wait_ge(a_out, 3)
                    nc.vector.tensor_reduce(cl[:], pi[:].rearrange("p b e -> p e b"), AX.X, ALU.add
                                            ).then_inc(S("colpart"), 1)
                    dve.wait_ge(S("colsum"), 1)
                    nc.vector.tensor_copy(cl[:], pb[0][0:T, 0:E]).then_inc(a_in, 1)
                    dve.wait_ge(a_out, 4)
                    nc.vector.tensor_tensor(la[:], la[:], over_b(cc[:]), ALU.subtract).then_inc(a_in, 1)
                    dve.wait_ge(a_out, 5)
                    done = 0
                    for seg, turns in enumerate((7, 6, 6)):
                        ch(nc.vector.memset(cc[:], 1.0))
                        start, per = ch.now, 5
                        with dve.Fori(0, turns) as j:
                            ch.enter(j, per, start)
                            ch(nc.vector.tensor_tensor(tmp[:], pi[:], over_b(cc[:]), ALU.mult))
                            ch(nc.vector.tensor_reduce(rl[:], tmp[:], AX.X, ALU.add))
                            ch(nc.vector.reciprocal(rr[:], rl[:]))
                            ch(nc.vector.tensor_tensor(tmp[:], pi[:], over_e(rr), ALU.mult))
                            nc.vector.tensor_reduce(cl[:], tmp[:].rearrange("p b e -> p e b"), AX.X, ALU.add
                                                    ).then_inc(S("colpart"), 1)
                            dve.wait_ge(S("colsum"), j + (done + 2))
                            ch(nc.vector.reciprocal(cc[:], pb[0][0:T, 0:E]))
                        ch.leave(per, turns, start)
                        done += turns
                        nc.vector.tensor_copy(rl[:], rr[:]).then_inc(a_in, 1)
                        dve.wait_ge(a_out, 5 + 3 * seg + 2)
                        ch(nc.vector.tensor_tensor(la[:], la[:], over_e(rl), ALU.add))
                        nc.vector.tensor_tensor(la[:], la[:], over_b(tmp[:, 0, :]), ALU.add).then_inc(a_in, 1)
                        dve.wait_ge(a_out, 5 + 3 * seg + 3)
                else:
                    ch(nc.vector.tensor_reduce(rr[:], la[:], AX.X, ALU.max))
                    nc.vector.tensor_tensor(la[:], la[:], over_e(rr), ALU.subtract).then_inc(a_in, 1)
                    dve.wait_ge(a_out, 5 + 9 + 1)
                    ch(nc.vector.tensor_reduce(rr[:], pi[:], AX.X, ALU.add))
                    ch(nc.vector.reciprocal(rl[:], rr[:]))
                    ch(nc.vector.tensor_tensor(pi[:], pi[:], over_e(rl), ALU.mult))
                if lay == 0:
                    ch(nc.vector.scalar_tensor_tensor(pi[:], pi[:], 2.0 ** -126, pi[:], ALU.is_ge, ALU.mult))
                    ch(nc.vector.tensor_copy(wtop[:, 0, :, :], pi[:, :, 0:TOPK].rearrange("p b k -> p k b")))
                for k, hot in enumerate((m1h, m2h)):
                    top = rr[:] if lay == 0 else wtop[:, 1, k, :]
                    ch(nc.vector.tensor_reduce(top, pi[:], AX.X, ALU.max))
                    ch(nc.vector.tensor_tensor(tmp[:], pi[:], top.unsqueeze(2).to_broadcast([T, B, E]),
                                               ALU.is_equal))
                    ch(nc.vector.tensor_tensor(tmp[:], tmp[:], iota_e[:], ALU.mult))
                    ch(nc.vector.tensor_reduce(rl[:], tmp[:], AX.X, ALU.min))
                    ch(nc.vector.tensor_tensor(hot[:], iota_e[:], over_e(rl), ALU.is_equal))
                    if k == 0:
                        ch(nc.vector.scalar_tensor_tensor(pi[:], hot[:], -2.0, pi[:], ALU.mult, ALU.add))
                nc.vector.tensor_tensor(msk[:], m1h[:], m2h[:], ALU.add).then_inc(S("mask_ready"), 1)
                dve.wait_ge(S("rank_ps"), lay + 1)
                ch(nc.vector.tensor_copy(cl[:], pb[3][0:T, 0:E]))
                ch(nc.vector.tensor_tensor(kcmp[:], cl[:].unsqueeze(2).to_broadcast([T, E, CPE]), kgrid[:],
                                           ALU.is_gt))
                ch(nc.vector.tensor_reduce(nt[:], kcmp[:], AX.X, ALU.add))
                ch(nc.vector.tensor_tensor(tcmp[:], nt[:].unsqueeze(1).to_broadcast([T, E, E]), tri[:], ALU.mult))
                ch(nc.vector.tensor_reduce(tb[:], tcmp[:], AX.X, ALU.add))
                ch(nc.vector.tensor_tensor(tend[:], tb[:], nt[:], ALU.add))
                ch(nc.vector.tensor_tensor(scmp[:], tend[:].unsqueeze(1).to_broadcast([T, TILES, E]), sgrid[:],
                                           ALU.is_le))
                ch(nc.vector.tensor_reduce(tef[:], scmp[:], AX.X, ALU.add))
                ch(nc.vector.tensor_scalar(tef[:], tef[:], E - 1.0, float(EW), ALU.min, ALU.mult))
                nc.vector.tensor_copy(te[:], tef[:]).then_inc(S("te_ready"), 1)
                ch(nc.vector.tensor_scalar(tb[:], tb[:], float(SLOTS), None, ALU.mult))
                ch(nc.vector.tensor_tensor(slotv[:], pb[2][0:T, 0:B * E].rearrange("p (b e) -> p b e", e=E),
                                           over_b(tb[:]), ALU.add))
                for k, hot in enumerate((m1h, m2h)):
                    ch(nc.vector.tensor_tensor(tmp[:], slotv[:], hot[:], ALU.mult))
                    ch(nc.vector.tensor_reduce(sf[:], tmp[:], AX.X, ALU.add))
                    ins = nc.vector.tensor_copy(slot[:, k, :], sf[:])
                    if k == 0:
                        ch(ins)
                ins.then_inc(S("slots_ready"), 1)

            def experts(lay):
                for s in range(TILES):
                    g0 = lay * TILES + s
                    dve.wait_ge(S("xT_hi"), g0 + 1)
                    nc.vector.tensor_tensor(xTlo[:, s, :, :].rearrange("p k n -> p (k n)"),
                                            pb[6 + s % 2][:, 0:KD * 128],
                                            xThi[:, s, :, :].rearrange("p k n -> p (k n)"), ALU.subtract
                                            ).then_inc(S("xT_sb"), 1)
                for p in range(PHASES[lay]):
                    ph = sum(PHASES[:lay]) + p
                    G = ph * TILES

                    def product(s, par, first):
                        dve.wait_ge(S("silu_ready"), s + (G + 1))
                        if first is None:
                            dve.wait_ge(S("hT_ps"), s + (G - 1))
                        elif G:
                            dve.wait_ge(S("hT_ps"), G)
                        nc.vector.scalar_tensor_tensor(hh[:, par, :], pb[par][:, FC:2 * FC], 1.0 / WSCALE,
                                                       sg[:, par, :], ALU.mult, ALU.mult
                                                       ).then_inc(S("h_ready"), 1)

                    def hT_low(s, par):
                        dve.wait_ge(S("hT_hi"), s + (G + 1))
                        nc.vector.tensor_tensor(hTlo[:, par, :, :].rearrange("p k n -> p (k n)"),
                                                pb[2 + par][:, 0:FC],
                                                hThi[:, par, :, :].rearrange("p k n -> p (k n)"), ALU.subtract
                                                ).then_inc(S("hT_lo"), 1)

                    def add(s, par):
                        dve.wait_ge(S("y_ps"), s + (G + 1))
                        to = yacc[:, s, :] if isinstance(s, int) else yacc[:, ds(s.at, 1), :].rearrange("p o d -> p (o d)")
                        if p == 0:
                            ins = nc.vector.tensor_scalar(to, pb[4 + par][:, 0:D], 1.0 / WSCALE, None, ALU.mult)
                        else:
                            ins = nc.vector.scalar_tensor_tensor(to, pb[4 + par][:, 0:D], 1.0 / WSCALE, to,
                                                                 ALU.mult, ALU.add)
                        ins.then_inc(S("y_acc"), 1)

                    def split(i, v):
                        w_lo(((ph + 1) % 2, i * 2 + v, i * 2 + v + (ph + 1) * E + 1), v, i + (ph + 1) * (E // 2))

                    pipeline(product, hT_low, add, split if ph + 1 < NPH else None, dve)

            def combine(lay):
                for b in range(B):
                    dve.wait_ge(S(f"gathered{b}"), 16 * TOPK * (lay + 1))
                    ch(nc.vector.scalar_tensor_tensor(x[:, b, :], yg[:, 0, b, :], wtop[:, lay, 0, b:b + 1],
                                                      x[:, b, :], ALU.mult, ALU.add))
                    ins = nc.vector.scalar_tensor_tensor(x[:, b, :], yg[:, 1, b, :], wtop[:, lay, 1, b:b + 1],
                                                         x[:, b, :], ALU.mult, ALU.add)
                    if lay == 0:
                        ch(ins)
                    else:
                        ins.then_inc(S("x_done"), 1)

            routing(0)
            experts(0)
            combine(0)
            per = 2 * (2 * 2) + 2 * 3
            start = ch.now
            with dve.Fori(0, 4) as i:
                ch.enter(i, per, start)
                norm(1, i, 0)
                for u in range(2):
                    b = i * 2 + u
                    dve.wait_ge(S("qkv_ps"), b + 1)
                    nc.vector.tensor_tensor(qT[:], pb[7][:, 0:HP * T].rearrange("p (m t) -> p m t", t=T),
                                            bq1[:].unsqueeze(2).to_broadcast([128, HP, T]), ALU.add
                                            ).then_inc(S("q_sb"), 1)
                    nc.vector.tensor_copy(v1[:, 0:2, :].rearrange("p j d -> p (j d)"), pb[4][0:KC, 0:2 * D]
                                          ).then_inc(S("q_sb"), 1)
                    nc.vector.tensor_copy(v1[:, 2, :], pb[5][0:KC, 0:D]).then_inc(S("qv_sb"), 1)

                    def even_out(h):
                        dve.wait_ge(S("eT_ps"), b * HEADS + h + 1)
                        if h >= 2:
                            dve.wait_ge(S("av_ps"), b * HEADS + h - 1)
                        nc.vector.tensor_copy(probsT[:, 0, :, :].rearrange("p j t -> p (j t)"),
                                              pb[4][0:KC, 0:NKC * T]).then_inc(S("eT_sb0"), 1)

                    for j in range(HEADS // 2):
                        dve.wait_ge(S("ss_ps"), b * (HEADS // 2) + j + 1)
                        for t in range(2):
                            mm = nc.vector.tensor_reduce(mx1[:, j % 2, t:t + 1], pb[2 * (j % 2) + t][0:T, 0:KEYS],
                                                         AX.X, ALU.max)
                            mm.then_inc(S("mx1_ready"), 1)
                        dve.wait_ge(S("mx1_ready"), b * HEADS + 2 * j + 2)
                        nc.vector.tensor_scalar(nb1[:, 2 * j:2 * j + 2], mx1[:, j % 2, :], -(DK ** -0.5), None,
                                                ALU.mult).then_inc(S("nb1_ready"), 1)
                        if j:
                            even_out(2 * j - 2)
                    even_out(HEADS - 2)
                    dve.wait_ge(S("e_ready"), b * HEADS + HEADS)
                    ch(nc.vector.reciprocal(rc1[:], rs1[:]))
                    dve.wait_ge(S("av_ps"), b * HEADS + HEADS)
                    ch(nc.vector.tensor_tensor(cat[:].rearrange("p (h d) -> p h d", d=DK),
                                               pb[6][0:T, 0:D].rearrange("p (h d) -> p h d", d=DK),
                                               rc1[:].unsqueeze(2).to_broadcast([T, HEADS, DK]), ALU.mult))
                    nc.vector.tensor_tensor(cat[:], cat[:], bv1[:], ALU.add).then_inc(S("cat_ready"), 1)
                    dve.wait_ge(S("wo_ps"), b + 1)
                    nc.vector.tensor_tensor(upd[:, u, :], pb[7][0:T, 256:256 + D], bo1[:], ALU.add
                                            ).then_inc(S("wo_used"), 1)
                    dve.wait_ge(S("wo_used"), b + 1)
                    ch(nc.vector.tensor_tensor(xb(i, u), xb(i, u), upd[:, u, :], ALU.add))
                norm(1, i, 1)
                logits(1, i)
            ch.leave(per, 4, start)
            dve.wait_ge(S("la_ready"), 2 * B)
            routing(1)
            experts(1)
            combine(1)


_SHAPES = {}


def kernel(**inputs):
    import numpy as np
    import concourse.bacc as bacc
    from concourse.bass_utils import run_bass_kernel_spmd as run

    f = {k: np.asarray(v) for k, v in inputs.items()}

    def chunks(w, k):
        return w.reshape(k, 128, -1).transpose(1, 0, 2)

    def pad_heads(w):
        r = w.reshape(w.shape[0], HEADS, DK)
        return np.concatenate([r, np.zeros_like(r)], axis=2).reshape(w.shape[0], 2 * HEADS * DK)

    ctx = f["ctx_512"]
    arr = {
        "x": f["x"],
        "ctxT": ctx.transpose(2, 0, 1),
        "ctxN": ctx.reshape(B, NKC, KC, C).transpose(2, 0, 1, 3),
        "wq0T": chunks(f["L0_xattn_Wq"].T, KD),
        "wk0T": chunks(f["L0_xattn_Wk"].T, KD),
        "wv0": f["L0_xattn_Wv"],
        "bq0": f["L0_xattn_bq"].reshape(KD, 128).T,
        "bk0": f["L0_xattn_bk"].reshape(KD, 128).T,
        "bv0": np.broadcast_to(f["L0_xattn_bv"], (T, D)),
        "wq1": chunks(pad_heads(f["L1_xattn_Wq"]), KD),
        "wk1": pad_heads(f["L1_xattn_Wk"]),
        "wv1": f["L1_xattn_Wv"],
        "wo1": chunks(f["L1_xattn_Wo"], KD),
        "bq1": pad_heads(f["L1_xattn_bq"][None])[0].reshape(HP, 128).T,
        "bk1": pad_heads(f["L1_xattn_bk"][None])[0].reshape(HP, 128).T,
        "bv1": np.broadcast_to(f["L1_xattn_bv"], (T, D)),
        "bo1": np.broadcast_to(f["L1_xattn_bo"], (T, D)),
        "router": np.stack([chunks(f["L0_ffn_gate_W"].T, KD), chunks(f["L1_ffn_router_w"].T, KD)], axis=1),
    }
    w1, w2 = f["L1_ffn_w1"], f["L1_ffn_w2"]
    inter = w1.shape[1] // 2
    layers = ((f["L0_ffn_W_gate"], f["L0_ffn_W_up"], f["L0_ffn_W_down"]), (w1[:, :inter], w1[:, inter:], w2))
    stream = []
    for (gate, up, down), n in zip(layers, PHASES):
        for p in range(n):
            for e in range(E):
                g = chunks(gate[e, p * FC:(p + 1) * FC].T, KD)
                u = chunks(up[e, p * FC:(p + 1) * FC].T, KD)
                d = chunks(down[e][:, p * FC:(p + 1) * FC].T, FC // 128)
                gu = np.concatenate([g, u], axis=2).reshape(128, -1)
                stream.append(np.concatenate([gu, d.reshape(128, -1)], axis=1))
    arr["wst"] = np.stack(stream, axis=1)

    nc = bacc.Bacc("TRN2", target_bir_lowering=False, num_devices=1)
    arrays, aps = {}, {}
    for name, v in arr.items():
        v = np.ascontiguousarray(v)
        arrays[f"in_{name}"] = v
        aps[name] = nc.dram_tensor(f"in_{name}", v.shape, mybir.dt.from_np(v.dtype), kind="ExternalInput").ap()
    aps["out"] = nc.dram_tensor("out_x", (B, T, D), F32, kind="ExternalOutput").ap()
    build(nc, aps)
    r = run(nc, [arrays], core_ids=[0])
    return r.results[0]["out_x"]
```

```python
from contextlib import ExitStack

import concourse.bass as bass
from concourse import mybir

ALU = mybir.AluOpType
ACT = mybir.ActivationFunctionType
F32 = mybir.dt.float32
F16 = mybir.dt.float16
I32 = mybir.dt.int32
U32 = mybir.dt.uint32
AX = mybir.AxisListType
ds = bass.ds

B, T, D = 8, 112, 256
KEYS, C = 375, 128
KC, NKC = 125, 3
KD = D // 128
E = 8
TOPK = 2
HEADS, DK = 16, 16
HP = 4
NTOK = B * T
SLOTS = 128
TILES = (NTOK * TOPK + E * (SLOTS - 1)) // SLOTS
CPE = NTOK // SLOTS
FC = 256
PHASES = (1024 // FC, 512 // FC)
EW = KD * 2 * FC + (FC // 128) * D
WSCALE = 256.0
EPS = 1e-5
SINK_ITERS, SINK_EPS = 20, 0.05
SINK_SEGS = 3
SINK_TURNS = (SINK_ITERS - 2) // SINK_SEGS
assert SINK_SEGS * SINK_TURNS + 2 == SINK_ITERS


class Chain:

    def __init__(self, eng, sem):
        self.eng, self.sem, self.base, self.n = eng, sem, 0, 0

    def __call__(self, ins):
        self.n += 1
        ins.then_inc(self.sem, 1)
        self.eng.wait_ge(self.sem, self.base + self.n)

    def enter(self, i, per, start):
        self.base, self.n = start + i * per, 0

    def leave(self, per, trips, start):
        assert self.n == per, (self.n, per)
        self.base, self.n = start + trips * per, 0

    @property
    def now(self):
        return self.base + self.n


class Step:

    def __init__(self, i, k):
        self.i, self.k = i, k

    def __add__(self, n):
        return self.i * 4 + (self.k + n)

    @property
    def at(self):
        return self + 0


class Batch:

    def __init__(self, i, k):
        self.i, self.k = i, k

    def __add__(self, n):
        return Batch(self.i, self.k + n)


def count(b, per, n):
    if isinstance(b, Batch):
        assert b.k * per + n >= 0
        return b.i * (2 * per) + (b.k * per + n)
    return b * per + n


def parity(b):
    return (b.k if isinstance(b, Batch) else b) % 2


TAIL = {0: "rcT", 3: "wo", 12: "xnT2", 14: "logits"}
NEXT = {1: "v0", 5: "xnT1", 6: "v1", 7: "q", 8: "k0", 9: "k1", 10: "k2", 11: "k3"}
BOTH = {**TAIL, **NEXT}


def unit_count(b, kind, name):
    order = [kind[h] for h in sorted(kind)]
    if isinstance(b, Batch) or b in range(1, B):
        first = count(b, len(BOTH), 2 * len(NEXT) - len(BOTH))
    else:
        first = {-1: 0, 0: len(NEXT), B: B * len(BOTH) - len(TAIL)}[b]
    return first + order.index(name)


def norm_count(b, second):
    if second:
        return count(b, 2, 2 * B + 4) if isinstance(b, Batch) or b < B - 2 else 2 * B + b + B + 1
    return count(b, 2, 2 * B - 1) if isinstance(b, Batch) or b > 1 else 2 * B + b + 1


def unit_bank(kind, name):
    return 6 + [kind[h] for h in sorted(kind)].index(name) % 2


def slot3(h):
    return 1 if h == HEADS - 1 else h % 3


def before3(h):
    return {0: -4, 1: -1, 2: -2, HEADS - 1: HEADS - 3}.get(h, h - 3)


def build(nc, a):
    ctx = ExitStack()
    with ctx:
        def sb(name, shape, dt=F32):
            return ctx.enter_context(nc.sbuf_tensor(name, shape, dt))

        sems = {}

        def S(name):
            if name not in sems:
                sems[name] = ctx.enter_context(nc.semaphore(name))
            return sems[name]

        pb = [ctx.enter_context(nc.psum_tensor(f"bank{i}", [128, 512], F32)) for i in range(8)]
        pall = None

        xg_dram = nc.dram_tensor("expert_rows", [TILES * SLOTS, D], F32, kind="Internal").ap()
        ys_dram = nc.dram_tensor("expert_results", [TILES * SLOTS, D], F32, kind="Internal").ap()

        x = sb("x", [T, B, D])
        xn = sb("xn", [T, B, D])
        whi = sb("whi", [128, 2, E * EW], F16)
        wlo = sb("wlo", [128, 2, E * EW], F16)
        stage = sb("stage", [128, 2, EW])
        ident = sb("ident", [128, 128])
        ones = sb("ones", [128, 128])
        lower16 = sb("lower16", [T, T], F16)
        ones16 = sb("ones16", [T, T], F16)
        lower = sb("lower", [T, T])
        ctT = sb("ctT", [128, 2, KEYS])
        bq0 = sb("bq0", [128, KD])
        bk0 = sb("bk0", [128, KD])
        bv0 = sb("bv0", [T, D])
        fold = sb("fold", [128, 2 * C + 4])
        wq1 = sb("wq1", [128, KD, HP * 128])
        wk1 = sb("wk1", [C, HP * 128])
        wv1 = sb("wv1", [C, D])
        wo1 = sb("wo1", [128, HP, D])
        bq1 = sb("bq1", [128, HP])
        bq1s = sb("bq1s", [128, HP])
        bk1 = sb("bk1", [128, HP])
        lowrow = sb("lowrow", [128, 1])
        bv1 = sb("bv1", [128, HP])
        bo1 = sb("bo1", [T, D])
        router = sb("router", [128, 2, KD, E])
        xnb = sb("xnb", [T, 2, D])
        stats = sb("stats", [T, 2, 6])
        mv = sb("mv", [T, 2, 2])
        vare = sb("vare", [T, 2, 1])
        rstd = sb("rstd", [T, 2, 1])
        carrier = sb("carrier", [T, 4, 1])
        mhalf = sb("mhalf", [T, 1])
        xnT = sb("xnT", [128, 2, KD, T])
        aT = sb("aT", [128, 2, T])
        qbk = sb("qbk", [T, 2, 1])
        mx0 = sb("mx0", [T, 2, 1])
        nb0 = sb("nb0", [T, 2, 1])
        rs0 = sb("rs0", [T, 2, 1])
        rc0 = sb("rc0", [T, 2, 1])
        upd = sb("upd", [T, 2, D])
        zT = sb("zT", [C, 2, T])
        la = sb("la", [T, B, E])
        pi = sb("pi", [T, B, E])
        tmp = sb("tmp", [T, B, E])
        msk = sb("msk", [T, B, E], F16)
        m1h = sb("m1h", [T, B, E], F16)
        m2h = sb("m2h", [T, B, E], F16)
        slotv = sb("slotv", [T, B, E])
        rr = sb("rr", [T, B])
        rl = sb("rl", [T, B])
        cc = sb("cc", [T, E])
        cl = sb("cl", [T, E])
        cm = sb("cm", [E, 1])
        cdiag = sb("cdiag", [E, E])
        wtop = sb("wtop", [T, 2, TOPK, B])
        sf = sb("sf", [T, B])
        slot = sb("slot", [T, TOPK, B], U32)
        iota_e = sb("iota_e", [T, B, E])
        kgrid = sb("kgrid", [T, E, CPE])
        kcmp = sb("kcmp", [T, E, CPE])
        nt = sb("nt", [T, E])
        tri = sb("tri", [T, E, E])
        tcmp = sb("tcmp", [T, E, E])
        tb = sb("tb", [T, E])
        tend = sb("tend", [T, E])
        sgrid = sb("sgrid", [T, TILES, E])
        scmp = sb("scmp", [T, TILES, E])
        tef = sb("tef", [T, TILES])
        te = sb("te", [T, TILES], I32)
        sg = sb("sg", [128, 2, FC])
        hh = sb("hh", [128, 2, FC])
        hThi = sb("hThi", [128, 2, FC // 128, 128], F16)
        hTlo = sb("hTlo", [128, 2, FC // 128, 128], F16)

        REGION = 10752
        region = sb("region", [128, REGION])
        XT = TILES * KD * 128
        xThi = region[:, 0:XT // 2].bitcast(F16).rearrange("p (s k n) -> p s k n", k=KD, n=128)
        xTlo = region[:, XT // 2:XT].bitcast(F16).rearrange("p (s k n) -> p s k n", k=KD, n=128)
        yacc = region[:, XT:XT + TILES * D].rearrange("p (s d) -> p s d", d=D)
        yg = whi[0:T, 1, 0:2 * TOPK * B * D].bitcast(F32).rearrange("p (k b d) -> p k b d", k=TOPK, b=B)
        at = [0]

        def carve(p, *dims):
            n = 1
            for v in dims:
                n *= v
            v = region[0:p, at[0]:at[0] + n]
            at[0] += n
            assert at[0] <= REGION, at
            if len(dims) == 1:
                return v
            names = "abcd"[:len(dims)]
            return v.rearrange(f"p ({' '.join(names)}) -> p {' '.join(names)}",
                               **{k: d for k, d in zip(names[1:], dims[1:])})

        def carve16(p, *dims):
            n = 1
            for v in dims:
                n *= v
            v = carve(p, (n + 1) // 2).bitcast(F16)[:, 0:n]
            names = "abcd"[:len(dims)]
            return v.rearrange(f"p ({' '.join(names)}) -> p {' '.join(names)}",
                               **{k: d for k, d in zip(names[1:], dims[1:])})

        NP = 4
        probs = carve(T, NP, KEYS)
        both = at[0]
        probsT = carve(KC, 2, NKC, T)
        ctN = carve(KC, 2, NKC, C)
        wq0T = carve(128, KD, D)
        wk0T = carve(128, KD, C)
        wv0 = carve(C, D)
        at[0] = both
        kst = carve16(128, 2 * HP, KEYS)
        kf = carve(128, HP, KEYS)
        kmh = carve16(128, KEYS)
        qf = carve(128, HP, T)
        qhi = carve16(128, 2 * HP, T)
        qlo = carve16(128, 2 * HP, T)
        v1h = carve16(KC, 2 * NKC, HEADS, 2, DK)
        eThi = carve16(KC, 3, NKC * T)
        eTlo = carve16(KC, 3, NKC * T)
        rce = carve(T, HEADS * 2 * DK)
        rcT = carve(128, HP * T)
        catT = carve(128, HP * T)
        nb1 = carve(T, HEADS)
        rs1 = carve(T, 2, HEADS)
        rc1 = carve(T, HEADS)

        def bc(ap, shape):
            return ap.to_broadcast(shape) if hasattr(ap, "to_broadcast") else ap.broadcast(shape)

        block = ctx.enter_context(nc.Block())
        NPH = sum(PHASES)

        def w_src(c0):
            return a["wst"][:, c0]

        def rows_in(eng, lay):
            eng.wait_ge(S("scattered"), 16 * TOPK * B * (lay + 1))
            n = TILES // 3
            for part in range(3):
                eng.dma_start(yacc[:, part * n:(part + 1) * n, :],
                              xg_dram.rearrange("(s p) d -> p s d", p=SLOTS)[:, part * n:(part + 1) * n, :]
                              ).then_inc(S(f"rows_in{part}"), 16)

        def results(eng, lay):
            eng.wait_ge(S("y_acc"), TILES * sum(PHASES[:lay + 1]))
            eng.dma_start(ys_dram.rearrange("(s p) d -> p s d", p=SLOTS), yacc).then_inc(S("ys_out"), 16)

        @block.sync
        def _(sp):
            sp.dma_start(x[:], a["x"].rearrange("b t d -> t b d")).then_inc(S("x_in"), 16)
            for dst, src in ((wq0T, "wq0T"), (wk0T, "wk0T"), (wv0, "wv0"), (bq0, "bq0"), (bk0, "bk0"),
                             (bv0, "bv0"), (wq1, "wq1"), (wk1, "wk1"), (wv1, "wv1"), (wo1, "wo1"),
                             (bq1, "bq1"), (bk1, "bk1"), (bv1, "bv1"), (bo1, "bo1"), (router, "router"), (lowrow, "lowrow")):
                sp.dma_start(dst[:], a[src]).then_inc(S("weights_in"), 16)

            def ctx_in(lay, i, u, wait):
                if wait is not None:
                    if lay == 0:
                        sp.wait_ge(S("z_ps"), wait)
                    else:
                        sp.wait_ge(S("k_sb"), wait * HP)
                sp.dma_start(ctT[:, u, :], a["ctxT"][:, ds(i * 2 + u, 1), :].rearrange("p o k -> p (o k)")
                             ).then_inc(S(f"ctx_in{u}"), 16)
                if lay == 0:
                    sp.dma_start(ctN[:, u, :, :], a["ctxN"][:, ds(i * 2 + u, 1), :, :].rearrange(
                        "p o j c -> p (o j) c")).then_inc(S(f"ctx_in{u}"), 16)

            def chunk_in(c, v, wait):
                if wait is not None:
                    sp.wait_ge(S("w_hi"), wait * 2)
                    sp.wait_ge(S("w_lo"), wait * 2)
                sp.dma_start(stage[:, v, :], a["wst"][:, ds(c, 1), :].rearrange("p o n -> p (o n)")
                             ).then_inc(S(f"w_in{v}"), 16)

            for u in range(2):
                ctx_in(0, 0, u, None)
            for v in range(2):
                chunk_in(v, v, None)
            with sp.Fori(1, 4) as i:
                for u in range(2):
                    ctx_in(0, i, u, i * 2 - 1 + u)
                for v in range(2):
                    chunk_in(i * 2 + v, v, i * 2 + v - 1)
            for u in range(2):
                sp.wait_ge(S("z_ps"), B)
                ctx_in(1, 0, u, None)
            rows_in(sp, 0)
            with sp.Fori(E // 2, (PHASES[0] + 1) * E // 2) as i:
                for v in range(2):
                    chunk_in(i * 2 + v, v, i * 2 + v - 1)
            results(sp, 0)
            with sp.Fori(1, 4) as i:
                for u in range(2):
                    ctx_in(1, i, u, i * 2 - 1 + u)
            rows_in(sp, 1)
            with sp.Fori((PHASES[0] + 1) * E // 2, NPH * E // 2) as i:
                for v in range(2):
                    chunk_in(i * 2 + v, v, i * 2 + v - 1)
            results(sp, 1)
            for b in range(0, B, 2):
                sp.wait_ge(S("x_done"), b + 2)
                sp.dma_start(a["out"][b:b + 2].rearrange("b t d -> t b d"), x[:, b:b + 2, :]
                             ).then_inc(S("out_done"), 16)
            sp.wait_ge(S("out_done"), 16 * B // 2)

        @block.gpsimd
        def _(pool):
            g = Chain(pool, S("pool_step"))
            g(pool.memset(ident[:], 0.0))
            g(pool.affine_select(out=ident[:], in_=ident[:], compare_op=ALU.not_equal, fill=1.0, base=0,
                                 pattern=[[-1, 128]], channel_multiplier=1))
            pool.memset(xnb[:], 0.0).then_inc(S("xn_kept"), 1)
            pool.memset(mhalf[:], -0.5).then_inc(S("const"), 1)
            pool.memset(ones[:], 1.0).then_inc(S("const"), 1)
            g(pool.memset(lower[:], 1.0))
            pool.affine_select(out=lower[:], in_=lower[:], compare_op=ALU.is_gt, fill=0.0, base=0,
                               pattern=[[1, T]], channel_multiplier=-1).then_inc(S("const"), 1)
            pool.iota(iota_e[:], [[0, B], [1, E]], base=-E, channel_multiplier=0,
                      allow_small_or_imprecise_dtypes=True).then_inc(S("const"), 1)
            pool.iota(kgrid[:], [[0, E], [SLOTS, CPE]], base=0, channel_multiplier=0,
                      allow_small_or_imprecise_dtypes=True).then_inc(S("const"), 1)
            pool.iota(sgrid[:], [[1, TILES], [0, E]], base=0, channel_multiplier=0,
                      allow_small_or_imprecise_dtypes=True).then_inc(S("const"), 1)
            g(pool.memset(tri[:], 1.0))
            pool.affine_select(out=tri[:], in_=tri[:], compare_op=ALU.is_gt, fill=0.0, base=0,
                               pattern=[[1, E], [-1, E]], channel_multiplier=0).then_inc(S("const"), 1)
            zeros = whi[:, 1, 0:2 * TILES * D].bitcast(F32)
            g(pool.memset(zeros, 0.0))
            pool.dma_start(xg_dram.rearrange("(s p) d -> p s d", p=SLOTS),
                           zeros.rearrange("p (s d) -> p s d", d=D)).then_inc(S("zeroed"), 16)

            def root(n, u):
                pool.wait_ge(S("var_ready"), n)
                pool.tensor_tensor(rstd[:, u, :], vare[:, u, :], mhalf[:], ALU.pow
                                   ).then_inc(S("rstd_ready"), 1)

            def widen(n):
                pool.wait_ge(S("rc_ready"), n)
                pool.tensor_tensor(rce[:].rearrange("p (h d) -> p h d", h=HEADS),
                                   rc1[:].unsqueeze(2).to_broadcast([T, HEADS, 2 * DK]),
                                   ones[0:T, 0:2 * DK].unsqueeze(1).to_broadcast([T, HEADS, 2 * DK]),
                                   ALU.mult).then_inc(S("rc_wide"), 1)

            def gather(b):
                for k in range(TOPK):
                    pool.indirect_dma_start(
                        out=yg[:, k, b, :], out_offset=None, in_=ys_dram,
                        in_offset=bass.IndirectOffsetOnAxis(ap=slot[:, k, b:b + 1], axis=0),
                    ).then_inc(S(f"gathered{b}"), 16)

            def q_halves(b):
                u = parity(b)
                pool.wait_ge(S("q_in"), count(b, 1, 1))
                pool.tensor_tensor(qhi[:, u * HP:(u + 1) * HP, :], qf[:], ones[:, 0:1].unsqueeze(2).to_broadcast(
                    [128, HP, T]), ALU.mult).then_inc(S("q_hi"), 1)
                pool.wait_ge(S("q_hi"), count(b, 1, 1))
                pool.tensor_tensor(qlo[:, u * HP:(u + 1) * HP, :], qf[:], qhi[:, u * HP:(u + 1) * HP, :],
                                   ALU.subtract).then_inc(S("q_sb"), 1)

            def k_halves(b, m):
                pool.wait_ge(S("k_in"), count(b, HP, m + 1))
                if isinstance(b, Batch) or b or m:
                    pool.wait_ge(S("k_sb"), count(b, HP, m))
                pool.tensor_tensor(kmh[:], kf[:, m, :], lowrow[:].to_broadcast([128, KEYS]), ALU.mult
                                   ).then_inc(S("k_hi"), 1)
                pool.wait_ge(S("k_hi"), count(b, HP, m + 1))
                pool.tensor_tensor(kst[:, parity(b) * HP + m, :], kf[:, m, :], kmh[:], ALU.subtract
                                   ).then_inc(S("k_sb"), 1)

            for lay in range(2):
                if lay == 0:
                    with pool.Fori(0, 4) as i:
                        for half in range(2):
                            for u in range(2):
                                root(i * 4 + (half * 2 + u + 1), u)
                else:
                    gather(0)
                    gather(1)
                    root(2 * B + 1, 0)
                    for b in range(2, B):
                        gather(b)
                    q_halves(0)
                    for m in range(HP):
                        k_halves(0, m)
                    root(2 * B + 2, 0)
                    q_halves(1)
                    for m in range(HP):
                        k_halves(1, m)
                    with pool.Fori(0, (B - 2) // 2) as i:
                        for b in (Batch(i, 1), Batch(i, 2)):
                            widen(count(b, 1, 0))
                            root(norm_count(b + 1, 0), 0)
                            root(norm_count(b + -1, 1), 1)
                            q_halves(b + 1)
                            for m in range(HP):
                                k_halves(b + 1, m)
                    for b in (B - 2, B - 1):
                        widen(b + 1)
                        root(norm_count(b, 1), 1)
                pool.wait_ge(S("slots_ready"), lay + 1)
                pool.wait_ge(S("zeroed"), 16)
                pool.wait_ge(S("xn_kept"), B * (lay + 1) + 1)
                for k in range(TOPK):
                    for b in range(B):
                        pool.indirect_dma_start(
                            out=xg_dram, out_offset=bass.IndirectOffsetOnAxis(ap=slot[:, k, b:b + 1], axis=0),
                            in_=xn[:, b, :], in_offset=None).then_inc(S("scattered"), 16)
                pool.wait_ge(S("ys_out"), 16 * (lay + 1))
                if lay == 1:
                    for b in range(B):
                        gather(b)

        def pipeline(A, Bf, Cf, extra=None, eng=None):
            def step(s, par):
                A(s, par, None)
                Bf(Step(s.i, s.k - 1) if isinstance(s, Step) else s - 1, 1 - par)
                Cf(Step(s.i, s.k - 2) if isinstance(s, Step) else s - 2, par)

            A(0, 0, 0)
            A(1, 1, 1)
            Bf(0, 0)
            for s in (2, 3):
                step(s, s % 2)
            with eng.Fori(0, 4) as i:
                for q in range(4):
                    step(Step(i, 4 + q), q % 2)
                    if extra is not None:
                        extra(i, q // 2, q % 2)
            step(TILES - 1, 0)
            last = TILES - 1
            Bf(last, last % 2)
            Cf(last - 1, (last - 1) % 2)
            Cf(last, last % 2)

        @block.tensor
        def _(pe):
            pe.wait_ge(S("weights_in"), 16 * 16)
            pe.wait_ge(S("const"), 7)
            pe.wait_ge(S("pool_step"), 4)
            f = pb[7]
            for k in range(KD):
                for e in range(KD):
                    pe.matmul(f[:, k * C:(k + 1) * C], wq0T[:, e, k * 128:(k + 1) * 128], wk0T[:, e, :],
                              start=(e == 0), stop=(e == KD - 1))
            for e in range(KD):
                pe.matmul(f[:, 2 * C:2 * C + 1], wk0T[:, e, :], bq0[:, e:e + 1], start=(e == 0), stop=(e == 1))
            for k in range(KD):
                for e in range(KD):
                    pe.matmul(f[:, 2 * C + 1 + k:2 * C + 2 + k], wq0T[:, e, k * 128:(k + 1) * 128],
                              bk0[:, e:e + 1], start=(e == 0), stop=(e == 1))
            for e in range(KD):
                last = pe.matmul(f[:, 2 * C + 3:2 * C + 4], bq0[:, e:e + 1].to_broadcast([128, 128]),
                                 bk0[:, e:e + 1], start=(e == 0), stop=(e == 1))
            for m in range(HP):
                last = pe.matmul(pb[6][0:T, 0:D], bv1[:, m:m + 1].to_broadcast([128, T]), wo1[:, m, :],
                                 start=(m == 0), stop=(m == HP - 1))
            last.then_inc(S("fold_ps"), 1)
            pe.wait_ge(S("fold_sb"), 1)

            def turn(lay, i, half):
                for u in range(2):
                    n = i * 4 + half * 2 + u + 1 + lay * 2 * B
                    pe.wait_ge(S("ln_ready"), n)
                    for k in range(KD):
                        last = pe.transpose(pb[4 + u][:, k * T:(k + 1) * T], xnb[:, u, k * 128:(k + 1) * 128],
                                            ident[0:T, 0:T])
                    last.then_inc(S("xnT_ps"), 1)

            def route(lay, i):
                for u in range(2):
                    pe.wait_ge(S("xnT_sb"), i * 4 + 2 + u + 1 + lay * 2 * B)
                    for k in range(KD):
                        last = pe.matmul(pb[4 + u][0:T, 256:256 + E], xnT[:, u, k, :], router[:, lay, k, :],
                                         start=(k == 0), stop=(k == 1))
                    last.then_inc(S("logit_ps"), 1)

            with pe.Fori(0, 4) as i:
                turn(0, i, 0)
                for u in range(2):
                    n = i * 2 + u + 1
                    pe.wait_ge(S("xnT_sb"), i * 4 + u + 1)
                    for k in range(KD):
                        pe.matmul(pb[6 + u][:, 0:T], fold[:, k * C:(k + 1) * C], xnT[:, u, k, :],
                                  start=(k == 0), stop=(k == 1))
                    for k in range(KD):
                        last = pe.matmul(pb[2 + u][0:T, 400:401], xnT[:, u, k, :],
                                         fold[:, 2 * C + 1 + k:2 * C + 2 + k], start=(k == 0), stop=(k == 1))
                    last.then_inc(S("a_ps"), 1)
                for u in range(2):
                    n = i * 2 + u + 1
                    pe.wait_ge(S("a_sb"), n)
                    pe.wait_ge(S(f"ctx_in{u}"), i * 32 + 32)
                    pe.matmul(pb[u][0:T, 0:KEYS], aT[:, u, :], ctT[:, u, :], start=True, stop=True
                              ).then_inc(S("s_ps"), 1)
                for u in range(2):
                    n = i * 2 + u + 1
                    pe.wait_ge(S("p_ready"), n)
                    for j in range(NKC):
                        last = pe.transpose(pb[2 + u][0:KC, j * T:(j + 1) * T],
                                            probs[:, u, j * KC:(j + 1) * KC], ident[0:T, 0:T])
                    last.then_inc(S("pT_ps"), 1)
                for u in range(2):
                    n = i * 2 + u + 1
                    pe.wait_ge(S("pT_sb"), n)
                    for j in range(NKC):
                        last = pe.matmul(pb[6 + u][:, 128:128 + T], ctN[:, u, j, :], probsT[:, u, j, :],
                                         start=(j == 0), stop=(j == NKC - 1))
                    last.then_inc(S("z_ps"), 1)
                for u in range(2):
                    n = i * 2 + u + 1
                    pe.wait_ge(S("z_sb"), n)
                    pe.matmul(pb[u][0:T, 0:D], zT[:, u, :], wv0[:], start=True, stop=True
                              ).then_inc(S("o_ps"), 1)
                turn(0, i, 1)
                route(0, i)

            def routing(lay):
                if lay == 0:
                    pe.wait_ge(S("cmax_part"), 1)
                    pe.transpose(pb[0][0:E, 0:T], cc[:], ident[0:T, 0:T]).then_inc(S("cmaxT"), 1)
                    pe.wait_ge(S("cdiag_ready"), 1)
                    pe.matmul(pb[1][0:T, 0:E], ones[0:E, 0:T], cdiag[:], start=True, stop=True
                              ).then_inc(S("cmax_all"), 1)

                    def colsum(n):
                        pe.wait_ge(S("colpart"), n)
                        pe.matmul(pb[0][0:T, 0:E], ones[0:T, 0:T], cl[:], start=True, stop=True
                                  ).then_inc(S("colsum"), 1)

                    colsum(1)
                    colsum(2)
                    with pe.Fori(0, SINK_SEGS) as j:
                        for k in range(SINK_TURNS):
                            colsum(j * SINK_TURNS + (3 + k))
                pe.wait_ge(S("mask_ready"), lay + 1)
                rank = pb[2][0:T, 0:B * E]
                pe.matmul(rank, lower16[:], m1h[:].rearrange("p b e -> p (b e)"), start=True, stop=False)
                for b in range(B - 1):
                    later = B - 1 - b
                    pe.matmul(pb[2][0:T, (b + 1) * E:B * E].rearrange("p (b e) -> p b e", e=E), ones16[:],
                              msk[:, b:b + 1, :].to_broadcast([T, later, E]), start=False, stop=False)
                pe.matmul(rank, lower16[:], m2h[:].rearrange("p b e -> p (b e)"), start=False, stop=True)
                for b in range(B):
                    last = pe.matmul(pb[3][0:T, 0:E], ones16[:], msk[:, b, :], start=(b == 0),
                                     stop=(b == B - 1))
                last.then_inc(S("rank_ps"), 1)

            def experts(lay):
                for s in range(TILES):
                    g0 = lay * TILES + s
                    pe.wait_ge(S(f"rows_in{s // (TILES // 3)}"), 16 * (lay + 1))
                    if s >= 8:
                        pe.wait_ge(S("xT_sb"), g0 - 7)
                    for k in range(KD):
                        last = pe.transpose(pb[s % 8][:, k * 128:(k + 1) * 128],
                                            yacc[:, s, k * 128:(k + 1) * 128], ident[:])
                    last.then_inc(S("rows_turned"), 1)
                pe.wait_ge(S("xT_sb"), TILES * (lay + 1))
                pe.wait_ge(S("te_ready"), lay + 1)
                regs = [pe.alloc_register(f"expert_at{lay}{q}") for q in range(4)]

                def expert_at(s):
                    return regs[(s.k if isinstance(s, Step) else s) % 4]

                for p in range(PHASES[lay]):
                    ph = sum(PHASES[:lay]) + p
                    G = ph * TILES
                    w = ph % 2
                    pe.wait_ge(S("w_lo"), (ph + 1) * E * 2)
                    pe.wait_ge(S("w_hi"), (ph + 1) * E * 2)

                    def gate_up(s, par, first):
                        pe.reg_load(expert_at(s), te[0:1, ds(s + 0, 1)])
                        off = pe.snap(expert_at(s), min_val=0, max_val=(E - 1) * EW)
                        if first is None:
                            pe.wait_ge(S("h_ready"), s + (G - 1))
                        elif G:
                            pe.wait_ge(S("h_ready"), G)
                        n = 0
                        for k in range(KD):
                            for st, mvg in ((xThi, whi), (xThi, wlo), (xTlo, whi)):
                                last = pe.matmul(pb[par][:, :], st_at(st, s, k), mvg[:, w, ds(off + k * 2 * FC, 2 * FC)],
                                                 start=(n == 0), stop=(n == 3 * KD - 1))
                                n += 1
                        last.then_inc(S("gu_ps"), 1)

                    def st_at(st, s, k):
                        if isinstance(s, int):
                            return st[:, s, k, :]
                        return st[:, ds(s.at, 1), k, :].rearrange("p o n -> p (o n)")

                    def turn_h(s, par):
                        pe.wait_ge(S("h_ready"), s + (G + 1))
                        if G or not isinstance(s, int) or s >= 2:
                            pe.wait_ge(S("hT_lo"), s + (G - 1))
                        for k in range(FC // 128):
                            last = pe.transpose(pb[2 + par][:, k * 128:(k + 1) * 128],
                                                hh[:, par, k * 128:(k + 1) * 128], ident[:])
                        last.then_inc(S("hT_ps"), 1)

                    def down(s, par):
                        off = pe.snap(expert_at(s), min_val=0, max_val=(E - 1) * EW)
                        pe.wait_ge(S("hT_lo"), s + (G + 1))
                        if G or not isinstance(s, int) or s >= 2:
                            pe.wait_ge(S("y_acc"), s + (G - 1))
                        n = 0
                        for k in range(FC // 128):
                            for st, mvg in ((hThi, whi), (hThi, wlo), (hTlo, whi)):
                                last = pe.matmul(pb[4 + par][:, 0:D], st[:, par, k, :],
                                                 mvg[:, w, ds(off + KD * 2 * FC + k * D, D)],
                                                 start=(n == 0), stop=(n == 3 * (FC // 128) - 1))
                                n += 1
                        last.then_inc(S("y_ps"), 1)

                    pipeline(gate_up, turn_h, down, eng=pe)

            routing(0)
            experts(0)

            def taken(name, of):
                if name in ("xnT1", "xnT2"):
                    pe.wait_ge(S("xnT_sb"), norm_count(of, int(name == "xnT2")))
                elif name == "q":
                    pe.wait_ge(S("q_in"), count(of, 1, 1))
                elif name in ("v0", "v1"):
                    pe.wait_ge(S("v_sb"), count(of, 2, 1 + int(name == "v1")))
                elif name[0] == "k":
                    pe.wait_ge(S("k_in"), count(of, HP, int(name[1]) + 1))
                elif name == "rcT":
                    pe.wait_ge(S("rcT_sb"), count(of, 1, 1))
                elif name == "wo":
                    pe.wait_ge(S("wo_used"), count(of, 1, 1))
                else:
                    pe.wait_ge(S("la_ready"), count(of, 1, B + 1))

            def unit(b, kind, name, of):
                w = pb[unit_bank(kind, name)]
                u = parity(of)
                order = [kind[h] for h in sorted(kind)]
                before = order.index(name) - 2
                if before >= 0:
                    taken(order[before], b + 1 if order[before] in NEXT.values() else b + -1)
                elif before == -2 and (isinstance(b, Batch) or b >= 0):
                    taken("k3", b if isinstance(b, Batch) or b < B else b + -1)
                    if isinstance(b, Batch) or b >= 2:
                        taken("logits", b + -2)
                if name in ("xnT1", "xnT2"):
                    half = int(name == "xnT2")
                    pe.wait_ge(S("ln_ready"), norm_count(of, half))
                    for k in range(KD):
                        last = pe.transpose(w[:, k * T:(k + 1) * T], xnb[:, half, k * 128:(k + 1) * 128],
                                            ident[0:T, 0:T])
                elif name == "q":
                    pe.wait_ge(S("xnT_sb"), norm_count(of, 0))
                    for m in range(HP):
                        for k in range(KD):
                            last = pe.matmul(w[:, m * T:(m + 1) * T], wq1[:, k, m * 128:(m + 1) * 128],
                                             xnT[:, 0, k, :], start=(k == 0), stop=(k == 1))
                elif name in ("v0", "v1"):
                    if name == "v0":
                        trips = of.i * 16 + (of.k // 2) * 16 if isinstance(of, Batch) else of // 2 * 16
                        pe.wait_ge(S(f"ctx_in{u}"), trips + (4 * 32 + 16))
                    for j in ((0, 1), (2,))[int(name == "v1")]:
                        last = pe.matmul(w[0:KC, (j % 2) * D:(j % 2) * D + D], ctT[:, u, j * KC:(j + 1) * KC],
                                         wv1[:], start=True, stop=True)
                elif name[0] == "k":
                    m = int(name[1])
                    last = pe.matmul(w[:, 0:KEYS], wk1[:, m * 128:(m + 1) * 128], ctT[:, u, :],
                                     start=True, stop=True)
                elif name == "rcT":
                    pe.wait_ge(S("rc_wide"), count(of, 1, 1))
                    for m in range(HP):
                        last = pe.transpose(w[:, m * T:(m + 1) * T], rce[:, m * 128:(m + 1) * 128],
                                            ident[0:T, 0:T])
                elif name == "wo":
                    pe.wait_ge(S("cat_ready"), count(of, 1, 1))
                    for m in range(HP):
                        last = pe.matmul(w[0:T, 0:D], catT[:, m * T:(m + 1) * T], wo1[:, m, :],
                                         start=(m == 0), stop=(m == HP - 1))
                else:
                    pe.wait_ge(S("xnT_sb"), norm_count(of, 1))
                    for k in range(KD):
                        last = pe.matmul(w[0:T, 0:E], xnT[:, 1, k, :], router[:, 1, k, :],
                                         start=(k == 0), stop=(k == 1))
                last.then_inc(S("unit_ps"), 1)

            def scores(b, h):
                r, m, u = 32 * (h % HP), h // HP, parity(b)
                if isinstance(b, Batch) or b > 0 or h >= 3:
                    pe.wait_ge(S("e_ready"), count(b, HEADS, before3(h) + 1))
                if h == 0:
                    pe.wait_ge(S("q_sb"), count(b, 1, 1))
                if h % HP == 0:
                    pe.wait_ge(S("k_sb"), count(b, HP, m + 1))
                to = pb[slot3(h)][0:T, 0:KEYS]
                pe.matmul(to, qhi[r:r + 2 * DK, u * HP + m, :], kst[r:r + 2 * DK, u * HP + m, :],
                          start=True, stop=False)
                pe.matmul(to, qlo[r:r + DK, u * HP + m, :], kst[r:r + DK, u * HP + m, :],
                          start=False, stop=True).then_inc(S("ss_ps"), 1)

            def turn_p(b, h):
                pe.wait_ge(S("e_ready"), count(b, HEADS, h + 1))
                if isinstance(b, Batch) or b > 0 or h >= 2:
                    pe.wait_ge(S("eT_lo"), count(b, HEADS, h - 1))
                for j in range(NKC):
                    last = pe.transpose(pb[3 + h % 2][0:KC, j * T:(j + 1) * T],
                                        probs[:, h % NP, j * KC:(j + 1) * KC], ident[0:T, 0:T])
                last.then_inc(S("eT_ps"), 1)

            def values(b, h):
                u = parity(b)
                pe.wait_ge(S("eT_lo"), count(b, HEADS, h + 1))
                if h == 0:
                    pe.wait_ge(S("v_sb"), count(b, 2, 2))
                    if isinstance(b, Batch) or b > 0:
                        pe.wait_ge(S("cat_ready"), count(b, 1, 0))
                r = 32 * (h % HP)
                to = pb[5][r:r + 2 * DK, (h // HP) * T:(h // HP + 1) * T]
                for n, half in enumerate((eThi, eTlo)):
                    for j in range(NKC):
                        last = pe.matmul(to, v1h[:, u * NKC + j, h, :, :].rearrange("p a d -> p (a d)"),
                                         half[:, slot3(h), j * T:(j + 1) * T],
                                         start=(n == 0 and j == 0), stop=(n == 1 and j == NKC - 1))
                last.then_inc(S("av_ps"), 1)

            def heads(b, kind, first=False, final=False):
                for h in range(HEADS):
                    if h + 2 < HEADS:
                        scores(b, h + 2)
                    elif not final:
                        scores(b + 1, h + 2 - HEADS)
                    turn_p(b, h)
                    if h >= 2:
                        values(b, h - 2)
                    elif not first:
                        values(b + -1, HEADS + h - 2)
                    if h in kind:
                        unit(b, kind, kind[h], b + 1 if kind[h] in NEXT.values() else b + -1)

            pe.wait_ge(S("ln_ready"), norm_count(0, 0))
            for name in NEXT.values():
                unit(-1, NEXT, name, 0)
            scores(0, 0)
            scores(0, 1)
            heads(0, NEXT, first=True)
            with pe.Fori(0, (B - 2) // 2) as i:
                heads(Batch(i, 1), BOTH)
                heads(Batch(i, 2), BOTH)
            heads(B - 1, TAIL, final=True)
            values(B - 1, HEADS - 2)
            values(B - 1, HEADS - 1)
            for name in TAIL.values():
                unit(B, TAIL, name, B - 1)
            routing(1)
            experts(1)

        @block.scalar
        def _(act):
            def xnT_out(lay, i, half):
                for u in range(2):
                    n = i * 4 + half * 2 + u + 1 + lay * 2 * B
                    act.wait_ge(S("xnT_ps"), n)
                    nc.scalar.copy(xnT[:, u, :, :].rearrange("p k t -> p (k t)"), pb[4 + u][:, 0:KD * T]
                                   ).then_inc(S("xnT_sb"), 1)
                    if half:
                        nc.scalar.copy(xn[:, ds(i * 2 + u, 1), :].rearrange("p o d -> p (o d)"), xnb[:, u, :]
                                       ).then_inc(S("xn_kept"), 1)

            def w_hi(c, v, m, half):
                act.wait_ge(S(f"w_in{v}"), m * 16 + 16)
                nc.scalar.mul(whi[:, c[0], ds(c[1] * EW + half * (EW // 2), EW // 2)],
                              stage[:, v, half * (EW // 2):(half + 1) * (EW // 2)], WSCALE
                              ).then_inc(S("w_hi"), 1)

            with act.Fori(0, 4) as i:
                xnT_out(0, i, 0)
                for u in range(2):
                    act.wait_ge(S("a_ps"), i * 2 + u + 1)
                    nc.scalar.activation(aT[:, u, :], pb[6 + u][:, 0:T], ACT.Identity,
                                         bias=fold[:, 2 * C:2 * C + 1]).then_inc(S("a_sb"), 1)
                w_hi((0, i * 2), 0, i, 0)
                w_hi((0, i * 2), 0, i, 1)
                for u in range(2):
                    act.wait_ge(S("nb_ready"), i * 2 + u + 1)
                    nc.scalar.activation(probs[:, u, :], pb[u][0:T, 0:KEYS], ACT.Exp, bias=nb0[:, u, :],
                                         accum_out=rs0[:, u, :]).then_inc(S("p_ready"), 1)
                w_hi((0, i * 2 + 1), 1, i, 0)
                w_hi((0, i * 2 + 1), 1, i, 1)
                for u in range(2):
                    act.wait_ge(S("z_ps"), i * 2 + u + 1)
                    nc.scalar.copy(zT[:, u, :], pb[6 + u][:, 128:128 + T]).then_inc(S("z_sb"), 1)
                xnT_out(0, i, 1)

            def routing(lay):
                lv = la[:].rearrange("p b e -> p (b e)")
                pv = pi[:].rearrange("p b e -> p (b e)")
                n = S("act_in")
                if lay == 1:
                    act.wait_ge(n, 5 + 2 * 3 + 1)
                    nc.scalar.activation(pv, lv, ACT.Exp).then_inc(S("act_out"), 1)
                    return
                act.wait_ge(n, 1)
                nc.scalar.activation(pv, lv, ACT.Exp).then_inc(S("act_out"), 1)
                act.wait_ge(n, 2)
                nc.scalar.activation(rl[:], rr[:], ACT.Ln).then_inc(S("act_out"), 1)
                act.wait_ge(n, 3)
                nc.scalar.activation(pv, lv, ACT.Exp).then_inc(S("act_out"), 1)
                act.wait_ge(n, 4)
                nc.scalar.activation(cc[:], pb[0][0:T, 0:E], ACT.Ln).then_inc(S("act_out"), 1)
                act.wait_ge(n, 5)
                nc.scalar.activation(pv, lv, ACT.Exp).then_inc(S("act_out"), 1)
                with act.Fori(0, SINK_SEGS) as i:
                    act.wait_ge(n, i * 2 + 6)
                    nc.scalar.activation(rl[:], rr[:], ACT.Ln).then_inc(S("act_out"), 1)
                    nc.scalar.activation(tmp[:, 0, :], cc[:], ACT.Ln).then_inc(S("act_out"), 1)
                    act.wait_ge(n, i * 2 + 7)
                    nc.scalar.activation(pv, lv, ACT.Exp).then_inc(S("act_out"), 1)

            def experts(lay):
                for s in range(TILES):
                    g0 = lay * TILES + s
                    act.wait_ge(S("rows_turned"), g0 + 1)
                    nc.scalar.copy(xThi[:, s, :, :].rearrange("p k n -> p (k n)"), pb[s % 8][:, 0:KD * 128]
                                   ).then_inc(S("xT_hi"), 1)
                for p in range(PHASES[lay]):
                    ph = sum(PHASES[:lay]) + p
                    G = ph * TILES

                    def silu(s, par, first):
                        act.wait_ge(S("gu_ps"), s + (G + 1))
                        if first is None:
                            act.wait_ge(S("h_ready"), s + (G - 1))
                        elif G:
                            act.wait_ge(S("h_ready"), G)
                        nc.scalar.activation(sg[:, par, :], pb[par][:, 0:FC], ACT.Silu, scale=1.0 / WSCALE
                                             ).then_inc(S("silu_ready"), 1)

                    def hT_high(s, par):
                        act.wait_ge(S("hT_ps"), s + (G + 1))
                        if G or not isinstance(s, int) or s >= 2:
                            act.wait_ge(S("y_ps"), s + (G - 1))
                        nc.scalar.copy(hThi[:, par, :, :].rearrange("p k n -> p (k n)"), pb[2 + par][:, 0:FC]
                                       ).then_inc(S("hT_hi"), 1)

                    def split(i, v, half):
                        w_hi(((ph + 1) % 2, i * 2 + v), v, i + (ph + 1) * (E // 2), half)

                    pipeline(silu, hT_high, lambda s, par: None, split if ph + 1 < NPH else None, act)

            routing(0)
            act.wait_ge(S("zeroed"), 16)
            experts(0)
            def unit(b, kind, name, of):
                n = unit_count(b, kind, name)
                u, w = parity(of), pb[unit_bank(kind, name)]
                if name in ("q", "wo", "logits"):
                    return
                act.wait_ge(S("unit_ps"), n + 1)
                if name in ("xnT1", "xnT2"):
                    half = int(name == "xnT2")
                    nc.scalar.copy(xnT[:, half, :, :].rearrange("p k t -> p (k t)"), w[:, 0:KD * T]
                                   ).then_inc(S("xnT_sb"), 1)
                    if half:
                        nc.scalar.copy(xn_of(of), xnb[:, 1, :]).then_inc(S("xn_kept"), 1)
                elif name in ("v0", "v1"):
                    for j in ((0, 1), (2,))[int(name == "v1")]:
                        last = nc.scalar.copy(v1h[:, u * NKC + j, :, 0, :],
                                              w[0:KC, (j % 2) * D:(j % 2) * D + D].rearrange(
                                                  "p (h d) -> p h d", d=DK))
                    last.then_inc(S("v_hi"), 1)
                elif name[0] == "k":
                    m = int(name[1])
                    if isinstance(of, Batch) or of > 0:
                        act.wait_ge(S("k_sb"), count(of, HP, m + 1 - HP))
                    nc.scalar.activation(kf[:, m, :], w[:, 0:KEYS], ACT.Identity, bias=bk1[:, m:m + 1]
                                         ).then_inc(S("k_in"), 1)
                else:
                    nc.scalar.copy(rcT[:], w[:, 0:HP * T]).then_inc(S("rcT_sb"), 1)

            def xn_of(b):
                if isinstance(b, Batch):
                    return xn[:, ds(b.i * 2 + b.k, 1), :].rearrange("p o d -> p (o d)")
                return xn[:, b, :]

            def exponent(b, h):
                act.wait_ge(S("nb1_ready"), count(b, HEADS, h + 1))
                nc.scalar.activation(probs[:, h % NP, :], pb[slot3(h)][0:T, 0:KEYS], ACT.Exp,
                                     bias=nb1[:, h:h + 1], accum_out=rs1[:, parity(b), h:h + 1]
                                     ).then_inc(S("e_ready"), 1)

            def eT_high(b, h):
                act.wait_ge(S("eT_ps"), count(b, HEADS, h + 1))
                if isinstance(b, Batch) or b > 0 or h >= 3:
                    act.wait_ge(S("av_ps"), count(b, HEADS, before3(h) + 1))
                nc.scalar.copy(eThi[:, slot3(h), :], pb[3 + h % 2][0:KC, 0:NKC * T]).then_inc(S("eT_hi"), 1)

            def heads(b, kind, first=False, final=False):
                for h in range(HEADS):
                    if h + 1 < HEADS:
                        exponent(b, h + 1)
                    elif not final:
                        exponent(b + 1, 0)
                    if h - 1 in kind:
                        unit(b, kind, kind[h - 1], b + 1 if kind[h - 1] in NEXT.values() else b + -1)
                    eT_high(b, h)

            for name in NEXT.values():
                unit(-1, NEXT, name, 0)
            exponent(0, 0)
            heads(0, NEXT, first=True)
            with act.Fori(0, (B - 2) // 2) as i:
                heads(Batch(i, 1), BOTH)
                heads(Batch(i, 2), BOTH)
            heads(B - 1, TAIL, final=True)
            for name in TAIL.values():
                unit(B, TAIL, name, B - 1)
            routing(1)
            experts(1)

        @block.vector
        def _(dve):
            ch = Chain(dve, S("dve_step"))
            dve.wait_ge(S("fold_ps"), 1)
            nc.vector.tensor_copy(fold[:], pb[7][:, 0:2 * C + 4]).then_inc(S("fold_sb"), 1)
            dve.wait_ge(S("fold_sb"), 1)
            dve.wait_ge(S("x_in"), 16)
            dve.wait_ge(S("weights_in"), 16 * 16)
            dve.wait_ge(S("const"), 7)
            dve.wait_ge(S("pool_step"), 5)

            ch(nc.vector.tensor_copy(lower16[:], lower[:]))
            ch(nc.vector.tensor_copy(ones16[:], ones[0:T, 0:T]))

            def carry(u):
                nc.vector.memset(carrier[:, u, :], 0.0)

            ch(nc.vector.scalar_tensor_tensor(bo1[:], pb[6][0:T, 0:D], 0.5, bo1[:], ALU.mult, ALU.add))
            ch(nc.vector.tensor_scalar(bq1s[:], bq1[:], DK ** -0.5, None, ALU.mult))

            def xb(i, u):
                return x[:, ds(i * 2 + u, 1), :].rearrange("p o d -> p (o d)")

            def norm(lay, i, half):
                for u in range(2):
                    n = i * 4 + half * 2 + u + 1 + lay * 2 * B
                    carry(2 * u)
                    ch(nc.vector.bn_stats(stats[:, u, :], xb(i, u)))
                    carry(2 * u + 1)
                    ch(nc.vector.bn_aggr(mv[:, u, :], stats[:, u, :]))
                    nc.vector.tensor_scalar(vare[:, u, :], mv[:, u, 1:2], EPS, None, ALU.add
                                            ).then_inc(S("var_ready"), 1)
                for u in range(2):
                    n = i * 4 + half * 2 + u + 1 + lay * 2 * B
                    dve.wait_ge(S("rstd_ready"), n)
                    if half == 0:
                        kept = i * 2 + lay * B + 1
                        dve.wait_ge(S("xn_kept"), kept)
                    nc.vector.tensor_scalar(xnb[:, u, :], xb(i, u), mv[:, u, 0:1], rstd[:, u, :],
                                            ALU.subtract, ALU.mult).then_inc(S("ln_ready"), 1)

            def logits(lay, i):
                for u in range(2):
                    dve.wait_ge(S("logit_ps"), i * 2 + u + 1 + lay * B)
                    nc.vector.tensor_scalar(la[:, ds(i * 2 + u, 1), :].rearrange("p o e -> p (o e)"),
                                            pb[4 + u][0:T, 256:256 + E], -1.0 / SINK_EPS if lay == 0 else 1.0,
                                            None, ALU.mult).then_inc(S("la_ready"), 1)

            def w_lo(w, e, chunk, v, m, half):
                at = ds(e * EW + half * (EW // 2), EW // 2)
                dve.wait_ge(S(f"w_in{v}"), m * 16 + 16)
                dve.wait_ge(S("w_hi"), chunk * 2 + (1 + half))
                nc.vector.scalar_tensor_tensor(wlo[:, w, at], stage[:, v, half * (EW // 2):(half + 1) * (EW // 2)],
                                               WSCALE, whi[:, w, at], ALU.mult, ALU.subtract
                                               ).then_inc(S("w_lo"), 1)

            per = 2 * (2 * 2) + 2 * 2 + 2 * 2
            start = ch.now
            with dve.Fori(0, 4) as i:
                ch.enter(i, per, start)
                norm(0, i, 0)
                for u in range(2):
                    n = i * 2 + u + 1
                    dve.wait_ge(S("a_ps"), n)
                    nc.vector.tensor_scalar(qbk[:, u, :], pb[2 + u][0:T, 400:401], fold[0:T, 2 * C + 3:2 * C + 4],
                                            None, ALU.add).then_inc(S("qbk_ready"), 1)
                for u in range(2):
                    n = i * 2 + u + 1
                    dve.wait_ge(S("s_ps"), n)
                    dve.wait_ge(S("qbk_ready"), n)
                    ch(nc.vector.tensor_reduce(mx0[:, u, :], pb[u][0:T, 0:KEYS], AX.X, ALU.max))
                    ch(nc.vector.tensor_tensor(mx0[:, u, :], mx0[:, u, :], qbk[:, u, :], ALU.add))
                    nc.vector.tensor_tensor(nb0[:, u, :], qbk[:, u, :], mx0[:, u, :], ALU.subtract
                                            ).then_inc(S("nb_ready"), 1)
                for half in range(2):
                    w_lo(0, i * 2, i * 2, 0, i, half)
                for u in range(2):
                    dve.wait_ge(S("pT_ps"), i * 2 + u + 1)
                    nc.vector.tensor_copy(probsT[:, u, :, :].rearrange("p j t -> p (j t)"),
                                          pb[2 + u][0:KC, 0:NKC * T]).then_inc(S("pT_sb"), 1)
                for half in range(2):
                    w_lo(0, i * 2 + 1, i * 2 + 1, 1, i, half)
                for u in range(2):
                    dve.wait_ge(S("p_ready"), i * 2 + u + 1)
                    ch(nc.vector.reciprocal(rc0[:, u, :], rs0[:, u, :]))
                    dve.wait_ge(S("o_ps"), i * 2 + u + 1)
                    ch(nc.vector.scalar_tensor_tensor(upd[:, u, :], pb[u][0:T, 0:D], rc0[:, u, :], bv0[:],
                                                      ALU.mult, ALU.add))
                    nc.vector.tensor_tensor(xb(i, u), xb(i, u), upd[:, u, :], ALU.add).then_inc(S("x_upd"), 1)
                dve.wait_ge(S("x_upd"), i * 2 + 2)
                norm(0, i, 1)
                logits(0, i)
            ch.leave(per, 4, start)
            dve.wait_ge(S("la_ready"), B)

            def v3(t):
                return t[:]

            def over_e(t):
                return t[:].unsqueeze(2).to_broadcast([T, B, E])

            def over_b(t):
                return t.unsqueeze(1).to_broadcast([T, B, E])

            def routing(lay):
                a_in, a_out = S("act_in"), S("act_out")
                if lay == 0:
                    ch(nc.vector.tensor_reduce(rr[:], la[:], AX.X, ALU.max))
                    nc.vector.tensor_tensor(la[:], la[:], over_e(rr), ALU.subtract).then_inc(a_in, 1)
                    dve.wait_ge(a_out, 1)
                    nc.vector.tensor_reduce(rr[:], pi[:], AX.X, ALU.add).then_inc(a_in, 1)
                    dve.wait_ge(a_out, 2)
                    ch(nc.vector.tensor_tensor(la[:], la[:], over_e(rl), ALU.subtract))
                    nc.vector.tensor_reduce(cc[:], la[:].rearrange("p b e -> p e b"), AX.X, ALU.max
                                            ).then_inc(S("cmax_part"), 1)
                    dve.wait_ge(S("cmaxT"), 1)
                    ch(nc.vector.tensor_reduce(cm[:], pb[0][0:E, 0:T], AX.X, ALU.max))
                    nc.vector.tensor_scalar(cdiag[:], ident[0:E, 0:E], cm[:], None, ALU.mult
                                            ).then_inc(S("cdiag_ready"), 1)
                    dve.wait_ge(S("cmax_all"), 1)
                    ch(nc.vector.tensor_copy(cl[:], pb[1][0:T, 0:E]))
                    nc.vector.tensor_tensor(la[:], la[:], over_b(cl[:]), ALU.subtract).then_inc(a_in, 1)
                    dve.wait_ge(a_out, 3)
                    nc.vector.tensor_reduce(cl[:], pi[:].rearrange("p b e -> p e b"), AX.X, ALU.add
                                            ).then_inc(S("colpart"), 1)
                    dve.wait_ge(S("colsum"), 1)
                    nc.vector.tensor_copy(cl[:], pb[0][0:T, 0:E]).then_inc(a_in, 1)
                    dve.wait_ge(a_out, 4)
                    nc.vector.tensor_tensor(la[:], la[:], over_b(cc[:]), ALU.subtract).then_inc(a_in, 1)
                    dve.wait_ge(a_out, 5)
                    def sink_turn(n):
                        ch(nc.vector.tensor_tensor(tmp[:], pi[:], over_b(cc[:]), ALU.mult))
                        ch(nc.vector.tensor_reduce(rl[:], tmp[:], AX.X, ALU.add))
                        ch(nc.vector.reciprocal(rr[:], rl[:]))
                        ch(nc.vector.tensor_tensor(tmp[:], pi[:], over_e(rr), ALU.mult))
                        nc.vector.tensor_reduce(cl[:], tmp[:].rearrange("p b e -> p e b"), AX.X, ALU.add
                                                ).then_inc(S("colpart"), 1)
                        dve.wait_ge(S("colsum"), n)
                        ch(nc.vector.reciprocal(cc[:], pb[0][0:T, 0:E]))

                    ch(nc.vector.memset(cc[:], 1.0))
                    sink_turn(2)
                    start, per = ch.now, 5 * SINK_TURNS + 2
                    with dve.Fori(0, SINK_SEGS) as j:
                        ch.enter(j, per, start)
                        for k in range(SINK_TURNS):
                            sink_turn(j * SINK_TURNS + (3 + k))
                        nc.vector.tensor_copy(rl[:], rr[:]).then_inc(a_in, 1)
                        dve.wait_ge(a_out, j * 3 + 7)
                        ch(nc.vector.tensor_tensor(la[:], la[:], over_e(rl), ALU.add))
                        nc.vector.tensor_tensor(la[:], la[:], over_b(tmp[:, 0, :]), ALU.add).then_inc(a_in, 1)
                        dve.wait_ge(a_out, j * 3 + 8)
                        ch(nc.vector.memset(cc[:], 1.0))
                    ch.leave(per, SINK_SEGS, start)
                else:
                    ch(nc.vector.tensor_reduce(rr[:], la[:], AX.X, ALU.max))
                    nc.vector.tensor_tensor(la[:], la[:], over_e(rr), ALU.subtract).then_inc(a_in, 1)
                    dve.wait_ge(a_out, 5 + 9 + 1)
                    ch(nc.vector.tensor_reduce(rr[:], pi[:], AX.X, ALU.add))
                    ch(nc.vector.reciprocal(rl[:], rr[:]))
                    ch(nc.vector.tensor_tensor(pi[:], pi[:], over_e(rl), ALU.mult))
                if lay == 0:
                    ch(nc.vector.scalar_tensor_tensor(pi[:], pi[:], 2.0 ** -126, pi[:], ALU.is_ge, ALU.mult))
                    ch(nc.vector.tensor_copy(wtop[:, 0, :, :], pi[:, :, 0:TOPK].rearrange("p b k -> p k b")))
                for k, hot in enumerate((m1h, m2h)):
                    top = rr[:] if lay == 0 else wtop[:, 1, k, :]
                    ch(nc.vector.tensor_reduce(top, pi[:], AX.X, ALU.max))
                    ch(nc.vector.tensor_tensor(tmp[:], pi[:], top.unsqueeze(2).to_broadcast([T, B, E]),
                                               ALU.is_equal))
                    ch(nc.vector.tensor_tensor(tmp[:], tmp[:], iota_e[:], ALU.mult))
                    ch(nc.vector.tensor_reduce(rl[:], tmp[:], AX.X, ALU.min))
                    ch(nc.vector.tensor_tensor(hot[:], iota_e[:], over_e(rl), ALU.is_equal))
                    if k == 0:
                        ch(nc.vector.scalar_tensor_tensor(pi[:], hot[:], -2.0, pi[:], ALU.mult, ALU.add))
                nc.vector.tensor_tensor(msk[:], m1h[:], m2h[:], ALU.add).then_inc(S("mask_ready"), 1)
                dve.wait_ge(S("rank_ps"), lay + 1)
                ch(nc.vector.tensor_copy(cl[:], pb[3][0:T, 0:E]))
                ch(nc.vector.tensor_tensor(kcmp[:], cl[:].unsqueeze(2).to_broadcast([T, E, CPE]), kgrid[:],
                                           ALU.is_gt))
                ch(nc.vector.tensor_reduce(nt[:], kcmp[:], AX.X, ALU.add))
                ch(nc.vector.tensor_tensor(tcmp[:], nt[:].unsqueeze(1).to_broadcast([T, E, E]), tri[:], ALU.mult))
                ch(nc.vector.tensor_reduce(tb[:], tcmp[:], AX.X, ALU.add))
                ch(nc.vector.tensor_tensor(tend[:], tb[:], nt[:], ALU.add))
                ch(nc.vector.tensor_tensor(scmp[:], tend[:].unsqueeze(1).to_broadcast([T, TILES, E]), sgrid[:],
                                           ALU.is_le))
                ch(nc.vector.tensor_reduce(tef[:], scmp[:], AX.X, ALU.add))
                ch(nc.vector.tensor_scalar(tef[:], tef[:], E - 1.0, float(EW), ALU.min, ALU.mult))
                nc.vector.tensor_copy(te[:], tef[:]).then_inc(S("te_ready"), 1)
                ch(nc.vector.tensor_scalar(tb[:], tb[:], float(SLOTS), None, ALU.mult))
                ch(nc.vector.tensor_tensor(slotv[:], pb[2][0:T, 0:B * E].rearrange("p (b e) -> p b e", e=E),
                                           over_b(tb[:]), ALU.add))
                for k, hot in enumerate((m1h, m2h)):
                    ch(nc.vector.tensor_tensor(tmp[:], slotv[:], hot[:], ALU.mult))
                    ch(nc.vector.tensor_reduce(sf[:], tmp[:], AX.X, ALU.add))
                    ins = nc.vector.tensor_copy(slot[:, k, :], sf[:])
                    if k == 0:
                        ch(ins)
                ins.then_inc(S("slots_ready"), 1)

            def experts(lay):
                for s in range(TILES):
                    g0 = lay * TILES + s
                    dve.wait_ge(S("xT_hi"), g0 + 1)
                    nc.vector.tensor_tensor(xTlo[:, s, :, :].rearrange("p k n -> p (k n)"),
                                            pb[s % 8][:, 0:KD * 128],
                                            xThi[:, s, :, :].rearrange("p k n -> p (k n)"), ALU.subtract
                                            ).then_inc(S("xT_sb"), 1)
                for p in range(PHASES[lay]):
                    ph = sum(PHASES[:lay]) + p
                    G = ph * TILES

                    def product(s, par, first):
                        dve.wait_ge(S("silu_ready"), s + (G + 1))
                        if first is None:
                            dve.wait_ge(S("hT_ps"), s + (G - 1))
                        elif G:
                            dve.wait_ge(S("hT_ps"), G)
                        nc.vector.scalar_tensor_tensor(hh[:, par, :], pb[par][:, FC:2 * FC], 1.0 / WSCALE,
                                                       sg[:, par, :], ALU.mult, ALU.mult
                                                       ).then_inc(S("h_ready"), 1)

                    def hT_low(s, par):
                        dve.wait_ge(S("hT_hi"), s + (G + 1))
                        nc.vector.tensor_tensor(hTlo[:, par, :, :].rearrange("p k n -> p (k n)"),
                                                pb[2 + par][:, 0:FC],
                                                hThi[:, par, :, :].rearrange("p k n -> p (k n)"), ALU.subtract
                                                ).then_inc(S("hT_lo"), 1)

                    def add(s, par):
                        dve.wait_ge(S("y_ps"), s + (G + 1))
                        to = yacc[:, s, :] if isinstance(s, int) else yacc[:, ds(s.at, 1), :].rearrange("p o d -> p (o d)")
                        if p == 0:
                            ins = nc.vector.tensor_scalar(to, pb[4 + par][:, 0:D], 1.0 / WSCALE, None, ALU.mult)
                        else:
                            ins = nc.vector.scalar_tensor_tensor(to, pb[4 + par][:, 0:D], 1.0 / WSCALE, to,
                                                                 ALU.mult, ALU.add)
                        ins.then_inc(S("y_acc"), 1)

                    def split(i, v, half):
                        w_lo((ph + 1) % 2, i * 2 + v, i * 2 + (v + (ph + 1) * E), v, i + (ph + 1) * (E // 2), half)

                    pipeline(product, hT_low, add, split if ph + 1 < NPH else None, dve)

            def combine(lay, b):
                dve.wait_ge(S(f"gathered{b}"), 16 * TOPK * (lay + 1))
                ch(nc.vector.scalar_tensor_tensor(x[:, b, :], yg[:, 0, b, :], wtop[:, lay, 0, b:b + 1],
                                                  x[:, b, :], ALU.mult, ALU.add))
                ins = nc.vector.scalar_tensor_tensor(x[:, b, :], yg[:, 1, b, :], wtop[:, lay, 1, b:b + 1],
                                                     x[:, b, :], ALU.mult, ALU.add)
                if lay == 0:
                    ch(ins)
                else:
                    ins.then_inc(S("x_done"), 1)

            routing(0)
            experts(0)
            combine(0, 0)
            def x_of(b):
                if isinstance(b, Batch):
                    return x[:, ds(b.i * 2 + b.k, 1), :].rearrange("p o d -> p (o d)")
                return x[:, b, :]

            def spread(b, u, part):
                if part == 0:
                    carry(2 * u)
                    nc.vector.bn_stats(stats[:, u, :], x_of(b)).then_inc(S("stats_ready"), 1)
                elif part == 1:
                    dve.wait_ge(S("stats_ready"), norm_count(b, u) + (-2 * B))
                    carry(2 * u + 1)
                    nc.vector.bn_aggr(mv[:, u, :], stats[:, u, :]).then_inc(S("mean_ready"), 1)
                else:
                    dve.wait_ge(S("mean_ready"), norm_count(b, u) + (-2 * B))
                    nc.vector.tensor_scalar(vare[:, u, :], mv[:, u, 1:2], EPS, None, ALU.add
                                            ).then_inc(S("var_ready"), 1)

            def normal(b, second):
                dve.wait_ge(S("rstd_ready"), norm_count(b, second))
                nc.vector.tensor_scalar(xnb[:, second, :], x_of(b), mv[:, second, 0:1], rstd[:, second, :],
                                        ALU.subtract, ALU.mult).then_inc(S("ln_ready"), 1)

            def unit(b, kind, name, of):
                n = unit_count(b, kind, name)
                u, w = parity(of), pb[unit_bank(kind, name)]
                if name in ("xnT1", "xnT2") or name[0] == "k":
                    return
                if name == "q":
                    dve.wait_ge(S("unit_ps"), n + 1)
                    nc.vector.scalar_tensor_tensor(
                        qf[:], w[:, 0:HP * T].rearrange("p (m t) -> p m t", t=T), DK ** -0.5,
                        bq1s[:].unsqueeze(2).to_broadcast([128, HP, T]), ALU.mult, ALU.add
                        ).then_inc(S("q_in"), 1)
                elif name in ("v0", "v1"):
                    dve.wait_ge(S("v_hi"), count(of, 2, 1 + int(name == "v1")))
                    for j in ((0, 1), (2,))[int(name == "v1")]:
                        last = nc.vector.tensor_tensor(
                            v1h[:, u * NKC + j, :, 1, :], w[0:KC, (j % 2) * D:(j % 2) * D + D].rearrange(
                                "p (h d) -> p h d", d=DK), v1h[:, u * NKC + j, :, 0, :], ALU.subtract)
                    last.then_inc(S("v_sb"), 1)
                elif name == "rcT":
                    dve.wait_ge(S("av_ps"), count(of, HEADS, HEADS))
                    dve.wait_ge(S("rcT_sb"), count(of, 1, 1))
                    nc.vector.tensor_tensor(catT[:], pb[5][:, 0:HP * T], rcT[:], ALU.mult
                                            ).then_inc(S("cat_ready"), 1)
                elif name == "wo":
                    dve.wait_ge(S("unit_ps"), n + 1)
                    nc.vector.tensor_tensor(upd[:, 0, :], w[0:T, 0:D], bo1[:], ALU.add).then_inc(S("wo_used"), 1)
                    dve.wait_ge(S("wo_used"), count(of, 1, 1))
                    ch(nc.vector.tensor_tensor(x_of(of), x_of(of), upd[:, 0, :], ALU.add))
                else:
                    dve.wait_ge(S("unit_ps"), n + 1)
                    to = la[:, ds(of.i * 2 + of.k, 1), :].rearrange("p o e -> p (o e)") \
                        if isinstance(of, Batch) else la[:, of, :]
                    nc.vector.tensor_copy(to, w[0:T, 0:E]).then_inc(S("la_ready"), 1)

            def maximum(b, h):
                dve.wait_ge(S("ss_ps"), count(b, HEADS, h + 1))
                nc.vector.tensor_reduce(nb1[:, h:h + 1], pb[slot3(h)][0:T, 0:KEYS], AX.X, ALU.max,
                                        negate=True).then_inc(S("nb1_ready"), 1)

            def eT_low(b, h):
                dve.wait_ge(S("eT_hi"), count(b, HEADS, h + 1))
                nc.vector.tensor_tensor(eTlo[:, slot3(h), :], pb[3 + h % 2][0:KC, 0:NKC * T],
                                        eThi[:, slot3(h), :], ALU.subtract).then_inc(S("eT_lo"), 1)

            def over_sums(b):
                dve.wait_ge(S("e_ready"), count(b, HEADS, HEADS))
                nc.vector.reciprocal(rc1[:], rs1[:, parity(b), :]).then_inc(S("rc_ready"), 1)

            def heads(b, kind, first=False, final=False):
                for h in range(HEADS):
                    name = kind.get(h - 1)
                    of = b + 1 if name in NEXT.values() else b + -1
                    if name in ("q", "wo", "logits"):
                        unit(b, kind, name, of)
                    if h + 2 < HEADS:
                        maximum(b, h + 2)
                    elif not final:
                        maximum(b + 1, h + 2 - HEADS)
                    if name in ("v0", "v1", "rcT"):
                        unit(b, kind, name, of)
                    if h in (0, 1, 2) and not final:
                        spread(b + 1, 0, h)
                    if h == 4 and not final:
                        normal(b + 1, 0)
                    if h in (5, 6, 7) and not first:
                        spread(b + -1, 1, h - 5)
                    if h == 10 and not first:
                        normal(b + -1, 1)
                    if first and 2 <= h < B:
                        combine(0, h)
                    if h == HEADS - 1:
                        over_sums(b)
                    eT_low(b, h)

            for part in range(3):
                spread(0, 0, part)
            normal(0, 0)
            for name in NEXT.values():
                unit(-1, NEXT, name, 0)
            combine(0, 1)
            maximum(0, 0)
            maximum(0, 1)
            heads(0, NEXT, first=True)
            per = 2 * 1
            start = ch.now
            with dve.Fori(0, (B - 2) // 2) as i:
                ch.enter(i, per, start)
                heads(Batch(i, 1), BOTH)
                heads(Batch(i, 2), BOTH)
            ch.leave(per, (B - 2) // 2, start)
            heads(B - 1, TAIL, final=True)
            for name in TAIL.values():
                unit(B, TAIL, name, B - 1)
                if name == "wo":
                    for part in range(3):
                        spread(B - 1, 1, part)
                    normal(B - 1, 1)
            dve.wait_ge(S("la_ready"), 2 * B)
            routing(1)
            experts(1)
            for b in range(B):
                combine(1, b)


_SHAPES = {}


def kernel(**inputs):
    import numpy as np
    import concourse.bacc as bacc
    from concourse.bass_utils import run_bass_kernel_spmd as run

    f = {k: np.asarray(v) for k, v in inputs.items()}

    def chunks(w, k):
        return w.reshape(k, 128, -1).transpose(1, 0, 2)

    def pad_heads(w):
        r = w.reshape(w.shape[0], HEADS, DK)
        return np.concatenate([r, r], axis=2).reshape(w.shape[0], 2 * HEADS * DK)

    ctx = f["ctx_512"]
    arr = {
        "x": f["x"],
        "ctxT": ctx.transpose(2, 0, 1),
        "ctxN": ctx.reshape(B, NKC, KC, C).transpose(2, 0, 1, 3),
        "wq0T": chunks(f["L0_xattn_Wq"].T, KD),
        "wk0T": chunks(f["L0_xattn_Wk"].T, KD),
        "wv0": f["L0_xattn_Wv"],
        "bq0": f["L0_xattn_bq"].reshape(KD, 128).T,
        "bk0": f["L0_xattn_bk"].reshape(KD, 128).T,
        "bv0": np.broadcast_to(f["L0_xattn_bv"], (T, D)),
        "wq1": chunks(pad_heads(f["L1_xattn_Wq"]), KD),
        "wk1": pad_heads(f["L1_xattn_Wk"]),
        "wv1": f["L1_xattn_Wv"],
        "wo1": chunks(pad_heads(f["L1_xattn_Wo"].T).T, HP),
        "bq1": pad_heads(f["L1_xattn_bq"][None])[0].reshape(HP, 128).T,
        "bk1": pad_heads(f["L1_xattn_bk"][None])[0].reshape(HP, 128).T,
        "bv1": pad_heads(f["L1_xattn_bv"][None])[0].reshape(HP, 128).T,
        "bo1": np.broadcast_to(f["L1_xattn_bo"], (T, D)),
        "router": np.stack([chunks(f["L0_ffn_gate_W"].T, KD), chunks(f["L1_ffn_router_w"].T, KD)], axis=1),
    }
    w1, w2 = f["L1_ffn_w1"], f["L1_ffn_w2"]
    inter = w1.shape[1] // 2
    layers = ((f["L0_ffn_W_gate"], f["L0_ffn_W_up"], f["L0_ffn_W_down"]), (w1[:, :inter], w1[:, inter:], w2))
    stream = []
    for (gate, up, down), n in zip(layers, PHASES):
        for p in range(n):
            for e in range(E):
                g = chunks(gate[e, p * FC:(p + 1) * FC].T, KD)
                u = chunks(up[e, p * FC:(p + 1) * FC].T, KD)
                d = chunks(down[e][:, p * FC:(p + 1) * FC].T, FC // 128)
                gu = np.concatenate([g, u], axis=2).reshape(128, -1)
                stream.append(np.concatenate([gu, d.reshape(128, -1)], axis=1))
    arr["wst"] = np.stack(stream, axis=1)

    nc = bacc.Bacc("TRN2", target_bir_lowering=False, num_devices=1)
    arr["lowrow"] = ((np.arange(128) // DK) % 2).astype(np.float32).reshape(128, 1)
    arrays, aps = {}, {}
    for name, v in arr.items():
        v = np.ascontiguousarray(v)
        arrays[f"in_{name}"] = v
        aps[name] = nc.dram_tensor(f"in_{name}", v.shape, mybir.dt.from_np(v.dtype), kind="ExternalInput").ap()
    aps["out"] = nc.dram_tensor("out_x", (B, T, D), F32, kind="ExternalOutput").ap()
    build(nc, aps)
    r = run(nc, [arrays], core_ids=[0])
    return r.results[0]["out_x"]
```

```python
from contextlib import ExitStack

import concourse.bass as bass
from concourse import mybir

ALU = mybir.AluOpType
ACT = mybir.ActivationFunctionType
F32 = mybir.dt.float32
F16 = mybir.dt.float16
I32 = mybir.dt.int32
U32 = mybir.dt.uint32
AX = mybir.AxisListType
ds = bass.ds

B, T, D = 8, 112, 256
KEYS, C = 375, 128
KC, NKC = 125, 3
KD = D // 128
E = 8
TOPK = 2
HEADS, DK = 16, 16
HP = 4
NTOK = B * T
SLOTS = 128
TILES = (NTOK * TOPK + E * (SLOTS - 1)) // SLOTS
CPE = NTOK // SLOTS
FC = 256
PHASES = (1024 // FC, 512 // FC)
EW = KD * 2 * FC + (FC // 128) * D
WSCALE = 256.0
EPS = 1e-5
ROW_PARTS = 3
NB = 4
SINK_ITERS, SINK_EPS = 20, 0.05
SINK_SEGS = 3
SINK_TURNS = (SINK_ITERS - 2) // SINK_SEGS
assert SINK_SEGS * SINK_TURNS + 2 == SINK_ITERS


class Chain:

    def __init__(self, eng, sem):
        self.eng, self.sem, self.base, self.n = eng, sem, 0, 0

    def __call__(self, ins):
        self.n += 1
        ins.then_inc(self.sem, 1)
        self.eng.wait_ge(self.sem, self.base + self.n)

    def enter(self, i, per, start):
        self.base, self.n = start + i * per, 0

    def leave(self, per, trips, start):
        assert self.n == per, (self.n, per)
        self.base, self.n = start + trips * per, 0

    @property
    def now(self):
        return self.base + self.n


class Step:

    def __init__(self, i, k):
        self.i, self.k = i, k

    def __add__(self, n):
        return self.i * 4 + (self.k + n)

    @property
    def at(self):
        return self + 0


class Batch:

    def __init__(self, i, k):
        self.i, self.k = i, k

    def __add__(self, n):
        return Batch(self.i, self.k + n)


def count(b, per, n):
    if isinstance(b, Batch):
        assert b.k * per + n >= 0
        return b.i * (2 * per) + (b.k * per + n)
    return b * per + n


def parity(b):
    return (b.k if isinstance(b, Batch) else b) % 2


TAIL = {0: "rcT", 3: "wo", 12: "xnT2", 14: "logits"}
NEXT = {1: "v0", 5: "xnT1", 6: "v1", 7: "q", 8: "k0", 9: "k1", 10: "k2", 11: "k3"}
BOTH = {**TAIL, **NEXT}


def unit_count(b, kind, name):
    order = [kind[h] for h in sorted(kind)]
    if isinstance(b, Batch) or b in range(1, B):
        first = count(b, len(BOTH), 2 * len(NEXT) - len(BOTH))
    else:
        first = {-1: 0, 0: len(NEXT), B: B * len(BOTH) - len(TAIL)}[b]
    return first + order.index(name)


def norm_count(b, second):
    if second:
        return count(b, 2, 2 * B + 4) if isinstance(b, Batch) or b < B - 2 else 2 * B + b + B + 1
    return count(b, 2, 2 * B - 1) if isinstance(b, Batch) or b > 1 else 2 * B + b + 1


def unit_bank(kind, name):
    return 6 + [kind[h] for h in sorted(kind)].index(name) % 2


def slot3(h):
    return 1 if h == HEADS - 1 else h % 3


def before3(h):
    return {0: -4, 1: -1, 2: -2, HEADS - 1: HEADS - 3}.get(h, h - 3)


def build(nc, a):
    ctx = ExitStack()
    with ctx:
        def sb(name, shape, dt=F32):
            return ctx.enter_context(nc.sbuf_tensor(name, shape, dt))

        sems = {}

        def S(name):
            if name not in sems:
                sems[name] = ctx.enter_context(nc.semaphore(name))
            return sems[name]

        pb = [ctx.enter_context(nc.psum_tensor(f"bank{i}", [128, 512], F32)) for i in range(8)]

        xg_dram = nc.dram_tensor("expert_rows", [TILES * SLOTS, D], F32, kind="Internal").ap()
        ys_dram = nc.dram_tensor("expert_results", [TILES * SLOTS, D], F32, kind="Internal").ap()

        x = sb("x", [T, B, D])
        xn = sb("xn", [T, B, D])
        whi = sb("whi", [128, 2, E * EW], F16)
        wlo = sb("wlo", [128, 2, E * EW], F16)
        stage = sb("stage", [128, 2, EW])
        ident = sb("ident", [128, 128])
        ones = sb("ones", [128, 128])
        lower16 = sb("lower16", [T, T], F16)
        ones16 = sb("ones16", [T, T], F16)
        lower = sb("lower", [T, T])
        ctT = sb("ctT", [128, 2, KEYS])
        bq0 = sb("bq0", [128, KD])
        bk0 = sb("bk0", [128, KD])
        bv0 = sb("bv0", [T, D])
        fold = sb("fold", [128, 2 * C + 4])
        wq1 = sb("wq1", [128, KD, HP * 128])
        wk1 = sb("wk1", [C, HP * 128])
        wv1 = sb("wv1", [C, D])
        wo1 = sb("wo1", [128, HP, D])
        bq1 = sb("bq1", [128, HP])
        bq1s = sb("bq1s", [128, HP])
        bk1 = sb("bk1", [128, HP])
        lowrow = sb("lowrow", [128, 1])
        bv1 = sb("bv1", [128, HP])
        bo1 = sb("bo1", [T, D])
        router = sb("router", [128, 2, KD, E])
        xnb = sb("xnb", [T, NB, D])
        stats = sb("stats", [T, NB, 6])
        mv = sb("mv", [T, NB, 2])
        vare = sb("vare", [T, NB, 1])
        rstd = sb("rstd", [T, NB, 1])
        carrier = sb("carrier", [T, 2 * NB, 1])
        mhalf = sb("mhalf", [T, 1])
        xnT = sb("xnT", [128, NB, KD, T])
        qbk = sb("qbk", [T, NB, 1])
        mx0 = sb("mx0", [T, NB, 1])
        nb0 = sb("nb0", [T, NB, 1])
        rs0 = sb("rs0", [T, NB, 1])
        rc0 = sb("rc0", [T, NB, 1])
        upd = sb("upd", [T, 1, D])
        la = sb("la", [T, B, E])
        pi = sb("pi", [T, B, E])
        tmp = sb("tmp", [T, B, E])
        msk = sb("msk", [T, B, E], F16)
        m1h = sb("m1h", [T, B, E], F16)
        m2h = sb("m2h", [T, B, E], F16)
        slotv = sb("slotv", [T, B, E])
        rr = sb("rr", [T, B])
        rl = sb("rl", [T, B])
        cc = sb("cc", [T, E])
        cl = sb("cl", [T, E])
        cm = sb("cm", [E, 1])
        cdiag = sb("cdiag", [E, E])
        wtop = sb("wtop", [T, 2, TOPK, B])
        sf = sb("sf", [T, B])
        slot = sb("slot", [T, TOPK, B], U32)
        iota_e = sb("iota_e", [T, B, E])
        kgrid = sb("kgrid", [T, E, CPE])
        kcmp = sb("kcmp", [T, E, CPE])
        nt = sb("nt", [T, E])
        tri = sb("tri", [T, E, E])
        tcmp = sb("tcmp", [T, E, E])
        tb = sb("tb", [T, E])
        tend = sb("tend", [T, E])
        sgrid = sb("sgrid", [T, TILES, E])
        scmp = sb("scmp", [T, TILES, E])
        tef = sb("tef", [T, TILES])
        te = sb("te", [T, TILES], I32)
        sg = sb("sg", [128, 2, FC])
        hh = sb("hh", [128, 2, FC])
        hThi = sb("hThi", [128, 2, FC // 128, 128], F16)
        hTlo = sb("hTlo", [128, 2, FC // 128, 128], F16)

        REGION = 10752
        region = sb("region", [128, REGION])
        XT = TILES * KD * 128
        xThi = region[:, 0:XT // 2].bitcast(F16).rearrange("p (s k n) -> p s k n", k=KD, n=128)
        xTlo = region[:, XT // 2:XT].bitcast(F16).rearrange("p (s k n) -> p s k n", k=KD, n=128)
        yacc = region[:, XT:XT + TILES * D].rearrange("p (s d) -> p s d", d=D)
        yg = whi[0:T, 1, 0:2 * TOPK * B * D].bitcast(F32).rearrange("p (k b d) -> p k b d", k=TOPK, b=B)
        at = [0]

        def carve(p, *dims):
            n = 1
            for v in dims:
                n *= v
            v = region[0:p, at[0]:at[0] + n]
            at[0] += n
            assert at[0] <= REGION, at
            if len(dims) == 1:
                return v
            names = "abcd"[:len(dims)]
            return v.rearrange(f"p ({' '.join(names)}) -> p {' '.join(names)}",
                               **{k: d for k, d in zip(names[1:], dims[1:])})

        def carve16(p, *dims):
            n = 1
            for v in dims:
                n *= v
            v = carve(p, (n + 1) // 2).bitcast(F16)[:, 0:n]
            names = "abcd"[:len(dims)]
            return v.rearrange(f"p ({' '.join(names)}) -> p {' '.join(names)}",
                               **{k: d for k, d in zip(names[1:], dims[1:])})

        NP = 4
        probs = carve(T, NP, KEYS)
        both = at[0]
        probsT = carve(KC, NB, NKC, T)
        ctN = carve(KC, NB, NKC, C)
        ct0 = carve(C, NB, KEYS)
        aT = carve(128, NB, T)
        zT = carve(C, NB, T)
        upd0 = carve(T, NB, D)
        wq0T = carve(128, KD, D)
        wk0T = carve(128, KD, C)
        wv0 = carve(C, D)
        at[0] = both
        kst = carve16(128, 2 * HP, KEYS)
        kf = carve(128, HP, KEYS)
        kmh = carve16(128, KEYS)
        qf = carve(128, HP, T)
        qhi = carve16(128, 2 * HP, T)
        qlo = carve16(128, 2 * HP, T)
        v1h = carve16(KC, 2 * NKC, HEADS, 2, DK)
        eThi = carve16(KC, 3, NKC * T)
        eTlo = carve16(KC, 3, NKC * T)
        rce = carve(T, HEADS * 2 * DK)
        rcT = carve(128, HP * T)
        catT = carve(128, HP * T)
        nb1 = carve(T, HEADS)
        rs1 = carve(T, 2, HEADS)
        rc1 = carve(T, HEADS)

        block = ctx.enter_context(nc.Block())
        NPH = sum(PHASES)

        def rows_in(eng, lay):
            eng.wait_ge(S("scattered"), 16 * TOPK * B * (lay + 1))
            n = TILES // ROW_PARTS
            for part in range(ROW_PARTS):
                eng.dma_start(yacc[:, part * n:(part + 1) * n, :],
                              xg_dram.rearrange("(s p) d -> p s d", p=SLOTS)[:, part * n:(part + 1) * n, :]
                              ).then_inc(S(f"rows_in{part}"), 16)

        def results(eng, lay):
            eng.wait_ge(S("y_acc"), TILES * sum(PHASES[:lay + 1]))
            eng.dma_start(ys_dram.rearrange("(s p) d -> p s d", p=SLOTS), yacc).then_inc(S("ys_out"), 16)

        @block.sync
        def _(sp):
            sp.dma_start(x[:], a["x"].rearrange("b t d -> t b d")).then_inc(S("x_in"), 16)
            first = ((wq0T, "wq0T"), (wk0T, "wk0T"), (bq0, "bq0"), (bk0, "bk0"), (wv0, "wv0"), (bv0, "bv0"),
                     (router, "router"))
            later = ((wq1, "wq1"), (wk1, "wk1"), (wv1, "wv1"), (wo1, "wo1"), (bq1, "bq1"), (bk1, "bk1"),
                     (bv1, "bv1"), (bo1, "bo1"), (lowrow, "lowrow"))
            for dst, src in first:
                sp.dma_start(dst[:], a[src]).then_inc(S("attn0_in"), 16)

            def ctx_in(i, u, wait):
                if wait is not None:
                    sp.wait_ge(S("k_sb"), wait * HP)
                sp.dma_start(ctT[:, u, :], a["ctxT"][:, ds(i * 2 + u, 1), :].rearrange("p o k -> p (o k)")
                             ).then_inc(S(f"ctx_in{u}"), 16)

            def ctx0_in(b):
                if b >= NB:
                    sp.wait_ge(S("z_ps"), b - NB + 1)
                sp.dma_start(ct0[:, b % NB, :], a["ctxT"][:, b, :]).then_inc(S(f"ctx0_in{b % NB}"), 16)
                sp.dma_start(ctN[:, b % NB, :, :], a["ctxN"][:, b, :, :]).then_inc(S(f"ctx0_in{b % NB}"), 16)

            def chunk_in(c, v, wait):
                if wait is not None:
                    sp.wait_ge(S("w_hi"), wait * 2)
                    sp.wait_ge(S("w_lo"), wait * 2)
                sp.dma_start(stage[:, v, :], a["wst"][:, ds(c, 1), :].rearrange("p o n -> p (o n)")
                             ).then_inc(S(f"w_in{v}"), 16)

            for b in range(NB):
                ctx0_in(b)
            for dst, src in later:
                sp.dma_start(dst[:], a[src]).then_inc(S("attn1_in"), 16)
            for c in range(E // 2):
                chunk_in(c, c % 2, c - 1 if c >= 2 else None)
            for b in range(NB, B):
                ctx0_in(b)
            for c in range(E // 2, E):
                chunk_in(c, c % 2, c - 1)
            for u in range(2):
                ctx_in(0, u, None)
            rows_in(sp, 0)
            with sp.Fori(E // 2, (PHASES[0] + 1) * E // 2) as i:
                for v in range(2):
                    chunk_in(i * 2 + v, v, i * 2 + v - 1)
            results(sp, 0)
            with sp.Fori(1, 4) as i:
                for u in range(2):
                    ctx_in(i, u, i * 2 - 1 + u)
            rows_in(sp, 1)
            with sp.Fori((PHASES[0] + 1) * E // 2, NPH * E // 2) as i:
                for v in range(2):
                    chunk_in(i * 2 + v, v, i * 2 + v - 1)
            results(sp, 1)
            for b in range(0, B, 2):
                sp.wait_ge(S("x_done"), b + 2)
                sp.dma_start(a["out"][b:b + 2].rearrange("b t d -> t b d"), x[:, b:b + 2, :]
                             ).then_inc(S("out_done"), 16)
            sp.wait_ge(S("out_done"), 16 * B // 2)

        @block.gpsimd
        def _(pool):
            g = Chain(pool, S("pool_step"))
            g(pool.memset(ident[:], 0.0))
            g(pool.affine_select(out=ident[:], in_=ident[:], compare_op=ALU.not_equal, fill=1.0, base=0,
                                 pattern=[[-1, 128]], channel_multiplier=1))
            pool.memset(xnb[:], 0.0).then_inc(S("xn_kept"), 1)
            pool.memset(mhalf[:], -0.5).then_inc(S("const"), 1)
            pool.memset(ones[:], 1.0).then_inc(S("const"), 1)
            g(pool.memset(lower[:], 1.0))
            pool.affine_select(out=lower[:], in_=lower[:], compare_op=ALU.is_gt, fill=0.0, base=0,
                               pattern=[[1, T]], channel_multiplier=-1).then_inc(S("const"), 1)
            pool.iota(iota_e[:], [[0, B], [1, E]], base=-E, channel_multiplier=0,
                      allow_small_or_imprecise_dtypes=True).then_inc(S("const"), 1)
            pool.iota(kgrid[:], [[0, E], [SLOTS, CPE]], base=0, channel_multiplier=0,
                      allow_small_or_imprecise_dtypes=True).then_inc(S("const"), 1)
            pool.iota(sgrid[:], [[1, TILES], [0, E]], base=0, channel_multiplier=0,
                      allow_small_or_imprecise_dtypes=True).then_inc(S("const"), 1)
            g(pool.memset(tri[:], 1.0))
            pool.affine_select(out=tri[:], in_=tri[:], compare_op=ALU.is_gt, fill=0.0, base=0,
                               pattern=[[1, E], [-1, E]], channel_multiplier=0).then_inc(S("const"), 1)
            zeros = whi[:, 1, 0:2 * TILES * D].bitcast(F32)
            g(pool.memset(zeros, 0.0))
            pool.dma_start(xg_dram.rearrange("(s p) d -> p s d", p=SLOTS),
                           zeros.rearrange("p (s d) -> p s d", d=D)).then_inc(S("zeroed"), 16)

            def root(n, u):
                pool.wait_ge(S("var_ready"), n)
                pool.tensor_tensor(rstd[:, u, :], vare[:, u, :], mhalf[:], ALU.pow
                                   ).then_inc(S("rstd_ready"), 1)

            def widen(n):
                pool.wait_ge(S("rc_ready"), n)
                pool.tensor_tensor(rce[:].rearrange("p (h d) -> p h d", h=HEADS),
                                   rc1[:].unsqueeze(2).to_broadcast([T, HEADS, 2 * DK]),
                                   ones[0:T, 0:2 * DK].unsqueeze(1).to_broadcast([T, HEADS, 2 * DK]),
                                   ALU.mult).then_inc(S("rc_wide"), 1)

            def gather(b):
                for k in range(TOPK):
                    pool.indirect_dma_start(
                        out=yg[:, k, b, :], out_offset=None, in_=ys_dram,
                        in_offset=bass.IndirectOffsetOnAxis(ap=slot[:, k, b:b + 1], axis=0),
                    ).then_inc(S(f"gathered{b}"), 16)

            def q_halves(b):
                u = parity(b)
                pool.wait_ge(S("q_in"), count(b, 1, 1))
                pool.tensor_tensor(qhi[:, u * HP:(u + 1) * HP, :], qf[:], ones[:, 0:1].unsqueeze(2).to_broadcast(
                    [128, HP, T]), ALU.mult).then_inc(S("q_hi"), 1)
                pool.wait_ge(S("q_hi"), count(b, 1, 1))
                pool.tensor_tensor(qlo[:, u * HP:(u + 1) * HP, :], qf[:], qhi[:, u * HP:(u + 1) * HP, :],
                                   ALU.subtract).then_inc(S("q_sb"), 1)

            def k_halves(b, m):
                pool.wait_ge(S("k_in"), count(b, HP, m + 1))
                if isinstance(b, Batch) or b or m:
                    pool.wait_ge(S("k_sb"), count(b, HP, m))
                pool.tensor_tensor(kmh[:], kf[:, m, :], lowrow[:].to_broadcast([128, KEYS]), ALU.mult
                                   ).then_inc(S("k_hi"), 1)
                pool.wait_ge(S("k_hi"), count(b, HP, m + 1))
                pool.tensor_tensor(kst[:, parity(b) * HP + m, :], kf[:, m, :], kmh[:], ALU.subtract
                                   ).then_inc(S("k_sb"), 1)

            for lay in range(2):
                if lay == 0:
                    with pool.Fori(0, B // NB) as i:
                        for half in range(2):
                            for u in range(NB):
                                root(i * (2 * NB) + (half * NB + u + 1), u)
                else:
                    gather(0)
                    gather(1)
                    root(2 * B + 1, 0)
                    for b in range(2, B):
                        gather(b)
                    q_halves(0)
                    for m in range(HP):
                        k_halves(0, m)
                    root(2 * B + 2, 0)
                    q_halves(1)
                    for m in range(HP):
                        k_halves(1, m)
                    with pool.Fori(0, (B - 2) // 2) as i:
                        for b in (Batch(i, 1), Batch(i, 2)):
                            widen(count(b, 1, 0))
                            root(norm_count(b + 1, 0), 0)
                            root(norm_count(b + -1, 1), 1)
                            q_halves(b + 1)
                            for m in range(HP):
                                k_halves(b + 1, m)
                    for b in (B - 2, B - 1):
                        widen(b + 1)
                        root(norm_count(b, 1), 1)
                pool.wait_ge(S("slots_ready"), lay + 1)
                pool.wait_ge(S("zeroed"), 16)
                pool.wait_ge(S("xn_kept"), B * (lay + 1) + 1)
                for k in range(TOPK):
                    for b in range(B):
                        pool.indirect_dma_start(
                            out=xg_dram, out_offset=bass.IndirectOffsetOnAxis(ap=slot[:, k, b:b + 1], axis=0),
                            in_=xn[:, b, :], in_offset=None).then_inc(S("scattered"), 16)
                pool.wait_ge(S("ys_out"), 16 * (lay + 1))
                if lay == 1:
                    for b in range(B):
                        gather(b)

        def pipeline(A, Bf, Cf, extra=None, eng=None):
            def step(s, par):
                A(s, par, None)
                Bf(Step(s.i, s.k - 1) if isinstance(s, Step) else s - 1, 1 - par)
                Cf(Step(s.i, s.k - 2) if isinstance(s, Step) else s - 2, par)

            A(0, 0, 0)
            A(1, 1, 1)
            Bf(0, 0)
            for s in (2, 3):
                step(s, s % 2)
            with eng.Fori(0, 4) as i:
                for q in range(4):
                    step(Step(i, 4 + q), q % 2)
                    if extra is not None:
                        extra(i, q // 2, q % 2)
            step(TILES - 1, 0)
            last = TILES - 1
            Bf(last, last % 2)
            Cf(last - 1, (last - 1) % 2)
            Cf(last, last % 2)

        @block.tensor
        def _(pe):
            pe.wait_ge(S("attn0_in"), 16 * 7)
            pe.wait_ge(S("const"), 7)
            pe.wait_ge(S("pool_step"), 4)
            f = pb[7]
            for k in range(KD):
                for e in range(KD):
                    pe.matmul(f[:, k * C:(k + 1) * C], wq0T[:, e, k * 128:(k + 1) * 128], wk0T[:, e, :],
                              start=(e == 0), stop=(e == KD - 1))
            for e in range(KD):
                pe.matmul(f[:, 2 * C:2 * C + 1], wk0T[:, e, :], bq0[:, e:e + 1], start=(e == 0), stop=(e == 1))
            for k in range(KD):
                for e in range(KD):
                    pe.matmul(f[:, 2 * C + 1 + k:2 * C + 2 + k], wq0T[:, e, k * 128:(k + 1) * 128],
                              bk0[:, e:e + 1], start=(e == 0), stop=(e == 1))
            for e in range(KD):
                last = pe.matmul(f[:, 2 * C + 3:2 * C + 4], bq0[:, e:e + 1].to_broadcast([128, 128]),
                                 bk0[:, e:e + 1], start=(e == 0), stop=(e == 1))
            last.then_inc(S("fold_ps"), 1)
            pe.wait_ge(S("fold_sb"), 1)

            def turn(i, half):
                for u in range(NB):
                    n = i * (2 * NB) + (half * NB + u + 1)
                    pe.wait_ge(S("ln_ready"), n)
                    for k in range(KD):
                        last = pe.transpose(pb[u][:, k * T:(k + 1) * T], xnb[:, u, k * 128:(k + 1) * 128],
                                            ident[0:T, 0:T])
                    last.then_inc(S("xnT_ps"), 1)

            def route(i):
                for u in range(NB):
                    pe.wait_ge(S("xnT_sb"), i * (2 * NB) + (NB + u + 1))
                    for k in range(KD):
                        last = pe.matmul(pb[u][0:T, 256:256 + E], xnT[:, u, k, :], router[:, 0, k, :],
                                         start=(k == 0), stop=(k == 1))
                    last.then_inc(S("logit_ps"), 1)

            with pe.Fori(0, B // NB) as i:
                turn(i, 0)
                for u in range(NB):
                    n = i * NB + (u + 1)
                    pe.wait_ge(S("xnT_sb"), i * (2 * NB) + (u + 1))
                    for k in range(KD):
                        pe.matmul(pb[4 + u][:, 0:T], fold[:, k * C:(k + 1) * C], xnT[:, u, k, :],
                                  start=(k == 0), stop=(k == 1))
                    for k in range(KD):
                        last = pe.matmul(pb[u][0:T, 400:401], xnT[:, u, k, :],
                                         fold[:, 2 * C + 1 + k:2 * C + 2 + k], start=(k == 0), stop=(k == 1))
                    last.then_inc(S("a_ps"), 1)
                for u in range(NB):
                    n = i * NB + (u + 1)
                    pe.wait_ge(S("a_sb"), n)
                    pe.wait_ge(S("qbk_ready"), n)
                    pe.wait_ge(S(f"ctx0_in{u}"), i * 32 + 32)
                    pe.matmul(pb[u][0:T, 0:KEYS], aT[:, u, :], ct0[:, u, :], start=True, stop=True
                              ).then_inc(S("s_ps"), 1)
                for u in range(NB):
                    n = i * NB + (u + 1)
                    pe.wait_ge(S("p_ready"), n)
                    for j in range(NKC):
                        last = pe.transpose(pb[4 + u][0:KC, j * T:(j + 1) * T],
                                            probs[:, u, j * KC:(j + 1) * KC], ident[0:T, 0:T])
                    last.then_inc(S("pT_ps"), 1)
                for u in range(NB):
                    n = i * NB + (u + 1)
                    pe.wait_ge(S("pT_sb"), n)
                    for j in range(NKC):
                        last = pe.matmul(pb[4 + u][:, 344:344 + T], ctN[:, u, j, :], probsT[:, u, j, :],
                                         start=(j == 0), stop=(j == NKC - 1))
                    last.then_inc(S("z_ps"), 1)
                for u in range(NB):
                    n = i * NB + (u + 1)
                    pe.wait_ge(S("z_sb"), n)
                    pe.matmul(pb[u][0:T, 0:D], zT[:, u, :], wv0[:], start=True, stop=True
                              ).then_inc(S("o_ps"), 1)
                turn(i, 1)
                route(i)

            def routing(lay):
                if lay == 0:
                    pe.wait_ge(S("cmax_part"), 1)
                    pe.transpose(pb[0][0:E, 0:T], cc[:], ident[0:T, 0:T]).then_inc(S("cmaxT"), 1)
                    pe.wait_ge(S("cdiag_ready"), 1)
                    pe.matmul(pb[1][0:T, 0:E], ones[0:E, 0:T], cdiag[:], start=True, stop=True
                              ).then_inc(S("cmax_all"), 1)

                    def colsum(n):
                        pe.wait_ge(S("colpart"), n)
                        pe.matmul(pb[0][0:T, 0:E], ones[0:T, 0:T], cl[:], start=True, stop=True
                                  ).then_inc(S("colsum"), 1)

                    colsum(1)
                    colsum(2)
                    with pe.Fori(0, SINK_SEGS) as j:
                        for k in range(SINK_TURNS):
                            colsum(j * SINK_TURNS + (3 + k))
                pe.wait_ge(S("mask_ready"), lay + 1)
                rank = pb[2][0:T, 0:B * E]
                pe.matmul(rank, lower16[:], m1h[:].rearrange("p b e -> p (b e)"), start=True, stop=False)
                for b in range(B - 1):
                    later = B - 1 - b
                    pe.matmul(pb[2][0:T, (b + 1) * E:B * E].rearrange("p (b e) -> p b e", e=E), ones16[:],
                              msk[:, b:b + 1, :].to_broadcast([T, later, E]), start=False, stop=False)
                pe.matmul(rank, lower16[:], m2h[:].rearrange("p b e -> p (b e)"), start=False, stop=True)
                for b in range(B):
                    last = pe.matmul(pb[3][0:T, 0:E], ones16[:], msk[:, b, :], start=(b == 0),
                                     stop=(b == B - 1))
                last.then_inc(S("rank_ps"), 1)

            def experts(lay):
                for s in range(TILES):
                    g0 = lay * TILES + s
                    pe.wait_ge(S(f"rows_in{s // (TILES // ROW_PARTS)}"), 16 * (lay + 1))
                    if s >= 8:
                        pe.wait_ge(S("xT_sb"), g0 - 7)
                    for k in range(KD):
                        last = pe.transpose(pb[s % 8][:, k * 128:(k + 1) * 128],
                                            yacc[:, s, k * 128:(k + 1) * 128], ident[:])
                    last.then_inc(S("rows_turned"), 1)
                pe.wait_ge(S("xT_sb"), TILES * (lay + 1))
                pe.wait_ge(S("te_ready"), lay + 1)
                regs = [pe.alloc_register(f"expert_at{lay}{q}") for q in range(4)]

                def expert_at(s):
                    return regs[(s.k if isinstance(s, Step) else s) % 4]

                for p in range(PHASES[lay]):
                    ph = sum(PHASES[:lay]) + p
                    G = ph * TILES
                    w = ph % 2
                    pe.wait_ge(S("w_lo"), (ph + 1) * E * 2)
                    pe.wait_ge(S("w_hi"), (ph + 1) * E * 2)

                    def gate_up(s, par, first):
                        pe.reg_load(expert_at(s), te[0:1, ds(s + 0, 1)])
                        off = pe.snap(expert_at(s), min_val=0, max_val=(E - 1) * EW)
                        if first is None:
                            pe.wait_ge(S("h_ready"), s + (G - 1))
                        elif G:
                            pe.wait_ge(S("h_ready"), G)
                        n = 0
                        for k in range(KD):
                            for st, mvg in ((xThi, whi), (xThi, wlo), (xTlo, whi)):
                                last = pe.matmul(pb[par][:, :], st_at(st, s, k), mvg[:, w, ds(off + k * 2 * FC, 2 * FC)],
                                                 start=(n == 0), stop=(n == 3 * KD - 1))
                                n += 1
                        last.then_inc(S("gu_ps"), 1)

                    def st_at(st, s, k):
                        if isinstance(s, int):
                            return st[:, s, k, :]
                        return st[:, ds(s.at, 1), k, :].rearrange("p o n -> p (o n)")

                    def turn_h(s, par):
                        pe.wait_ge(S("h_ready"), s + (G + 1))
                        if G or not isinstance(s, int) or s >= 2:
                            pe.wait_ge(S("hT_lo"), s + (G - 1))
                        for k in range(FC // 128):
                            last = pe.transpose(pb[2 + par][:, k * 128:(k + 1) * 128],
                                                hh[:, par, k * 128:(k + 1) * 128], ident[:])
                        last.then_inc(S("hT_ps"), 1)

                    def down(s, par):
                        off = pe.snap(expert_at(s), min_val=0, max_val=(E - 1) * EW)
                        pe.wait_ge(S("hT_lo"), s + (G + 1))
                        if G or not isinstance(s, int) or s >= 2:
                            pe.wait_ge(S("y_acc"), s + (G - 1))
                        n = 0
                        for k in range(FC // 128):
                            for st, mvg in ((hThi, whi), (hThi, wlo), (hTlo, whi)):
                                last = pe.matmul(pb[4 + par][:, 0:D], st[:, par, k, :],
                                                 mvg[:, w, ds(off + KD * 2 * FC + k * D, D)],
                                                 start=(n == 0), stop=(n == 3 * (FC // 128) - 1))
                                n += 1
                        last.then_inc(S("y_ps"), 1)

                    pipeline(gate_up, turn_h, down, eng=pe)

            pe.wait_ge(S("attn1_in"), 16 * 9)
            for m in range(HP):
                last = pe.matmul(pb[6][0:T, 0:D], bv1[:, m:m + 1].to_broadcast([128, T]), wo1[:, m, :],
                                 start=(m == 0), stop=(m == HP - 1))
            last.then_inc(S("bv_ps"), 1)
            routing(0)
            experts(0)

            def taken(name, of):
                if name in ("xnT1", "xnT2"):
                    pe.wait_ge(S("xnT_sb"), norm_count(of, int(name == "xnT2")))
                elif name == "q":
                    pe.wait_ge(S("q_in"), count(of, 1, 1))
                elif name in ("v0", "v1"):
                    pe.wait_ge(S("v_sb"), count(of, 2, 1 + int(name == "v1")))
                elif name[0] == "k":
                    pe.wait_ge(S("k_in"), count(of, HP, int(name[1]) + 1))
                elif name == "rcT":
                    pe.wait_ge(S("rcT_sb"), count(of, 1, 1))
                elif name == "wo":
                    pe.wait_ge(S("wo_used"), count(of, 1, 1))
                else:
                    pe.wait_ge(S("la_ready"), count(of, 1, B + 1))

            def unit(b, kind, name, of):
                w = pb[unit_bank(kind, name)]
                u = parity(of)
                order = [kind[h] for h in sorted(kind)]
                before = order.index(name) - 2
                if before >= 0:
                    taken(order[before], b + 1 if order[before] in NEXT.values() else b + -1)
                elif before == -2 and (isinstance(b, Batch) or b >= 0):
                    taken("k3", b if isinstance(b, Batch) or b < B else b + -1)
                    if isinstance(b, Batch) or b >= 2:
                        taken("logits", b + -2)
                if name in ("xnT1", "xnT2"):
                    half = int(name == "xnT2")
                    pe.wait_ge(S("ln_ready"), norm_count(of, half))
                    for k in range(KD):
                        last = pe.transpose(w[:, k * T:(k + 1) * T], xnb[:, half, k * 128:(k + 1) * 128],
                                            ident[0:T, 0:T])
                elif name == "q":
                    pe.wait_ge(S("xnT_sb"), norm_count(of, 0))
                    for m in range(HP):
                        for k in range(KD):
                            last = pe.matmul(w[:, m * T:(m + 1) * T], wq1[:, k, m * 128:(m + 1) * 128],
                                             xnT[:, 0, k, :], start=(k == 0), stop=(k == 1))
                elif name in ("v0", "v1"):
                    if name == "v0":
                        trips = of.i * 16 + (of.k // 2 + 1) * 16 if isinstance(of, Batch) else (of // 2 + 1) * 16
                        pe.wait_ge(S(f"ctx_in{u}"), trips)
                    for j in ((0, 1), (2,))[int(name == "v1")]:
                        last = pe.matmul(w[0:KC, (j % 2) * D:(j % 2) * D + D], ctT[:, u, j * KC:(j + 1) * KC],
                                         wv1[:], start=True, stop=True)
                elif name[0] == "k":
                    m = int(name[1])
                    last = pe.matmul(w[:, 0:KEYS], wk1[:, m * 128:(m + 1) * 128], ctT[:, u, :],
                                     start=True, stop=True)
                elif name == "rcT":
                    pe.wait_ge(S("rc_wide"), count(of, 1, 1))
                    for m in range(HP):
                        last = pe.transpose(w[:, m * T:(m + 1) * T], rce[:, m * 128:(m + 1) * 128],
                                            ident[0:T, 0:T])
                elif name == "wo":
                    pe.wait_ge(S("cat_ready"), count(of, 1, 1))
                    for m in range(HP):
                        last = pe.matmul(w[0:T, 0:D], catT[:, m * T:(m + 1) * T], wo1[:, m, :],
                                         start=(m == 0), stop=(m == HP - 1))
                else:
                    pe.wait_ge(S("xnT_sb"), norm_count(of, 1))
                    for k in range(KD):
                        last = pe.matmul(w[0:T, 0:E], xnT[:, 1, k, :], router[:, 1, k, :],
                                         start=(k == 0), stop=(k == 1))
                last.then_inc(S("unit_ps"), 1)

            def scores(b, h):
                r, m, u = 32 * (h % HP), h // HP, parity(b)
                if isinstance(b, Batch) or b > 0 or h >= 3:
                    pe.wait_ge(S("e_ready"), count(b, HEADS, before3(h) + 1))
                if h == 0:
                    pe.wait_ge(S("q_sb"), count(b, 1, 1))
                if h % HP == 0:
                    pe.wait_ge(S("k_sb"), count(b, HP, m + 1))
                to = pb[slot3(h)][0:T, 0:KEYS]
                pe.matmul(to, qhi[r:r + 2 * DK, u * HP + m, :], kst[r:r + 2 * DK, u * HP + m, :],
                          start=True, stop=False)
                pe.matmul(to, qlo[r:r + DK, u * HP + m, :], kst[r:r + DK, u * HP + m, :],
                          start=False, stop=True).then_inc(S("ss_ps"), 1)

            def turn_p(b, h):
                pe.wait_ge(S("e_ready"), count(b, HEADS, h + 1))
                if isinstance(b, Batch) or b > 0 or h >= 2:
                    pe.wait_ge(S("eT_lo"), count(b, HEADS, h - 1))
                for j in range(NKC):
                    last = pe.transpose(pb[3 + h % 2][0:KC, j * T:(j + 1) * T],
                                        probs[:, h % NP, j * KC:(j + 1) * KC], ident[0:T, 0:T])
                last.then_inc(S("eT_ps"), 1)

            def values(b, h):
                u = parity(b)
                pe.wait_ge(S("eT_lo"), count(b, HEADS, h + 1))
                if h == 0:
                    pe.wait_ge(S("v_sb"), count(b, 2, 2))
                    if isinstance(b, Batch) or b > 0:
                        pe.wait_ge(S("cat_ready"), count(b, 1, 0))
                r = 32 * (h % HP)
                to = pb[5][r:r + 2 * DK, (h // HP) * T:(h // HP + 1) * T]
                for n, half in enumerate((eThi, eTlo)):
                    for j in range(NKC):
                        last = pe.matmul(to, v1h[:, u * NKC + j, h, :, :].rearrange("p a d -> p (a d)"),
                                         half[:, slot3(h), j * T:(j + 1) * T],
                                         start=(n == 0 and j == 0), stop=(n == 1 and j == NKC - 1))
                last.then_inc(S("av_ps"), 1)

            def heads(b, kind, first=False, final=False):
                for h in range(HEADS):
                    if h + 2 < HEADS:
                        scores(b, h + 2)
                    elif not final:
                        scores(b + 1, h + 2 - HEADS)
                    turn_p(b, h)
                    if h >= 2:
                        values(b, h - 2)
                    elif not first:
                        values(b + -1, HEADS + h - 2)
                    if h in kind:
                        unit(b, kind, kind[h], b + 1 if kind[h] in NEXT.values() else b + -1)

            pe.wait_ge(S("ln_ready"), norm_count(0, 0))
            for name in NEXT.values():
                unit(-1, NEXT, name, 0)
            scores(0, 0)
            scores(0, 1)
            heads(0, NEXT, first=True)
            with pe.Fori(0, (B - 2) // 2) as i:
                heads(Batch(i, 1), BOTH)
                heads(Batch(i, 2), BOTH)
            heads(B - 1, TAIL, final=True)
            values(B - 1, HEADS - 2)
            values(B - 1, HEADS - 1)
            for name in TAIL.values():
                unit(B, TAIL, name, B - 1)
            routing(1)
            experts(1)

        @block.scalar
        def _(act):
            def xnT_out(i, half):
                for u in range(NB):
                    n = i * (2 * NB) + (half * NB + u + 1)
                    act.wait_ge(S("xnT_ps"), n)
                    nc.scalar.copy(xnT[:, u, :, :].rearrange("p k t -> p (k t)"), pb[u][:, 0:KD * T]
                                   ).then_inc(S("xnT_sb"), 1)
                    if half:
                        nc.scalar.copy(xn[:, ds(i * NB + u, 1), :].rearrange("p o d -> p (o d)"), xnb[:, u, :]
                                       ).then_inc(S("xn_kept"), 1)

            def w_hi(c, v, m, half):
                act.wait_ge(S(f"w_in{v}"), m * 16 + 16)
                nc.scalar.mul(whi[:, c[0], ds(c[1] * EW + half * (EW // 2), EW // 2)],
                              stage[:, v, half * (EW // 2):(half + 1) * (EW // 2)], WSCALE
                              ).then_inc(S("w_hi"), 1)

            with act.Fori(0, B // NB) as i:
                def chunk_hi(c):
                    for half in range(2):
                        w_hi((0, i * (E // 2) + c), c % 2, i * 2 + c // 2, half)

                xnT_out(i, 0)
                for u in range(NB):
                    act.wait_ge(S("a_ps"), i * NB + (u + 1))
                    nc.scalar.activation(aT[:, u, :], pb[4 + u][:, 0:T], ACT.Identity,
                                         bias=fold[:, 2 * C:2 * C + 1]).then_inc(S("a_sb"), 1)
                chunk_hi(0)
                for u in range(NB):
                    act.wait_ge(S("nb_ready"), i * NB + (u + 1))
                    nc.scalar.activation(probs[:, u, :], pb[u][0:T, 0:KEYS], ACT.Exp, bias=nb0[:, u, :],
                                         accum_out=rs0[:, u, :]).then_inc(S("p_ready"), 1)
                chunk_hi(1)
                chunk_hi(2)
                for u in range(NB):
                    act.wait_ge(S("z_ps"), i * NB + (u + 1))
                    nc.scalar.copy(zT[:, u, :], pb[4 + u][:, 344:344 + T]).then_inc(S("z_sb"), 1)
                chunk_hi(3)
                xnT_out(i, 1)

            def routing(lay):
                lv = la[:].rearrange("p b e -> p (b e)")
                pv = pi[:].rearrange("p b e -> p (b e)")
                n = S("act_in")
                if lay == 1:
                    act.wait_ge(n, 5 + 2 * 3 + 1)
                    nc.scalar.activation(pv, lv, ACT.Exp).then_inc(S("act_out"), 1)
                    return
                act.wait_ge(n, 1)
                nc.scalar.activation(pv, lv, ACT.Exp).then_inc(S("act_out"), 1)
                act.wait_ge(n, 2)
                nc.scalar.activation(rl[:], rr[:], ACT.Ln).then_inc(S("act_out"), 1)
                act.wait_ge(n, 3)
                nc.scalar.activation(pv, lv, ACT.Exp).then_inc(S("act_out"), 1)
                act.wait_ge(n, 4)
                nc.scalar.activation(cc[:], pb[0][0:T, 0:E], ACT.Ln).then_inc(S("act_out"), 1)
                act.wait_ge(n, 5)
                nc.scalar.activation(pv, lv, ACT.Exp).then_inc(S("act_out"), 1)
                with act.Fori(0, SINK_SEGS) as i:
                    act.wait_ge(n, i * 2 + 6)
                    nc.scalar.activation(rl[:], rr[:], ACT.Ln).then_inc(S("act_out"), 1)
                    nc.scalar.activation(tmp[:, 0, :], cc[:], ACT.Ln).then_inc(S("act_out"), 1)
                    act.wait_ge(n, i * 2 + 7)
                    nc.scalar.activation(pv, lv, ACT.Exp).then_inc(S("act_out"), 1)

            def experts(lay):
                for s in range(TILES):
                    g0 = lay * TILES + s
                    act.wait_ge(S("rows_turned"), g0 + 1)
                    nc.scalar.copy(xThi[:, s, :, :].rearrange("p k n -> p (k n)"), pb[s % 8][:, 0:KD * 128]
                                   ).then_inc(S("xT_hi"), 1)
                for p in range(PHASES[lay]):
                    ph = sum(PHASES[:lay]) + p
                    G = ph * TILES

                    def silu(s, par, first):
                        act.wait_ge(S("gu_ps"), s + (G + 1))
                        if first is None:
                            act.wait_ge(S("h_ready"), s + (G - 1))
                        elif G:
                            act.wait_ge(S("h_ready"), G)
                        nc.scalar.activation(sg[:, par, :], pb[par][:, 0:FC], ACT.Silu, scale=1.0 / WSCALE
                                             ).then_inc(S("silu_ready"), 1)

                    def hT_high(s, par):
                        act.wait_ge(S("hT_ps"), s + (G + 1))
                        if G or not isinstance(s, int) or s >= 2:
                            act.wait_ge(S("y_ps"), s + (G - 1))
                        nc.scalar.copy(hThi[:, par, :, :].rearrange("p k n -> p (k n)"), pb[2 + par][:, 0:FC]
                                       ).then_inc(S("hT_hi"), 1)

                    def split(i, v, half):
                        w_hi(((ph + 1) % 2, i * 2 + v), v, i + (ph + 1) * (E // 2), half)

                    pipeline(silu, hT_high, lambda s, par: None, split if ph + 1 < NPH else None, act)

            routing(0)
            act.wait_ge(S("zeroed"), 16)
            experts(0)
            def unit(b, kind, name, of):
                n = unit_count(b, kind, name)
                u, w = parity(of), pb[unit_bank(kind, name)]
                if name in ("q", "wo", "logits"):
                    return
                act.wait_ge(S("unit_ps"), n + 1)
                if name in ("xnT1", "xnT2"):
                    half = int(name == "xnT2")
                    nc.scalar.copy(xnT[:, half, :, :].rearrange("p k t -> p (k t)"), w[:, 0:KD * T]
                                   ).then_inc(S("xnT_sb"), 1)
                    if half:
                        nc.scalar.copy(xn_of(of), xnb[:, 1, :]).then_inc(S("xn_kept"), 1)
                elif name in ("v0", "v1"):
                    for j in ((0, 1), (2,))[int(name == "v1")]:
                        last = nc.scalar.copy(v1h[:, u * NKC + j, :, 0, :],
                                              w[0:KC, (j % 2) * D:(j % 2) * D + D].rearrange(
                                                  "p (h d) -> p h d", d=DK))
                    last.then_inc(S("v_hi"), 1)
                elif name[0] == "k":
                    m = int(name[1])
                    if isinstance(of, Batch) or of > 0:
                        act.wait_ge(S("k_sb"), count(of, HP, m + 1 - HP))
                    nc.scalar.activation(kf[:, m, :], w[:, 0:KEYS], ACT.Identity, bias=bk1[:, m:m + 1]
                                         ).then_inc(S("k_in"), 1)
                else:
                    nc.scalar.copy(rcT[:], w[:, 0:HP * T]).then_inc(S("rcT_sb"), 1)

            def xn_of(b):
                if isinstance(b, Batch):
                    return xn[:, ds(b.i * 2 + b.k, 1), :].rearrange("p o d -> p (o d)")
                return xn[:, b, :]

            def exponent(b, h):
                act.wait_ge(S("nb1_ready"), count(b, HEADS, h + 1))
                nc.scalar.activation(probs[:, h % NP, :], pb[slot3(h)][0:T, 0:KEYS], ACT.Exp,
                                     bias=nb1[:, h:h + 1], accum_out=rs1[:, parity(b), h:h + 1]
                                     ).then_inc(S("e_ready"), 1)

            def eT_high(b, h):
                act.wait_ge(S("eT_ps"), count(b, HEADS, h + 1))
                if isinstance(b, Batch) or b > 0 or h >= 3:
                    act.wait_ge(S("av_ps"), count(b, HEADS, before3(h) + 1))
                nc.scalar.copy(eThi[:, slot3(h), :], pb[3 + h % 2][0:KC, 0:NKC * T]).then_inc(S("eT_hi"), 1)

            def heads(b, kind, first=False, final=False):
                for h in range(HEADS):
                    if h + 1 < HEADS:
                        exponent(b, h + 1)
                    elif not final:
                        exponent(b + 1, 0)
                    if h - 1 in kind:
                        unit(b, kind, kind[h - 1], b + 1 if kind[h - 1] in NEXT.values() else b + -1)
                    eT_high(b, h)

            for name in NEXT.values():
                unit(-1, NEXT, name, 0)
            exponent(0, 0)
            heads(0, NEXT, first=True)
            with act.Fori(0, (B - 2) // 2) as i:
                heads(Batch(i, 1), BOTH)
                heads(Batch(i, 2), BOTH)
            heads(B - 1, TAIL, final=True)
            for name in TAIL.values():
                unit(B, TAIL, name, B - 1)
            routing(1)
            experts(1)

        @block.vector
        def _(dve):
            ch = Chain(dve, S("dve_step"))
            dve.wait_ge(S("fold_ps"), 1)
            nc.vector.tensor_copy(fold[:], pb[7][:, 0:2 * C + 4]).then_inc(S("fold_sb"), 1)
            dve.wait_ge(S("fold_sb"), 1)
            dve.wait_ge(S("x_in"), 16)
            dve.wait_ge(S("attn0_in"), 16 * 7)
            dve.wait_ge(S("const"), 7)
            dve.wait_ge(S("pool_step"), 5)

            ch(nc.vector.tensor_copy(lower16[:], lower[:]))
            ch(nc.vector.tensor_copy(ones16[:], ones[0:T, 0:T]))

            def carry(u):
                nc.vector.memset(carrier[:, u, :], 0.0)


            def xb(i, u):
                return x[:, ds(i * NB + u, 1), :].rearrange("p o d -> p (o d)")

            def norm(i, half):
                for u in range(NB):
                    carry(2 * u)
                    ch(nc.vector.bn_stats(stats[:, u, :], xb(i, u)))
                    carry(2 * u + 1)
                    ch(nc.vector.bn_aggr(mv[:, u, :], stats[:, u, :]))
                    nc.vector.tensor_scalar(vare[:, u, :], mv[:, u, 1:2], EPS, None, ALU.add
                                            ).then_inc(S("var_ready"), 1)
                for u in range(NB):
                    n = i * (2 * NB) + (half * NB + u + 1)
                    dve.wait_ge(S("rstd_ready"), n)
                    if half == 0:
                        kept = i * NB + 1
                        dve.wait_ge(S("xn_kept"), kept)
                    nc.vector.tensor_scalar(xnb[:, u, :], xb(i, u), mv[:, u, 0:1], rstd[:, u, :],
                                            ALU.subtract, ALU.mult).then_inc(S("ln_ready"), 1)

            def logits(i):
                for u in range(NB):
                    dve.wait_ge(S("logit_ps"), i * NB + (u + 1))
                    nc.vector.tensor_scalar(la[:, ds(i * NB + u, 1), :].rearrange("p o e -> p (o e)"),
                                            pb[u][0:T, 256:256 + E], -1.0 / SINK_EPS, None, ALU.mult).then_inc(S("la_ready"), 1)

            def w_lo(w, e, chunk, v, m, half):
                at = ds(e * EW + half * (EW // 2), EW // 2)
                dve.wait_ge(S(f"w_in{v}"), m * 16 + 16)
                dve.wait_ge(S("w_hi"), chunk * 2 + (1 + half))
                nc.vector.scalar_tensor_tensor(wlo[:, w, at], stage[:, v, half * (EW // 2):(half + 1) * (EW // 2)],
                                               WSCALE, whi[:, w, at], ALU.mult, ALU.subtract
                                               ).then_inc(S("w_lo"), 1)

            per = NB * (2 * 2 + 2 + 2)
            start = ch.now
            with dve.Fori(0, B // NB) as i:
                def chunk_lo(c):
                    for half in range(2):
                        w_lo(0, i * (E // 2) + c, i * (E // 2) + c, c % 2, i * 2 + c // 2, half)

                ch.enter(i, per, start)
                norm(i, 0)
                for u in range(NB):
                    n = i * NB + (u + 1)
                    dve.wait_ge(S("a_ps"), n)
                    nc.vector.tensor_scalar(qbk[:, u, :], pb[u][0:T, 400:401], fold[0:T, 2 * C + 3:2 * C + 4],
                                            None, ALU.add).then_inc(S("qbk_ready"), 1)
                for u in range(NB):
                    n = i * NB + (u + 1)
                    dve.wait_ge(S("s_ps"), n)
                    dve.wait_ge(S("qbk_ready"), n)
                    ch(nc.vector.tensor_reduce(mx0[:, u, :], pb[u][0:T, 0:KEYS], AX.X, ALU.max))
                    ch(nc.vector.tensor_tensor(mx0[:, u, :], mx0[:, u, :], qbk[:, u, :], ALU.add))
                    nc.vector.tensor_tensor(nb0[:, u, :], qbk[:, u, :], mx0[:, u, :], ALU.subtract
                                            ).then_inc(S("nb_ready"), 1)
                chunk_lo(0)
                for u in range(NB):
                    dve.wait_ge(S("pT_ps"), i * NB + (u + 1))
                    nc.vector.tensor_copy(probsT[:, u, :, :].rearrange("p j t -> p (j t)"),
                                          pb[4 + u][0:KC, 0:NKC * T]).then_inc(S("pT_sb"), 1)
                chunk_lo(1)
                chunk_lo(2)
                for u in range(NB):
                    dve.wait_ge(S("p_ready"), i * NB + (u + 1))
                    ch(nc.vector.reciprocal(rc0[:, u, :], rs0[:, u, :]))
                    dve.wait_ge(S("o_ps"), i * NB + (u + 1))
                    ch(nc.vector.scalar_tensor_tensor(upd0[:, u, :], pb[u][0:T, 0:D], rc0[:, u, :], bv0[:],
                                                      ALU.mult, ALU.add))
                    nc.vector.tensor_tensor(xb(i, u), xb(i, u), upd0[:, u, :], ALU.add).then_inc(S("x_upd"), 1)
                dve.wait_ge(S("x_upd"), i * NB + NB)
                norm(i, 1)
                chunk_lo(3)
                logits(i)
            ch.leave(per, B // NB, start)
            dve.wait_ge(S("la_ready"), B)

            def over_e(t):
                return t[:].unsqueeze(2).to_broadcast([T, B, E])

            def over_b(t):
                return t.unsqueeze(1).to_broadcast([T, B, E])

            def routing(lay):
                a_in, a_out = S("act_in"), S("act_out")
                if lay == 0:
                    ch(nc.vector.tensor_reduce(rr[:], la[:], AX.X, ALU.max))
                    nc.vector.tensor_tensor(la[:], la[:], over_e(rr), ALU.subtract).then_inc(a_in, 1)
                    dve.wait_ge(a_out, 1)
                    nc.vector.tensor_reduce(rr[:], pi[:], AX.X, ALU.add).then_inc(a_in, 1)
                    dve.wait_ge(a_out, 2)
                    ch(nc.vector.tensor_tensor(la[:], la[:], over_e(rl), ALU.subtract))
                    nc.vector.tensor_reduce(cc[:], la[:].rearrange("p b e -> p e b"), AX.X, ALU.max
                                            ).then_inc(S("cmax_part"), 1)
                    dve.wait_ge(S("cmaxT"), 1)
                    ch(nc.vector.tensor_reduce(cm[:], pb[0][0:E, 0:T], AX.X, ALU.max))
                    nc.vector.tensor_scalar(cdiag[:], ident[0:E, 0:E], cm[:], None, ALU.mult
                                            ).then_inc(S("cdiag_ready"), 1)
                    dve.wait_ge(S("cmax_all"), 1)
                    ch(nc.vector.tensor_copy(cl[:], pb[1][0:T, 0:E]))
                    nc.vector.tensor_tensor(la[:], la[:], over_b(cl[:]), ALU.subtract).then_inc(a_in, 1)
                    dve.wait_ge(a_out, 3)
                    nc.vector.tensor_reduce(cl[:], pi[:].rearrange("p b e -> p e b"), AX.X, ALU.add
                                            ).then_inc(S("colpart"), 1)
                    dve.wait_ge(S("colsum"), 1)
                    nc.vector.tensor_copy(cl[:], pb[0][0:T, 0:E]).then_inc(a_in, 1)
                    dve.wait_ge(a_out, 4)
                    nc.vector.tensor_tensor(la[:], la[:], over_b(cc[:]), ALU.subtract).then_inc(a_in, 1)
                    dve.wait_ge(a_out, 5)
                    def sink_turn(n):
                        ch(nc.vector.tensor_tensor(tmp[:], pi[:], over_b(cc[:]), ALU.mult))
                        ch(nc.vector.tensor_reduce(rl[:], tmp[:], AX.X, ALU.add))
                        ch(nc.vector.reciprocal(rr[:], rl[:]))
                        ch(nc.vector.tensor_tensor(tmp[:], pi[:], over_e(rr), ALU.mult))
                        nc.vector.tensor_reduce(cl[:], tmp[:].rearrange("p b e -> p e b"), AX.X, ALU.add
                                                ).then_inc(S("colpart"), 1)
                        dve.wait_ge(S("colsum"), n)
                        ch(nc.vector.reciprocal(cc[:], pb[0][0:T, 0:E]))

                    ch(nc.vector.memset(cc[:], 1.0))
                    sink_turn(2)
                    start, per = ch.now, 5 * SINK_TURNS + 2
                    with dve.Fori(0, SINK_SEGS) as j:
                        ch.enter(j, per, start)
                        for k in range(SINK_TURNS):
                            sink_turn(j * SINK_TURNS + (3 + k))
                        nc.vector.tensor_copy(rl[:], rr[:]).then_inc(a_in, 1)
                        dve.wait_ge(a_out, j * 3 + 7)
                        ch(nc.vector.tensor_tensor(la[:], la[:], over_e(rl), ALU.add))
                        nc.vector.tensor_tensor(la[:], la[:], over_b(tmp[:, 0, :]), ALU.add).then_inc(a_in, 1)
                        dve.wait_ge(a_out, j * 3 + 8)
                        ch(nc.vector.memset(cc[:], 1.0))
                    ch.leave(per, SINK_SEGS, start)
                else:
                    ch(nc.vector.tensor_reduce(rr[:], la[:], AX.X, ALU.max))
                    nc.vector.tensor_tensor(la[:], la[:], over_e(rr), ALU.subtract).then_inc(a_in, 1)
                    dve.wait_ge(a_out, 5 + 9 + 1)
                    ch(nc.vector.tensor_reduce(rr[:], pi[:], AX.X, ALU.add))
                    ch(nc.vector.reciprocal(rl[:], rr[:]))
                    ch(nc.vector.tensor_tensor(pi[:], pi[:], over_e(rl), ALU.mult))
                if lay == 0:
                    ch(nc.vector.scalar_tensor_tensor(pi[:], pi[:], 2.0 ** -126, pi[:], ALU.is_ge, ALU.mult))
                    ch(nc.vector.tensor_copy(wtop[:, 0, :, :], pi[:, :, 0:TOPK].rearrange("p b k -> p k b")))
                for k, hot in enumerate((m1h, m2h)):
                    top = rr[:] if lay == 0 else wtop[:, 1, k, :]
                    ch(nc.vector.tensor_reduce(top, pi[:], AX.X, ALU.max))
                    ch(nc.vector.tensor_tensor(tmp[:], pi[:], top.unsqueeze(2).to_broadcast([T, B, E]),
                                               ALU.is_equal))
                    ch(nc.vector.tensor_tensor(tmp[:], tmp[:], iota_e[:], ALU.mult))
                    ch(nc.vector.tensor_reduce(rl[:], tmp[:], AX.X, ALU.min))
                    ch(nc.vector.tensor_tensor(hot[:], iota_e[:], over_e(rl), ALU.is_equal))
                    if k == 0:
                        ch(nc.vector.scalar_tensor_tensor(pi[:], hot[:], -2.0, pi[:], ALU.mult, ALU.add))
                nc.vector.tensor_tensor(msk[:], m1h[:], m2h[:], ALU.add).then_inc(S("mask_ready"), 1)
                dve.wait_ge(S("rank_ps"), lay + 1)
                ch(nc.vector.tensor_copy(cl[:], pb[3][0:T, 0:E]))
                ch(nc.vector.tensor_tensor(kcmp[:], cl[:].unsqueeze(2).to_broadcast([T, E, CPE]), kgrid[:],
                                           ALU.is_gt))
                ch(nc.vector.tensor_reduce(nt[:], kcmp[:], AX.X, ALU.add))
                ch(nc.vector.tensor_tensor(tcmp[:], nt[:].unsqueeze(1).to_broadcast([T, E, E]), tri[:], ALU.mult))
                ch(nc.vector.tensor_reduce(tb[:], tcmp[:], AX.X, ALU.add))
                ch(nc.vector.tensor_tensor(tend[:], tb[:], nt[:], ALU.add))
                ch(nc.vector.tensor_tensor(scmp[:], tend[:].unsqueeze(1).to_broadcast([T, TILES, E]), sgrid[:],
                                           ALU.is_le))
                ch(nc.vector.tensor_reduce(tef[:], scmp[:], AX.X, ALU.add))
                ch(nc.vector.tensor_scalar(tef[:], tef[:], E - 1.0, float(EW), ALU.min, ALU.mult))
                nc.vector.tensor_copy(te[:], tef[:]).then_inc(S("te_ready"), 1)
                ch(nc.vector.tensor_scalar(tb[:], tb[:], float(SLOTS), None, ALU.mult))
                ch(nc.vector.tensor_tensor(slotv[:], pb[2][0:T, 0:B * E].rearrange("p (b e) -> p b e", e=E),
                                           over_b(tb[:]), ALU.add))
                for k, hot in enumerate((m1h, m2h)):
                    ch(nc.vector.tensor_tensor(tmp[:], slotv[:], hot[:], ALU.mult))
                    ch(nc.vector.tensor_reduce(sf[:], tmp[:], AX.X, ALU.add))
                    ins = nc.vector.tensor_copy(slot[:, k, :], sf[:])
                    if k == 0:
                        ch(ins)
                ins.then_inc(S("slots_ready"), 1)

            def experts(lay):
                for s in range(TILES):
                    g0 = lay * TILES + s
                    dve.wait_ge(S("xT_hi"), g0 + 1)
                    nc.vector.tensor_tensor(xTlo[:, s, :, :].rearrange("p k n -> p (k n)"),
                                            pb[s % 8][:, 0:KD * 128],
                                            xThi[:, s, :, :].rearrange("p k n -> p (k n)"), ALU.subtract
                                            ).then_inc(S("xT_sb"), 1)
                for p in range(PHASES[lay]):
                    ph = sum(PHASES[:lay]) + p
                    G = ph * TILES

                    def product(s, par, first):
                        dve.wait_ge(S("silu_ready"), s + (G + 1))
                        if first is None:
                            dve.wait_ge(S("hT_ps"), s + (G - 1))
                        elif G:
                            dve.wait_ge(S("hT_ps"), G)
                        nc.vector.scalar_tensor_tensor(hh[:, par, :], pb[par][:, FC:2 * FC], 1.0 / WSCALE,
                                                       sg[:, par, :], ALU.mult, ALU.mult
                                                       ).then_inc(S("h_ready"), 1)

                    def hT_low(s, par):
                        dve.wait_ge(S("hT_hi"), s + (G + 1))
                        nc.vector.tensor_tensor(hTlo[:, par, :, :].rearrange("p k n -> p (k n)"),
                                                pb[2 + par][:, 0:FC],
                                                hThi[:, par, :, :].rearrange("p k n -> p (k n)"), ALU.subtract
                                                ).then_inc(S("hT_lo"), 1)

                    def add(s, par):
                        dve.wait_ge(S("y_ps"), s + (G + 1))
                        to = yacc[:, s, :] if isinstance(s, int) else yacc[:, ds(s.at, 1), :].rearrange("p o d -> p (o d)")
                        if p == 0:
                            ins = nc.vector.tensor_scalar(to, pb[4 + par][:, 0:D], 1.0 / WSCALE, None, ALU.mult)
                        else:
                            ins = nc.vector.scalar_tensor_tensor(to, pb[4 + par][:, 0:D], 1.0 / WSCALE, to,
                                                                 ALU.mult, ALU.add)
                        ins.then_inc(S("y_acc"), 1)

                    def split(i, v, half):
                        w_lo((ph + 1) % 2, i * 2 + v, i * 2 + (v + (ph + 1) * E), v, i + (ph + 1) * (E // 2), half)

                    pipeline(product, hT_low, add, split if ph + 1 < NPH else None, dve)

            def combine(lay, b):
                dve.wait_ge(S(f"gathered{b}"), 16 * TOPK * (lay + 1))
                ch(nc.vector.scalar_tensor_tensor(x[:, b, :], yg[:, 0, b, :], wtop[:, lay, 0, b:b + 1],
                                                  x[:, b, :], ALU.mult, ALU.add))
                ins = nc.vector.scalar_tensor_tensor(x[:, b, :], yg[:, 1, b, :], wtop[:, lay, 1, b:b + 1],
                                                     x[:, b, :], ALU.mult, ALU.add)
                if lay == 0:
                    ch(ins)
                else:
                    ins.then_inc(S("x_done"), 1)

            dve.wait_ge(S("bv_ps"), 1)
            ch(nc.vector.scalar_tensor_tensor(bo1[:], pb[6][0:T, 0:D], 0.5, bo1[:], ALU.mult, ALU.add))
            ch(nc.vector.tensor_scalar(bq1s[:], bq1[:], DK ** -0.5, None, ALU.mult))
            routing(0)
            experts(0)
            combine(0, 0)
            def x_of(b):
                if isinstance(b, Batch):
                    return x[:, ds(b.i * 2 + b.k, 1), :].rearrange("p o d -> p (o d)")
                return x[:, b, :]

            def spread(b, u, part):
                if part == 0:
                    carry(2 * u)
                    nc.vector.bn_stats(stats[:, u, :], x_of(b)).then_inc(S("stats_ready"), 1)
                elif part == 1:
                    dve.wait_ge(S("stats_ready"), norm_count(b, u) + (-2 * B))
                    carry(2 * u + 1)
                    nc.vector.bn_aggr(mv[:, u, :], stats[:, u, :]).then_inc(S("mean_ready"), 1)
                else:
                    dve.wait_ge(S("mean_ready"), norm_count(b, u) + (-2 * B))
                    nc.vector.tensor_scalar(vare[:, u, :], mv[:, u, 1:2], EPS, None, ALU.add
                                            ).then_inc(S("var_ready"), 1)

            def normal(b, second):
                dve.wait_ge(S("rstd_ready"), norm_count(b, second))
                nc.vector.tensor_scalar(xnb[:, second, :], x_of(b), mv[:, second, 0:1], rstd[:, second, :],
                                        ALU.subtract, ALU.mult).then_inc(S("ln_ready"), 1)

            def unit(b, kind, name, of):
                n = unit_count(b, kind, name)
                u, w = parity(of), pb[unit_bank(kind, name)]
                if name in ("xnT1", "xnT2") or name[0] == "k":
                    return
                if name == "q":
                    dve.wait_ge(S("unit_ps"), n + 1)
                    nc.vector.scalar_tensor_tensor(
                        qf[:], w[:, 0:HP * T].rearrange("p (m t) -> p m t", t=T), DK ** -0.5,
                        bq1s[:].unsqueeze(2).to_broadcast([128, HP, T]), ALU.mult, ALU.add
                        ).then_inc(S("q_in"), 1)
                elif name in ("v0", "v1"):
                    dve.wait_ge(S("v_hi"), count(of, 2, 1 + int(name == "v1")))
                    for j in ((0, 1), (2,))[int(name == "v1")]:
                        last = nc.vector.tensor_tensor(
                            v1h[:, u * NKC + j, :, 1, :], w[0:KC, (j % 2) * D:(j % 2) * D + D].rearrange(
                                "p (h d) -> p h d", d=DK), v1h[:, u * NKC + j, :, 0, :], ALU.subtract)
                    last.then_inc(S("v_sb"), 1)
                elif name == "rcT":
                    dve.wait_ge(S("av_ps"), count(of, HEADS, HEADS))
                    dve.wait_ge(S("rcT_sb"), count(of, 1, 1))
                    nc.vector.tensor_tensor(catT[:], pb[5][:, 0:HP * T], rcT[:], ALU.mult
                                            ).then_inc(S("cat_ready"), 1)
                elif name == "wo":
                    dve.wait_ge(S("unit_ps"), n + 1)
                    nc.vector.tensor_tensor(upd[:, 0, :], w[0:T, 0:D], bo1[:], ALU.add).then_inc(S("wo_used"), 1)
                    dve.wait_ge(S("wo_used"), count(of, 1, 1))
                    ch(nc.vector.tensor_tensor(x_of(of), x_of(of), upd[:, 0, :], ALU.add))
                else:
                    dve.wait_ge(S("unit_ps"), n + 1)
                    to = la[:, ds(of.i * 2 + of.k, 1), :].rearrange("p o e -> p (o e)") \
                        if isinstance(of, Batch) else la[:, of, :]
                    nc.vector.tensor_copy(to, w[0:T, 0:E]).then_inc(S("la_ready"), 1)

            def maximum(b, h):
                dve.wait_ge(S("ss_ps"), count(b, HEADS, h + 1))
                nc.vector.tensor_reduce(nb1[:, h:h + 1], pb[slot3(h)][0:T, 0:KEYS], AX.X, ALU.max,
                                        negate=True).then_inc(S("nb1_ready"), 1)

            def eT_low(b, h):
                dve.wait_ge(S("eT_hi"), count(b, HEADS, h + 1))
                nc.vector.tensor_tensor(eTlo[:, slot3(h), :], pb[3 + h % 2][0:KC, 0:NKC * T],
                                        eThi[:, slot3(h), :], ALU.subtract).then_inc(S("eT_lo"), 1)

            def over_sums(b):
                dve.wait_ge(S("e_ready"), count(b, HEADS, HEADS))
                nc.vector.reciprocal(rc1[:], rs1[:, parity(b), :]).then_inc(S("rc_ready"), 1)

            def heads(b, kind, first=False, final=False):
                for h in range(HEADS):
                    name = kind.get(h - 1)
                    of = b + 1 if name in NEXT.values() else b + -1
                    if name in ("q", "wo", "logits"):
                        unit(b, kind, name, of)
                    if h + 2 < HEADS:
                        maximum(b, h + 2)
                    elif not final:
                        maximum(b + 1, h + 2 - HEADS)
                    if name in ("v0", "v1", "rcT"):
                        unit(b, kind, name, of)
                    if h in (0, 1, 2) and not final:
                        spread(b + 1, 0, h)
                    if h == 4 and not final:
                        normal(b + 1, 0)
                    if h in (5, 6, 7) and not first:
                        spread(b + -1, 1, h - 5)
                    if h == 10 and not first:
                        normal(b + -1, 1)
                    if first and 2 <= h < B:
                        combine(0, h)
                    if h == HEADS - 1:
                        over_sums(b)
                    eT_low(b, h)

            for part in range(3):
                spread(0, 0, part)
            normal(0, 0)
            for name in NEXT.values():
                unit(-1, NEXT, name, 0)
            combine(0, 1)
            maximum(0, 0)
            maximum(0, 1)
            heads(0, NEXT, first=True)
            per = 2 * 1
            start = ch.now
            with dve.Fori(0, (B - 2) // 2) as i:
                ch.enter(i, per, start)
                heads(Batch(i, 1), BOTH)
                heads(Batch(i, 2), BOTH)
            ch.leave(per, (B - 2) // 2, start)
            heads(B - 1, TAIL, final=True)
            for name in TAIL.values():
                unit(B, TAIL, name, B - 1)
                if name == "wo":
                    for part in range(3):
                        spread(B - 1, 1, part)
                    normal(B - 1, 1)
            dve.wait_ge(S("la_ready"), 2 * B)
            routing(1)
            experts(1)
            for b in range(B):
                combine(1, b)


def kernel(**inputs):
    import numpy as np
    import concourse.bacc as bacc
    from concourse.bass_utils import run_bass_kernel_spmd as run

    f = {k: np.asarray(v) for k, v in inputs.items()}

    def chunks(w, k):
        return w.reshape(k, 128, -1).transpose(1, 0, 2)

    def pad_heads(w):
        r = w.reshape(w.shape[0], HEADS, DK)
        return np.concatenate([r, r], axis=2).reshape(w.shape[0], 2 * HEADS * DK)

    ctx = f["ctx_512"]
    arr = {
        "x": f["x"],
        "ctxT": ctx.transpose(2, 0, 1),
        "ctxN": ctx.reshape(B, NKC, KC, C).transpose(2, 0, 1, 3),
        "wq0T": chunks(f["L0_xattn_Wq"].T, KD),
        "wk0T": chunks(f["L0_xattn_Wk"].T, KD),
        "wv0": f["L0_xattn_Wv"],
        "bq0": f["L0_xattn_bq"].reshape(KD, 128).T,
        "bk0": f["L0_xattn_bk"].reshape(KD, 128).T,
        "bv0": np.broadcast_to(f["L0_xattn_bv"], (T, D)),
        "wq1": chunks(pad_heads(f["L1_xattn_Wq"]), KD),
        "wk1": pad_heads(f["L1_xattn_Wk"]),
        "wv1": f["L1_xattn_Wv"],
        "wo1": chunks(pad_heads(f["L1_xattn_Wo"].T).T, HP),
        "bq1": pad_heads(f["L1_xattn_bq"][None])[0].reshape(HP, 128).T,
        "bk1": pad_heads(f["L1_xattn_bk"][None])[0].reshape(HP, 128).T,
        "bv1": pad_heads(f["L1_xattn_bv"][None])[0].reshape(HP, 128).T,
        "bo1": np.broadcast_to(f["L1_xattn_bo"], (T, D)),
        "router": np.stack([chunks(f["L0_ffn_gate_W"].T, KD), chunks(f["L1_ffn_router_w"].T, KD)], axis=1),
    }
    w1, w2 = f["L1_ffn_w1"], f["L1_ffn_w2"]
    inter = w1.shape[1] // 2
    layers = ((f["L0_ffn_W_gate"], f["L0_ffn_W_up"], f["L0_ffn_W_down"]), (w1[:, :inter], w1[:, inter:], w2))
    stream = []
    for (gate, up, down), n in zip(layers, PHASES):
        for p in range(n):
            for e in range(E):
                g = chunks(gate[e, p * FC:(p + 1) * FC].T, KD)
                u = chunks(up[e, p * FC:(p + 1) * FC].T, KD)
                d = chunks(down[e][:, p * FC:(p + 1) * FC].T, FC // 128)
                gu = np.concatenate([g, u], axis=2).reshape(128, -1)
                stream.append(np.concatenate([gu, d.reshape(128, -1)], axis=1))
    arr["wst"] = np.stack(stream, axis=1)

    nc = bacc.Bacc("TRN2", target_bir_lowering=False, num_devices=1)
    arr["lowrow"] = ((np.arange(128) // DK) % 2).astype(np.float32).reshape(128, 1)
    arrays, aps = {}, {}
    for name, v in arr.items():
        v = np.ascontiguousarray(v)
        arrays[f"in_{name}"] = v
        aps[name] = nc.dram_tensor(f"in_{name}", v.shape, mybir.dt.from_np(v.dtype), kind="ExternalInput").ap()
    aps["out"] = nc.dram_tensor("out_x", (B, T, D), F32, kind="ExternalOutput").ap()
    build(nc, aps)
    r = run(nc, [arrays], core_ids=[0])
    return r.results[0]["out_x"]
```
